# Optimizing a Trainium2 kernel written in Bass

```python
import numpy as np
import jax
import jax.numpy as jnp

def _softmax(x, axis=-1):
    return jax.nn.softmax(x, axis=axis)

def _gelu(x):
    return jax.nn.gelu(x, approximate=True)

def _silu(x):
    return jax.nn.silu(x)

def _sigmoid(x):
    return jax.nn.sigmoid(x)

def _layernorm(x, axis=-1, eps=1e-05):
    m = jnp.mean(x, axis=axis, keepdims=True)
    v = jnp.var(x, axis=axis, keepdims=True)
    return (x - m) / jnp.sqrt(v + eps)

def _scatter_add(tgt, idx, src, axis=0):
    return tgt.at[idx].add(src)

def _segment_sum(src, seg, n):
    return jax.ops.segment_sum(src, seg, n)
kernel_name = 'mk_seq_preln_d2_jaxref_r8_d51e60'

def setup_inputs(seed: int=0):
    np.random.seed(seed)
    _w = jnp.asarray

    def _L0_attn_setup():
        import jax, jax.numpy as jnp
        import numpy as np
        N_EMBD = 256
        N_HEAD = 8
        HEAD_DIM = 32
        HALF = HEAD_DIM // 2
        LAMBDA_INIT = 0.8
        RMS_EPS = 1.1920929e-07

        def _rms_norm(x):
            return x * jax.lax.rsqrt(jnp.mean(x * x, axis=-1, keepdims=True) + RMS_EPS)

        def _causal_attn(q, k, v, mask):
            scale = 1.0 / jnp.sqrt(jnp.asarray(q.shape[-1], q.dtype))
            scores = jnp.einsum('bhqd,bhkd->bhqk', q, k) * scale
            scores = jnp.where(mask, scores, -jnp.inf)
            attn = jax.nn.softmax(scores, axis=-1)
            return jnp.einsum('bhqk,bhkd->bhqd', attn, v)
        key = jax.random.key(seed)
        ks = jax.random.split(key, 10)
        B, T, C = (2, 256, N_EMBD)
        x = jax.random.normal(ks[0], (B, T, C), dtype=jnp.float32)
        wq = jax.random.normal(ks[1], (C, C), dtype=jnp.float32) * 0.02
        wk = jax.random.normal(ks[2], (C, C), dtype=jnp.float32) * 0.02
        wv = jax.random.normal(ks[3], (C, C), dtype=jnp.float32) * 0.02
        wo = jax.random.normal(ks[4], (C, C), dtype=jnp.float32) * 0.02
        lq1 = jax.random.normal(ks[5], (HEAD_DIM,), dtype=jnp.float32) * 0.1
        lk1 = jax.random.normal(ks[6], (HEAD_DIM,), dtype=jnp.float32) * 0.1
        lq2 = jax.random.normal(ks[7], (HEAD_DIM,), dtype=jnp.float32) * 0.1
        lk2 = jax.random.normal(ks[8], (HEAD_DIM,), dtype=jnp.float32) * 0.1
        return {'x': x, 'wq': wq, 'wk': wk, 'wv': wv, 'wo': wo, 'lq1': lq1, 'lk1': lk1, 'lq2': lq2, 'lk2': lk2}
    _L0_attn_in = _L0_attn_setup()

    def _L0_ffn_setup():
        import jax, jax.numpy as jnp
        import numpy as np
        DIM_IN = 256
        DIM_HIDDEN = 1024
        key = jax.random.key(seed)
        k_x, k_g, k_u, k_d = jax.random.split(key, 4)
        s_in = 1.0 / np.sqrt(DIM_IN)
        s_hid = 1.0 / np.sqrt(DIM_HIDDEN)
        x = jax.random.normal(k_x, (4, 256, DIM_IN), dtype=jnp.float32)
        w_gate = jax.random.uniform(k_g, (DIM_HIDDEN, DIM_IN), jnp.float32, -s_in, s_in)
        w_up = jax.random.uniform(k_u, (DIM_HIDDEN, DIM_IN), jnp.float32, -s_in, s_in)
        w_down = jax.random.uniform(k_d, (DIM_IN, DIM_HIDDEN), jnp.float32, -s_hid, s_hid)
        return {'x': x, 'w_gate': w_gate, 'w_up': w_up, 'w_down': w_down}
    _L0_ffn_in = _L0_ffn_setup()

    def _L1_attn_setup():
        import jax, jax.numpy as jnp
        import numpy as np
        NUM_STEPS = 3
        NUM_HEADS = 8
        HEAD_DIM = 128
        EPS = 1e-05

        def layernorm(x, g, b):
            mu = jnp.mean(x, -1, keepdims=True)
            var = jnp.mean(jnp.square(x - mu), -1, keepdims=True)
            return (x - mu) * jax.lax.rsqrt(var + EPS) * g + b

        def entmax15(x):
            x = (x - jnp.max(x, -1, keepdims=True)) / 2.0
            xs = jnp.flip(jnp.sort(x, -1), -1)
            rho = jnp.arange(1, x.shape[-1] + 1, dtype=x.dtype)
            mean = jnp.cumsum(xs, -1) / rho
            meansq = jnp.cumsum(xs * xs, -1) / rho
            ss = rho * (meansq - jnp.square(mean))
            tau = mean - jnp.sqrt(jnp.clip((1.0 - ss) / rho, 0.0, None))
            support = jnp.sum(tau <= xs, -1, keepdims=True)
            tau_star = jnp.take_along_axis(tau, support - 1, -1)
            return jnp.square(jnp.clip(x - tau_star, 0.0, None))
        key = jax.random.key(seed)
        ks = jax.random.split(key, 6)
        B, S, Hd, Md, N = (2, 128, 256, 128, 256)
        THD = NUM_HEADS * HEAD_DIM
        return {'hidden': jax.random.normal(ks[0], (B, S, Hd), jnp.float32), 'memory': jax.random.normal(ks[1], (N, Md), jnp.float32), 'Wq': jax.random.normal(ks[2], (THD, Hd), jnp.float32) / np.float32(np.sqrt(Hd)), 'Wk': jax.random.normal(ks[3], (THD, Md), jnp.float32) / np.float32(np.sqrt(Md)), 'Wv': jax.random.normal(ks[4], (THD, Md), jnp.float32) / np.float32(np.sqrt(Md)), 'Wo': jax.random.normal(ks[5], (Hd, THD), jnp.float32) / np.float32(np.sqrt(THD)), 'log_beta': jnp.full((NUM_HEADS,), float(np.log(1.0 / np.sqrt(HEAD_DIM))), jnp.float32), 'g_state': jnp.ones((Hd,), jnp.float32), 'b_state': jnp.zeros((Hd,), jnp.float32), 'g_mem': jnp.ones((Md,), jnp.float32), 'b_mem': jnp.zeros((Md,), jnp.float32)}
    _L1_attn_in = _L1_attn_setup()

    def _L1_ffn_setup():
        import jax, jax.numpy as jnp
        import numpy as np
        HIDDEN = 256
        INTER = 688
        LUT_SIZE = 16

        def _ghost_linear(x, idx, lut):
            w = lut[idx]
            return jnp.einsum('bsh,oh->bso', x, w)
        key = jax.random.key(seed)
        k_x, k_lut, k_g, k_u, k_d = jax.random.split(key, 5)
        x = jax.random.normal(k_x, (2, 512, HIDDEN), dtype=jnp.float32)
        lut = jax.random.normal(k_lut, (LUT_SIZE,), dtype=jnp.float32) * 0.02
        gate_idx = jax.random.randint(k_g, (INTER, HIDDEN), 0, LUT_SIZE, dtype=jnp.int32)
        up_idx = jax.random.randint(k_u, (INTER, HIDDEN), 0, LUT_SIZE, dtype=jnp.int32)
        down_idx = jax.random.randint(k_d, (HIDDEN, INTER), 0, LUT_SIZE, dtype=jnp.int32)
        return {'x': x, 'lut': lut, 'gate_idx': gate_idx, 'up_idx': up_idx, 'down_idx': down_idx}
    _L1_ffn_in = _L1_ffn_setup()
    _d = {'L0_attn_x': _L0_attn_in['x'], 'L0_attn_wq': _L0_attn_in['wq'], 'L0_attn_wk': _L0_attn_in['wk'], 'L0_attn_wv': _L0_attn_in['wv'], 'L0_attn_wo': _L0_attn_in['wo'], 'L0_attn_lq1': _L0_attn_in['lq1'], 'L0_attn_lk1': _L0_attn_in['lk1'], 'L0_attn_lq2': _L0_attn_in['lq2'], 'L0_attn_lk2': _L0_attn_in['lk2'], 'L0_ffn_w_gate': _L0_ffn_in['w_gate'], 'L0_ffn_w_up': _L0_ffn_in['w_up'], 'L0_ffn_w_down': _L0_ffn_in['w_down'], 'L1_attn_memory': _L1_attn_in['memory'], 'L1_attn_Wq': _L1_attn_in['Wq'], 'L1_attn_Wk': _L1_attn_in['Wk'], 'L1_attn_Wv': _L1_attn_in['Wv'], 'L1_attn_Wo': _L1_attn_in['Wo'], 'L1_attn_log_beta': _L1_attn_in['log_beta'], 'L1_attn_g_state': _L1_attn_in['g_state'], 'L1_attn_b_state': _L1_attn_in['b_state'], 'L1_attn_g_mem': _L1_attn_in['g_mem'], 'L1_attn_b_mem': _L1_attn_in['b_mem'], 'L1_ffn_lut': _L1_ffn_in['lut'], 'L1_ffn_gate_idx': _L1_ffn_in['gate_idx'], 'L1_ffn_up_idx': _L1_ffn_in['up_idx'], 'L1_ffn_down_idx': _L1_ffn_in['down_idx']}
    _x0 = _d['L0_attn_x']
    _d['L0_attn_x'] = jax.random.normal(jax.random.fold_in(jax.random.key(seed), 1), (2, 1024, 256), dtype=_x0.dtype)
    del _x0
    return _d

def reference(L0_attn_x, L0_attn_wq, L0_attn_wk, L0_attn_wv, L0_attn_wo, L0_attn_lq1, L0_attn_lk1, L0_attn_lq2, L0_attn_lk2, L0_ffn_w_gate, L0_ffn_w_up, L0_ffn_w_down, L1_attn_memory, L1_attn_Wq, L1_attn_Wk, L1_attn_Wv, L1_attn_Wo, L1_attn_log_beta, L1_attn_g_state, L1_attn_b_state, L1_attn_g_mem, L1_attn_b_mem, L1_ffn_lut, L1_ffn_gate_idx, L1_ffn_up_idx, L1_ffn_down_idx):

    def _L0_attn_ref(x, wq, wk, wv, wo, lq1, lk1, lq2, lk2):
        import jax, jax.numpy as jnp
        import numpy as np
        N_EMBD = 256
        N_HEAD = 8
        HEAD_DIM = 32
        HALF = HEAD_DIM // 2
        LAMBDA_INIT = 0.8
        RMS_EPS = 1.1920929e-07

        def _rms_norm(x):
            return x * jax.lax.rsqrt(jnp.mean(x * x, axis=-1, keepdims=True) + RMS_EPS)

        def _causal_attn(q, k, v, mask):
            scale = 1.0 / jnp.sqrt(jnp.asarray(q.shape[-1], q.dtype))
            scores = jnp.einsum('bhqd,bhkd->bhqk', q, k) * scale
            scores = jnp.where(mask, scores, -jnp.inf)
            attn = jax.nn.softmax(scores, axis=-1)
            return jnp.einsum('bhqk,bhkd->bhqd', attn, v)
        B, T, C = x.shape
        lambda_1 = jnp.exp(jnp.sum(lq1 * lk1))
        lambda_2 = jnp.exp(jnp.sum(lq2 * lk2))
        lambda_full = lambda_1 - lambda_2 + LAMBDA_INIT
        q = (x @ wq.T).reshape(B, T, N_HEAD, 2, HALF).transpose(0, 2, 1, 3, 4)
        k = (x @ wk.T).reshape(B, T, N_HEAD, 2, HALF).transpose(0, 2, 1, 3, 4)
        v = (x @ wv.T).reshape(B, T, N_HEAD, HEAD_DIM).transpose(0, 2, 1, 3)
        q1 = _rms_norm(q[..., 0, :])
        q2 = _rms_norm(q[..., 1, :])
        k1 = _rms_norm(k[..., 0, :])
        k2 = _rms_norm(k[..., 1, :])
        mask = jnp.tril(jnp.ones((T, T), dtype=bool))
        y1 = _causal_attn(q1, k1, v, mask)
        y2 = _causal_attn(q2, k2, v, mask)
        y = y1 - lambda_full * y2
        y = y.transpose(0, 2, 1, 3).reshape(B, T, C)
        return y @ wo.T * (1.0 - LAMBDA_INIT)

    def _L0_ffn_ref(x, w_gate, w_up, w_down):
        import jax, jax.numpy as jnp
        import numpy as np
        DIM_IN = 256
        DIM_HIDDEN = 1024
        gate = jnp.einsum('bsd,hd->bsh', x, w_gate)
        up = jnp.einsum('bsd,hd->bsh', x, w_up)
        gated = jax.nn.silu(gate) * up
        return jnp.einsum('bsh,dh->bsd', gated, w_down)

    def _L1_attn_ref(hidden, memory, Wq, Wk, Wv, Wo, log_beta, g_state, b_state, g_mem, b_mem):
        import jax, jax.numpy as jnp
        import numpy as np
        NUM_STEPS = 3
        NUM_HEADS = 8
        HEAD_DIM = 128
        EPS = 1e-05

        def layernorm(x, g, b):
            mu = jnp.mean(x, -1, keepdims=True)
            var = jnp.mean(jnp.square(x - mu), -1, keepdims=True)
            return (x - mu) * jax.lax.rsqrt(var + EPS) * g + b

        def entmax15(x):
            x = (x - jnp.max(x, -1, keepdims=True)) / 2.0
            xs = jnp.flip(jnp.sort(x, -1), -1)
            rho = jnp.arange(1, x.shape[-1] + 1, dtype=x.dtype)
            mean = jnp.cumsum(xs, -1) / rho
            meansq = jnp.cumsum(xs * xs, -1) / rho
            ss = rho * (meansq - jnp.square(mean))
            tau = mean - jnp.sqrt(jnp.clip((1.0 - ss) / rho, 0.0, None))
            support = jnp.sum(tau <= xs, -1, keepdims=True)
            tau_star = jnp.take_along_axis(tau, support - 1, -1)
            return jnp.square(jnp.clip(x - tau_star, 0.0, None))
        B, S, _ = hidden.shape
        N = memory.shape[0]
        H, hd = (NUM_HEADS, HEAD_DIM)
        Q = layernorm(hidden, g_state, b_state) @ Wq.T
        mn = layernorm(memory, g_mem, b_mem)
        K = (mn @ Wk.T).reshape(N, H, hd).transpose(1, 0, 2)
        V = (mn @ Wv.T).reshape(N, H, hd).transpose(1, 0, 2)
        xi = Q.reshape(B, S, H, hd).transpose(0, 2, 1, 3)
        beta = jnp.exp(log_beta)[None, :, None, None]
        for _ in range(NUM_STEPS):
            scores = jnp.einsum('bhsd,hnd->bhsn', xi, K) * beta
            w = entmax15(scores)
            xi = jnp.einsum('bhsn,hnd->bhsd', w, V)
        out = xi.transpose(0, 2, 1, 3).reshape(B, S, H * hd) @ Wo.T
        return out

    def _L1_ffn_ref(x, lut, gate_idx, up_idx, down_idx):
        import jax, jax.numpy as jnp
        import numpy as np
        HIDDEN = 256
        INTER = 688
        LUT_SIZE = 16

        def _ghost_linear(x, idx, lut):
            w = lut[idx]
            return jnp.einsum('bsh,oh->bso', x, w)
        gate = _ghost_linear(x, gate_idx, lut)
        up = _ghost_linear(x, up_idx, lut)
        h = jax.nn.silu(gate) * up
        return _ghost_linear(h, down_idx, lut)
    x = L0_attn_x
    x = x + _L0_attn_ref(_layernorm(x, axis=-1), L0_attn_wq, L0_attn_wk, L0_attn_wv, L0_attn_wo, L0_attn_lq1, L0_attn_lk1, L0_attn_lq2, L0_attn_lk2)
    x = x + _L0_ffn_ref(_layernorm(x, axis=-1), L0_ffn_w_gate, L0_ffn_w_up, L0_ffn_w_down)
    x = x + _L1_attn_ref(_layernorm(x, axis=-1), L1_attn_memory, L1_attn_Wq, L1_attn_Wk, L1_attn_Wv, L1_attn_Wo, L1_attn_log_beta, L1_attn_g_state, L1_attn_b_state, L1_attn_g_mem, L1_attn_b_mem)
    x = x + _L1_ffn_ref(_layernorm(x, axis=-1), L1_ffn_lut, L1_ffn_gate_idx, L1_ffn_up_idx, L1_ffn_down_idx)
    return x

_drawn_inputs = setup_inputs


def setup_inputs(seed=0):
    import zlib

    import numpy as np

    out = dict(_drawn_inputs(seed))
    spreads = {'L1_attn_log_beta': (-2.4260151386260986, 0.2),
     'L1_attn_g_state': (1.0, 0.2),
     'L1_attn_b_state': (0.0, 0.1),
     'L1_attn_g_mem': (1.0, 0.2),
     'L1_attn_b_mem': (0.0, 0.1)}
    factors = {'L0_attn_wq': 8.0,
     'L0_attn_wk': 8.0,
     'L0_attn_wv': 8.0,
     'L0_attn_wo': 8.0,
     'L0_attn_lq1': 8.0,
     'L0_attn_lk1': 8.0,
     'L0_attn_lq2': 64.0,
     'L0_attn_lk2': 200.0}
    for name, (base, spread) in spreads.items():
        noise = np.random.default_rng([zlib.crc32(name.encode()), seed]).standard_normal(out[name].shape)
        drawn = base * np.exp(spread * noise) if base else spread * noise
        out[name] = jnp.asarray(drawn.astype(out[name].dtype))
    for name, factor in factors.items():
        out[name] = (out[name] * factor).astype(out[name].dtype)
    return out
```

```python
from contextlib import ExitStack

import concourse.bass as bass
from concourse import mybir

F32 = mybir.dt.float32
BF16 = mybir.dt.bfloat16
I32 = mybir.dt.int32
ALU = mybir.AluOpType
ACT = mybir.ActivationFunctionType
AX = mybir.AxisListType

P = 128
B, T, C = 2, 1024, 256
NT = B * T // P
TPB = T // P
KC = C // P
BANK = 512
LN_EPS = 1e-5

HEADS, HALF = 8, 16
HD = 2 * HALF
HPG = P // HD
GROUPS = HEADS // HPG
MAPS = 2 * HPG
CHUNK = 512
CHUNKS = T // CHUNK
KPC = CHUNK // P
LAMBDA_INIT = 0.8
RMS_EPS = 1.1920929e-07
PIECES = [(0, 0), (0, 1), (1, 0), (1, 1), (0, 2), (2, 0)]
STACK = len(PIECES) * HALF
PARTS = 3
DMA = 16


class Memory:

    BYTES = {F32: 4, BF16: 2, I32: 4}

    def __init__(self, nc, at):
        self.nc, self.at = nc, at

    def take(self, name, shape, dtype=F32):
        size = self.BYTES[dtype]
        for n in shape[1:]:
            size *= n
        t = self.nc.alloc_sbuf_tensor_at(name, shape, dtype, offset=self.at)
        self.at = -(-(self.at + size) // 32) * 32
        return t


def stats_are_in(dve, spare, stats, semaphore, value):
    dve.wait_ge(semaphore, value)
    dve.bn_stats(spare, stats)


def attention(nc, io, mem, X, ident, ps):
    norm_x = mem.take("norm_x", [P, TPB * C])
    norm_T = mem.take("norm_T", [P, KC, T])
    w_qk = [mem.take("w_q", [P, KC, C]), mem.take("w_k", [P, KC, C])]
    w_v = mem.take("w_v", [P, KC, C])
    w_o = mem.take("w_o", [P, KC, C])
    parts = [mem.take("q_parts", [P, PARTS, T], BF16), mem.take("k_parts", [P, PARTS, T], BF16)]
    stacks = [[mem.take(f"stack_{n}{g}", [STACK, MAPS, T], BF16) for n in "qk"] for g in range(GROUPS)]
    V = mem.take("V", [P, TPB * C])
    probs = mem.take("probs", [P, 3, HPG, CHUNK])
    yT = mem.take("yT", [P, GROUPS, T])
    square = mem.take("square", [P, 2, CHUNK])
    root = mem.take("root", [P, 2, CHUNK])
    unit_qk = mem.take("unit_qk", [P, 2, CHUNK])
    rest = mem.take("rest", [P, 2, CHUNK])
    rden = mem.take("rden", [P, 2, CHUNK])
    y_half = mem.take("y_half", [P, 2, CHUNK])
    causal = mem.take("causal", [P, HPG, P])
    same_half = mem.take("same_half", [P, P])
    ones = mem.take("ones", [P, HD])
    stats = mem.take("stats", [P, TPB + 1, 6])
    mean_var = mem.take("mean_var", [P, TPB, 2])
    rstd = mem.take("rstd", [P, TPB])
    power, eps = mem.take("power", [P, TPB]), mem.take("eps", [P, TPB])
    rms_eps = mem.take("rms_eps", [P, 1])
    lvec = mem.take("lvec", [P, 4, HD])
    lprod = mem.take("lprod", [P, 2, HD])
    lsum = mem.take("lsum", [P, 2])
    lexp = mem.take("lexp", [P, 2])
    neg_lambda = mem.take("neg_lambda", [P, 1])
    assert mem.at <= nc.sbuf_usable_end, mem.at
    scratch = [[nc.dram_tensor(f"parts_{n}{g}", [P, PARTS, T], BF16, kind="Internal").ap() for n in "qk"]
               for g in range(GROUPS)]

    sem = nc.alloc_semaphore
    x_loaded = [sem(f"x_loaded{b}") for b in range(B)]
    w_loaded = {n: sem(f"{n}_loaded") for n in ("wq", "wk", "wv", "wo")}
    l_loaded = sem("l_loaded")
    consts_ready, const_step = sem("consts_ready"), sem("const_step")
    ident_step = sem("ident_step")
    lambda_step, lexp_ready = sem("lambda_step"), sem("lexp_ready")
    stats_done, rstd_step, rstd_ready, normed = sem("stats_done"), sem("rstd_step"), sem("rstd_ready"), sem("normed")
    aggr_done = sem("aggr_done")
    turned, norm_T_ready = sem("turned"), sem("norm_T_ready")
    proj_ready, square_ready, sumsq_ready, root_ready = sem("proj_ready"), sem("square_ready"), sem("sumsq_ready"), sem("root_ready")
    recip_done, unit_done, first_done, rest_ready = sem("recip_done"), sem("unit_done"), sem("first_done"), sem("rest_ready")
    second_ready, split_done = sem("second_ready"), sem("split_done")
    parts_saved = [[sem(f"parts_saved_{n}{g}") for n in "qk"] for g in range(GROUPS)]
    stack_loaded = [[sem(f"stack_loaded_{n}{g}") for n in "qk"] for g in range(GROUPS)]
    v_ready, V_copied = sem("v_ready"), sem("V_copied")
    scores_ready, probs_ready, masked, pv_done = sem("scores_ready"), sem("probs_ready"), sem("masked"), sem("pv_done")
    rden_done, y_free, half_done, y_ready = sem("rden_done"), sem("y_free"), sem("half_done"), sem("y_ready")
    o_ready, o_added = sem("o_ready"), sem("o_added")

    plan = [(g, c, s, kt) for g in range(GROUPS) for c in range(CHUNKS) for s in range(2)
            for kt in range(KPC * (c + 1))]
    TILES = len(plan)
    BLOCKS = GROUPS * CHUNKS * 2
    UNITS = GROUPS * 2 * CHUNKS
    TURNS = CHUNKS * KC
    SLOTS = 3
    OB = TPB // 2

    def first_query(c, kt):
        return max(0, kt - KPC * c) * P

    def is_diagonal(n):
        _, c, _, kt = plan[n]
        return kt >= KPC * c

    def is_last(n):
        _, c, _, kt = plan[n]
        return kt == KPC * (c + 1) - 1

    DIAGONALS = sum(is_diagonal(n) for n in range(TILES))

    def unit(u):
        return u // (2 * CHUNKS), u // CHUNKS % 2, u % CHUNKS, 2 * (u % 4)

    block = nc.Block()
    block.__enter__()

    @block.sync
    def _(sp):
        x_view = io["x"].rearrange("(n p) c -> p n c", p=P)
        for b in range(B):
            sp.dma_start(X[:, b * TPB * C:(b + 1) * TPB * C].rearrange("p (n c) -> p n c", c=C),
                         x_view[:, b * TPB:(b + 1) * TPB, :]).then_inc(x_loaded[b], DMA)
            if b == 0:
                for n, w in (("wq", w_qk[0]), ("wk", w_qk[1]), ("wv", w_v), ("wo", w_o)):
                    sp.dma_start(w[:, :, :], io[n].rearrange("(k p) n -> p k n", p=P)).then_inc(w_loaded[n], DMA)
                for n, name in enumerate(("lq1", "lk1", "lq2", "lk2")):
                    sp.dma_start(lvec[:, n, :], io[name].partition_broadcast(P)).then_inc(l_loaded, DMA)
        for i in range(B):
            for g in range(GROUPS):
                for t in range(2):
                    sp.wait_ge(split_done, i * UNITS + (2 * g + t + 1) * CHUNKS)
                    sp.dma_start(scratch[g][t], parts[t][:, :, :]).then_inc(parts_saved[g][t], DMA)
                    sp.wait_ge(parts_saved[g][t], i * DMA + DMA)
                    rows = scratch[g][t].rearrange("(m r) a n -> r m a n", r=HALF)
                    for n, piece in enumerate(PIECES):
                        sp.dma_start(stacks[g][t][n * HALF:(n + 1) * HALF, :, :],
                                     rows[:, :, piece[t], :]).then_inc(stack_loaded[g][t], DMA)
            for g in range(GROUPS):
                for t in range(2):
                    sp.wait_ge(stack_loaded[g][t], (i + 1) * (len(PIECES) * DMA))
            sp.wait_ge(scores_ready, (i + 1) * (2 * TILES))

    @block.gpsimd
    def _(pool):
        pool.memset(ident[:, :], 0.0).then_inc(ident_step, 1)
        pool.memset(causal[:, :, :], 1.0).then_inc(const_step, 1)
        pool.memset(same_half[:, :], 1.0).then_inc(const_step, 1)
        pool.memset(ones[:, :], 1.0).then_inc(consts_ready, 1)
        pool.memset(rms_eps[:, :], RMS_EPS).then_inc(consts_ready, 1)
        pool.memset(power[:, :], -0.5).then_inc(consts_ready, 1)
        pool.memset(eps[:, :], LN_EPS).then_inc(consts_ready, 1)
        pool.wait_ge(ident_step, 1)
        pool.affine_select(out=ident[:, :], in_=ident[:, :], compare_op=ALU.not_equal, fill=1.0, base=0,
                           pattern=[[-1, P]], channel_multiplier=1).then_inc(consts_ready, 1)
        pool.wait_ge(const_step, 2)
        pool.affine_select(out=causal[:, :, :], in_=causal[:, :, :], compare_op=ALU.is_ge, fill=0.0, base=0,
                           pattern=[[0, HPG], [1, P]], channel_multiplier=-1).then_inc(consts_ready, 1)
        halves = same_half[:, :].rearrange("p (a r) -> p a r", r=HALF)
        pool.affine_select(out=halves, in_=halves, compare_op=ALU.is_ge, fill=0.0, base=0,
                           pattern=[[-HALF, MAPS], [0, HALF]], channel_multiplier=1).then_inc(const_step, 1)
        pool.wait_ge(const_step, 3)
        pool.affine_select(out=halves, in_=halves, compare_op=ALU.is_ge, fill=0.0, base=HALF - 1,
                           pattern=[[HALF, MAPS], [0, HALF]], channel_multiplier=-1).then_inc(consts_ready, 1)
        pool.wait_ge(consts_ready, 4)
        with pool.Fori(0, B) as i:
            pool.wait_ge(aggr_done, i * TPB + TPB)
            pool.tensor_tensor(rstd[:, :], mean_var[:, :, 1], eps[:, :], ALU.add).then_inc(rstd_step, 1)
            pool.wait_ge(rstd_step, i + 1)
            pool.tensor_tensor(rstd[:, :], rstd[:, :], power[:, :], ALU.pow).then_inc(rstd_ready, 1)
            for u in range(UNITS):
                _, t, c, _ = unit(u)
                cols = slice(c * CHUNK, (c + 1) * CHUNK)
                pool.wait_ge(second_ready, i * UNITS + u + 1)
                pool.tensor_tensor(parts[t][:, 2, cols], rest[:, u % 2, :], parts[t][:, 1, cols],
                                   ALU.subtract).then_inc(split_done, 1)
            pool.wait_ge(normed, i * TPB + TPB)

    @block.scalar
    def _(act):
        act.wait_ge(lambda_step, 2)
        act.activation(lexp[:, :], lsum[:, :], ACT.Exp).then_inc(lexp_ready, 1)
        act.wait_ge(consts_ready, 7)
        with act.Fori(0, B) as i:
            for n in range(TURNS):
                c, kc = divmod(n, KC)
                act.wait_ge(turned, i * TURNS + n + 1)
                act.activation(norm_T[:, kc, c * CHUNK:(c + 1) * CHUNK], ps[:, n, :], ACT.Copy)\
                   .then_inc(norm_T_ready, 1)

            def squares(u):
                act.wait_ge(proj_ready, i * UNITS + u + 1)
                act.activation(square[:, u % 2, :], ps[:, unit(u)[3], :], ACT.Square).then_inc(square_ready, 1)

            def second_part(u):
                _, t, c, _ = unit(u)
                act.wait_ge(rest_ready, i * UNITS + u + 1)
                act.activation(parts[t][:, 1, c * CHUNK:(c + 1) * CHUNK], rest[:, u % 2, :], ACT.Copy)\
                   .then_inc(second_ready, 1)

            squares(0)
            for u in range(UNITS):
                if u + 1 < UNITS:
                    squares(u + 1)
                act.wait_ge(sumsq_ready, i * UNITS + u + 1)
                if u >= 2:
                    act.wait_ge(unit_done, i * UNITS + u - 1)
                act.activation(root[:, u % 2, :], ps[:, unit(u)[3] + 1, :], ACT.Sqrt,
                               bias=rms_eps[:, :], scale=1.0 / HALF).then_inc(root_ready, 1)
                if u >= 1:
                    second_part(u - 1)
            second_part(UNITS - 1)
            for n in range(OB // 2):
                act.wait_ge(v_ready, i * (OB // 2) + n + 1)
                act.activation(V[:, n * 2 * BANK:(n + 1) * 2 * BANK],
                               ps[:, 2 * n:2 * n + 2, :].rearrange("p a b -> p (a b)"), ACT.Copy).then_inc(V_copied, 1)
            for n, (g, c, s, kt) in enumerate(plan):
                lo = first_query(c, kt)
                for pair in range(2):
                    act.wait_ge(scores_ready, i * 2 * TILES + 2 * n + pair + 1)
                    if pair == 0 and n >= SLOTS:
                        act.wait_ge(pv_done, i * TILES + n - SLOTS + 1)
                    bank = 2 * ((2 * n + pair) % SLOTS)
                    act.activation(probs[:, n % SLOTS, 2 * pair:2 * pair + 2, lo:], ps[:, bank:bank + 2, lo:],
                                   ACT.Exp, scale=HALF ** -0.5).then_inc(probs_ready, 1)
            act.wait_ge(pv_done, i * TILES + TILES)

    @block.vector
    def _(dve):
        dve.wait_ge(l_loaded, 4 * DMA)
        for n in range(2):
            dve.tensor_tensor_reduce(out=lprod[:, n, :], in0=lvec[:, 2 * n, :], in1=lvec[:, 2 * n + 1, :], scale=1.0,
                                     scalar=0.0, op0=ALU.mult, op1=ALU.add,
                                     accum_out=lsum[:, n:n + 1]).then_inc(lambda_step, 1)
        dve.wait_ge(lexp_ready, 1)
        dve.tensor_tensor(neg_lambda[:, :], lexp[:, 1:2], lexp[:, 0:1], ALU.subtract).then_inc(lambda_step, 1)
        dve.wait_ge(lambda_step, 3)
        dve.tensor_scalar(neg_lambda[:, :], neg_lambda[:, :], -LAMBDA_INIT, None, ALU.add).then_inc(lambda_step, 1)
        dve.wait_ge(lambda_step, 4)
        dve.wait_ge(x_loaded[0], DMA)
        with dve.Fori(0, B) as i:
            for t in range(TPB):
                dve.bn_stats(stats[:, t, :], X[:, bass.ds(i * (TPB * C) + t * C, C)]).then_inc(stats_done, 1)
            stats_are_in(dve, stats[:, TPB, :], stats[:, 0, :], stats_done, i * TPB + TPB)
            for t in range(TPB):
                dve.bn_aggr(mean_var[:, t, :], stats[:, t, :]).then_inc(aggr_done, 1)
            dve.wait_ge(rstd_ready, i + 1)
            for t in range(TPB):
                dve.tensor_scalar(norm_x[:, t * C:(t + 1) * C], X[:, bass.ds(i * (TPB * C) + t * C, C)],
                                  mean_var[:, t, 0:1], rstd[:, t:t + 1], ALU.subtract, ALU.mult).then_inc(normed, 1)
            for u in range(UNITS):
                g, t, c, bank = unit(u)
                cols = slice(c * CHUNK, (c + 1) * CHUNK)
                now = i * UNITS + u + 1
                dve.wait_ge(root_ready, now)
                dve.reciprocal(root[:, u % 2, :], root[:, u % 2, :]).then_inc(recip_done, 1)
                dve.wait_ge(recip_done, now)
                dve.tensor_tensor(unit_qk[:, u % 2, :], ps[:, bank, :], root[:, u % 2, :], ALU.mult)\
                   .then_inc(unit_done, 1)
                dve.wait_ge(unit_done, now)
                if c == 0 and g > 0:
                    dve.wait_ge(parts_saved[g - 1][t], i * DMA + DMA)
                dve.tensor_copy(parts[t][:, 0, cols], unit_qk[:, u % 2, :]).then_inc(first_done, 1)
                dve.wait_ge(first_done, now)
                if u >= 2:
                    dve.wait_ge(split_done, i * UNITS + u - 1)
                dve.tensor_tensor(rest[:, u % 2, :], unit_qk[:, u % 2, :], parts[t][:, 0, cols], ALU.subtract)\
                   .then_inc(rest_ready, 1)
            diagonals = blocks = 0
            for n, (g, c, s, kt) in enumerate(plan):
                if is_diagonal(n):
                    lo = first_query(c, kt)
                    dve.wait_ge(probs_ready, i * 2 * TILES + 2 * n + 2)
                    seen = probs[:, n % SLOTS, :, lo:lo + P]
                    dve.tensor_tensor(seen, seen, causal[:, :, :], ALU.mult).then_inc(masked, 1)
                if is_last(n):
                    dve.wait_ge(pv_done, i * TILES + n + 1)
                    dve.reciprocal(rden[:, s, :], ps[:, 7, :]).then_inc(rden_done, 1)
                    dve.wait_ge(rden_done, i * BLOCKS + blocks + 1)
                    dve.tensor_tensor(y_half[:, s, :], ps[:, 6, :], rden[:, s, :], ALU.mult).then_inc(y_free, 1)
                    blocks += 1
                    if s == 1:
                        dve.wait_ge(y_free, i * BLOCKS + blocks)
                        dve.scalar_tensor_tensor(yT[:, g, c * CHUNK:(c + 1) * CHUNK], y_half[:, 1, :],
                                                 neg_lambda[:, :], y_half[:, 0, :], ALU.mult, ALU.add)\
                           .then_inc(y_ready, 1)
            for n in range(OB):
                dve.wait_ge(o_ready, i * OB + n + 1)
                tiles = X[:, bass.ds(i * (TPB * C) + n * BANK, BANK)]
                dve.scalar_tensor_tensor(tiles, ps[:, n, :], 1.0 - LAMBDA_INIT, tiles, ALU.mult, ALU.add)\
                   .then_inc(o_added, 1)
            dve.wait_ge(turned, i * TURNS + TURNS)
            dve.wait_ge(split_done, i * UNITS + UNITS)
            for t in range(2):
                dve.wait_ge(parts_saved[GROUPS - 1][t], i * DMA + DMA)
            dve.wait_ge(x_loaded[1], DMA)
        dve.wait_ge(o_added, B * OB)

    @block.tensor
    def _(pe):
        pe.wait_ge(consts_ready, 7)
        for n in ("wq", "wk", "wv", "wo"):
            pe.wait_ge(w_loaded[n], DMA)
        with pe.Fori(0, B) as i:
            for n in range(TURNS):
                c, kc = divmod(n, KC)
                pe.wait_ge(normed, i * TPB + (c + 1) * KPC)
                for t in range(KPC):
                    at = (c * KPC + t) * C + kc * P
                    last = pe.transpose(ps[:, n, t * P:(t + 1) * P], norm_x[:, at:at + P], ident[:, :])
                last.then_inc(turned, 1)
            pe.wait_ge(norm_T_ready, i * TURNS + TURNS)

            def project(u):
                g, t, c, bank = unit(u)
                if u >= 4:
                    pe.wait_ge(unit_done, i * UNITS + u - 3)
                for kc in range(KC):
                    last = pe.matmul(ps[:, bank, :], w_qk[t][:, kc, g * P:(g + 1) * P],
                                     norm_T[:, kc, c * CHUNK:(c + 1) * CHUNK], start=kc == 0, stop=kc == KC - 1)
                last.then_inc(proj_ready, 1)

            project(0)
            for u in range(UNITS):
                if u + 1 < UNITS:
                    project(u + 1)
                pe.wait_ge(square_ready, i * UNITS + u + 1)
                pe.matmul(ps[:, unit(u)[3] + 1, :], same_half[:, :], square[:, u % 2, :], start=True, stop=True)\
                  .then_inc(sumsq_ready, 1)
            pe.wait_ge(unit_done, i * UNITS + UNITS)
            for t in range(TPB):
                for kc in range(KC):
                    last = pe.matmul(ps[:, t // 2, t % 2 * C:(t % 2 + 1) * C], norm_T[:, kc, t * P:(t + 1) * P],
                                     w_v[:, kc, :], start=kc == 0, stop=kc == KC - 1)
                if t % 4 == 3:
                    last.then_inc(v_ready, 1)
            pe.wait_ge(V_copied, i * (OB // 2) + OB // 2)

            def scores(n):
                g, c, s, kt = plan[n]
                lo = first_query(c, kt)
                if n == 0 or plan[n - 1][0] != g:
                    for t in range(2):
                        pe.wait_ge(stack_loaded[g][t], (i + 1) * (len(PIECES) * DMA))
                for pair in range(2):
                    o = 2 * n + pair
                    if o >= SLOTS:
                        pe.wait_ge(probs_ready, i * 2 * TILES + o - SLOTS + 1)
                    for j in range(2):
                        m = (2 * pair + j) * 2 + s
                        last = pe.matmul(ps[:, 2 * (o % SLOTS) + j, lo:], stacks[g][1][:, m, kt * P:(kt + 1) * P],
                                         stacks[g][0][:, m, c * CHUNK + lo:(c + 1) * CHUNK], start=True, stop=True)
                    last.then_inc(scores_ready, 1)

            diagonals = blocks = 0
            scores(0)
            for n, (g, c, s, kt) in enumerate(plan):
                lo = first_query(c, kt)
                if n + 1 < TILES:
                    scores(n + 1)
                if kt == 0 and blocks:
                    pe.wait_ge(y_free, i * BLOCKS + blocks)
                pe.wait_ge(probs_ready, i * 2 * TILES + 2 * n + 2)
                if is_diagonal(n):
                    diagonals += 1
                    pe.wait_ge(masked, i * DIAGONALS + diagonals)
                for h in range(HPG):
                    at = kt * C + (g * HPG + h) * HD
                    pe.matmul(ps[h * HD:(h + 1) * HD, 6, lo:], V[:, at:at + HD], probs[:, n % SLOTS, h, lo:],
                              start=kt == 0, stop=is_last(n))
                for h in range(HPG):
                    last = pe.matmul(ps[h * HD:(h + 1) * HD, 7, lo:], ones[:, :], probs[:, n % SLOTS, h, lo:],
                                     start=kt == 0, stop=is_last(n))
                last.then_inc(pv_done, 1)
                blocks += is_last(n)
            pe.wait_ge(y_ready, i * (BLOCKS // 2) + BLOCKS // 2)
            for t in range(TPB):
                for g in range(GROUPS):
                    last = pe.matmul(ps[:, t // 2, t % 2 * C:(t % 2 + 1) * C], yT[:, g, t * P:(t + 1) * P],
                                     w_o[:, g, :], start=g == 0, stop=g == GROUPS - 1)
                if t % 2:
                    last.then_inc(o_ready, 1)
            pe.wait_ge(o_added, i * OB + OB)

    block.__exit__(None, None, None)


MEM, MW, RH, RD = 256, 128, 8, 128
MC = MEM // P
STEPS = 3
EVALS = 5
ACT_HEADS = 6

HID0, HID1 = 1024, 688
F0, F1 = HID0 // P, -(-HID1 // P)
LUT = 16
FC = 512
TPF = FC // P


def retrieval_weights(nc, io, mem, W, ident, ps):
    mem_x = mem.take("mem_x", [P, MC, MW])
    mem_n = mem.take("mem_n", [P, MC, MW])
    mem_T = mem.take("mem_T", [P, MEM])
    wk = mem.take("r_wk", [P, RH * RD])
    wv = mem.take("r_wv", [P, RH * RD])
    wq = mem.take("r_wq", [P, RH, C])
    wo = mem.take("r_wo", [P, RH, C])
    K = mem.take("r_K", [P, RH, MEM])
    V = mem.take("r_V", [P, RH, MEM])
    gb_mem = mem.take("gb_mem", [P, 2])
    beta = mem.take("beta", [P, RH])
    stats = mem.take("m_stats", [P, MC, 6])
    mean_var = mem.take("m_mean_var", [P, MC, 2])
    rstd = mem.take("m_rstd", [P, MC])
    power, eps = mem.take("m_power", [P, MC]), mem.take("m_eps", [P, MC])
    assert mem.at <= nc.sbuf_usable_end, mem.at
    sem = nc.alloc_semaphore
    loaded = {n: sem(f"m_{n}_loaded") for n in ("x", "gb", "beta", "wk", "wv", "wq", "wo")}
    state_loaded = sem("state_loaded")
    stats_done, aggr_done, rstd_step, normed = sem("m_stats_done"), sem("m_aggr_done"), sem("m_rstd_step"), sem("m_normed")
    power_set = sem("m_power_set")
    turned, mem_T_ready, beta_step = sem("m_turned"), sem("m_mem_T_ready"), sem("m_beta_step")
    kv_ready, K_copied, V_copied = sem("kv_ready"), sem("K_copied"), sem("m_V_copied")
    product_ready, product_copied = sem("product_ready"), [sem("product_copied_act"), sem("product_copied_dve")]
    groups = [(a, pair) for a in range(3) for pair in range(RH // 2)]

    with nc.Block() as block:
        @block.sync
        def _(sp):
            sp.dma_start(mem_x[:, :, :], io["memory"].rearrange("(n p) c -> p n c", p=P)).then_inc(loaded["x"], DMA)
            sp.dma_start(gb_mem[:, 0:1], io["g_mem"].rearrange("(p a) -> p a", a=1)).then_inc(loaded["gb"], DMA)
            sp.dma_start(gb_mem[:, 1:2], io["b_mem"].rearrange("(p a) -> p a", a=1)).then_inc(loaded["gb"], DMA)
            sp.dma_start(beta[:, :], io["log_beta"].partition_broadcast(P)).then_inc(loaded["beta"], DMA)
            sp.dma_start(wk[:, :], io["Wk"]).then_inc(loaded["wk"], DMA)
            sp.dma_start(wv[:, :], io["Wv"]).then_inc(loaded["wv"], DMA)
            sp.dma_start(wq[:, :, :], io["Wq"].rearrange("(h d) c -> d h c", d=RD)).then_inc(loaded["wq"], DMA)
            sp.dma_start(wo[:, :, :], io["Wo"].rearrange("(h d) c -> d h c", d=RD)).then_inc(loaded["wo"], DMA)
            sp.dma_start(W["g_state"][:, :], io["g_state"]).then_inc(state_loaded, DMA)
            sp.dma_start(W["b_state"][:, :], io["b_state"]).then_inc(state_loaded, DMA)
            sp.wait_ge(state_loaded, 2 * DMA)

        @block.gpsimd
        def _(pool):
            pool.memset(power[:, :], -0.5).then_inc(power_set, 1)
            pool.memset(eps[:, :], LN_EPS).then_inc(power_set, 1)
            pool.wait_ge(power_set, 2)
            pool.wait_ge(aggr_done, MC)
            pool.tensor_tensor(rstd[:, :], mean_var[:, :, 1], eps[:, :], ALU.add).then_inc(rstd_step, 1)
            pool.wait_ge(rstd_step, 1)
            pool.tensor_tensor(rstd[:, :], rstd[:, :], power[:, :], ALU.pow).then_inc(rstd_step, 1)

        @block.scalar
        def _(act):
            act.wait_ge(loaded["beta"], DMA)
            act.activation(beta[:, :], beta[:, :], ACT.Exp).then_inc(beta_step, 1)
            act.wait_ge(turned, 1)
            act.wait_ge(loaded["gb"], 2 * DMA)
            act.activation(mem_T[:, :], ps[:, 0, 0:MEM], ACT.Identity, scale=gb_mem[:, 0:1], bias=gb_mem[:, 1:2])\
               .then_inc(mem_T_ready, 1)
            for n in range(RH // 4):
                act.wait_ge(kv_ready, RH // 4 + n + 1)
                act.activation(V[:, 4 * n:4 * n + 4, :].rearrange("p a b -> p (a b)"),
                               ps[:, 4 + 2 * n:6 + 2 * n, :].rearrange("p a b -> p (a b)"), ACT.Copy).then_inc(V_copied, 1)
            for n, (a, pair) in enumerate(groups):
                if n % 2 == 0:
                    act.wait_ge(product_ready, n + 1)
                    bank = 2 * (n % 4)
                    act.activation(W["GMU"][a][:, 2 * pair * MC:(2 * pair + 2) * MC, :].rearrange("p a b -> p (a b)"),
                                   ps[:, bank:bank + 2, :].rearrange("p a b -> p (a b)"), ACT.Copy)\
                       .then_inc(product_copied[0], 1)
            act.wait_ge(product_copied[0], len(groups) // 2)

        @block.vector
        def _(dve):
            dve.wait_ge(loaded["x"], DMA)
            for n in range(MC):
                dve.bn_stats(stats[:, n, :], mem_x[:, n, :]).then_inc(stats_done, 1)
            for n in range(MC):
                dve.wait_ge(stats_done, n + 1)
                dve.bn_aggr(mean_var[:, n, :], stats[:, n, :]).then_inc(aggr_done, 1)
            dve.wait_ge(rstd_step, 2)
            for n in range(MC):
                dve.tensor_scalar(mem_n[:, n, :], mem_x[:, n, :], mean_var[:, n, 0:1], rstd[:, n:n + 1],
                                  ALU.subtract, ALU.mult).then_inc(normed, 1)
            dve.wait_ge(beta_step, 1)
            dve.tensor_scalar(beta[:, :], beta[:, :], 0.5, None, ALU.mult).then_inc(beta_step, 1)
            dve.wait_ge(beta_step, 2)
            for h in range(RH):
                dve.wait_ge(kv_ready, h // 4 + 1)
                dve.tensor_scalar(K[:, h, :], ps[:, h // 2, h % 2 * MEM:(h % 2 + 1) * MEM], beta[:, h:h + 1], None,
                                  ALU.mult).then_inc(K_copied, 1)
            for n, (a, pair) in enumerate(groups):
                if n % 2 == 1:
                    dve.wait_ge(product_ready, n + 1)
                    bank = 2 * (n % 4)
                    dve.tensor_copy(W["GMU"][a][:, 2 * pair * MC:(2 * pair + 2) * MC, :].rearrange("p a b -> p (a b)"),
                                    ps[:, bank:bank + 2, :].rearrange("p a b -> p (a b)")).then_inc(product_copied[1], 1)
            dve.wait_ge(product_copied[1], len(groups) // 2)

        @block.tensor
        def _(pe):
            pe.wait_ge(normed, MC)
            for n in range(MC):
                last = pe.transpose(ps[:, 0, n * P:(n + 1) * P], mem_n[:, n, :], ident[:, :])
            last.then_inc(turned, 1)
            pe.wait_ge(mem_T_ready, 1)
            for name, w, bank in (("wk", wk, 0), ("wv", wv, 4)):
                pe.wait_ge(loaded[name], DMA)
                for h in range(RH):
                    last = pe.matmul(ps[:, bank + h // 2, h % 2 * MEM:(h % 2 + 1) * MEM], w[:, h * RD:(h + 1) * RD],
                                     mem_T[:, :], start=True, stop=True)
                    if h % 4 == 3:
                        last.then_inc(kv_ready, 1)
            pe.wait_ge(K_copied, RH)
            pe.wait_ge(V_copied, RH // 4)
            pe.wait_ge(loaded["wq"], DMA)
            pe.wait_ge(loaded["wo"], DMA)
            for n, (a, pair) in enumerate(groups):
                if n >= 4:
                    pe.wait_ge(product_copied[n % 2], (n - 4) // 2 + 1)
                left, right = ((wq, K), (V, K), (V, wo))[a]
                for k in range(2 * MC):
                    h, block_ = 2 * pair + k // MC, k % MC
                    last = pe.matmul(ps[:, 2 * (n % 4) + k // 2, k % 2 * MEM:(k % 2 + 1) * MEM],
                                     left[:, h, block_ * P:(block_ + 1) * P], right[:, h, :], start=True, stop=True)
                last.then_inc(product_ready, 1)


def retrieval(nc, io, mem, X, W, ident, ps):
    R = 2
    TURNS = NT // R
    G, M, U = W["GMU"]
    norm_x = [mem.take(f"rt_norm_x{r}", [P, C]) for r in range(R)]
    hid_T = [mem.take(f"rt_hid_T{r}", [P, KC, P]) for r in range(R)]
    S = [mem.take(f"rt_scores{r}", [P, RH, MEM]) for r in range(R)]
    over = [mem.take(f"rt_over{r}", [P, RH, MEM]) for r in range(R)]
    weights_T = [mem.take(f"rt_weights_T{r}", [P, RH * MC, P]) for r in range(R)]
    stats = [mem.take(f"rt_stats{r}", [P, RH, 2, 3]) for r in range(R)]
    small = [[mem.take(f"rt_small{r}{n}", [P, RH, 2]) for n in range(2)] for r in range(R)]
    vec = {(n, r): mem.take(f"rt_{n}{r}", [P, RH]) for r in range(R)
           for n in ("top", "nt", "s2", "root", "s1", "step")}
    x_stats = [mem.take(f"rt_x_stats{r}", [P, 6]) for r in range(R + 1)]
    mean_var = mem.take("rt_mean_var", [P, R, 2])
    v1, v2, v3 = (mem.take(f"rt_v{n}", [P, R]) for n in range(3))
    power, eps = mem.take("rt_power", [P, R]), mem.take("rt_eps", [P, R])
    assert mem.at <= nc.sbuf_usable_end, mem.at
    sem = nc.alloc_semaphore
    each = lambda name: [sem(f"rt_{name}{r}") for r in range(R)]
    power_set = sem("rt_power_set")
    x_stats_done, aggr_done, rstd_step, normed = sem("rt_x_stats_done"), sem("rt_aggr_done"), sem("rt_rstd_step"), each("normed")
    turn_full, turn_taken = sem("rt_turn_full"), sem("rt_turn_taken")
    scores_full, scores_taken = sem("rt_scores_full"), sem("rt_scores_taken")
    top_done, nt_ready = each("top_done"), each("nt_ready")
    act_relu, dve_relu = each("act_relu"), each("dve_relu")
    stats_ready, s2_ready, root_ready, chain = each("stats_ready"), each("s2_ready"), each("root_ready"), each("chain")
    out_full, out_added = each("out_full"), each("out_added")
    DVE_HEADS = RH - ACT_HEADS
    RELUS = EVALS + 1
    TG = RH * MC // 4
    LINKS = 6

    turns = [("hid", r, 0, 0) for r in range(R)] + [("w", r, s, n) for s in range(STEPS) for r in range(R) for n in range(TG)]
    turn_no = {use: n for n, use in enumerate(turns)}
    uses = [(s, r, half) for s in range(STEPS) for r in range(R) for half in range(2)]
    use_no = {use: n for n, use in enumerate(uses)}
    TU, SU = len(turns), len(uses)

    with nc.Block() as block:
        @block.gpsimd
        def _(pool):
            pool.memset(power[:, :], -0.5).then_inc(power_set, 1)
            pool.memset(eps[:, :], LN_EPS).then_inc(power_set, 1)
            pool.wait_ge(power_set, 2)
            with pool.Fori(0, TURNS) as i:
                pool.wait_ge(aggr_done, i * R + R)
                var = mean_var[:, :, 1]
                links = ((v1, var, eps, ALU.add), (v1, v1[:, :], power, ALU.pow), (v2, v1[:, :], v1, ALU.mult),
                         (v2, v2[:, :], None, ALU.mult), (v2, v2[:, :], eps, ALU.add),
                         (v2, v2[:, :], power, ALU.pow), (v3, v1[:, :], v2, ALU.mult))
                for n, (out, a, b, op) in enumerate(links):
                    if n:
                        pool.wait_ge(rstd_step, i * len(links) + n)
                    pool.tensor_tensor(out[:, :], a, var if b is None else b[:, :], op).then_inc(rstd_step, 1)
                pool.wait_ge(normed[R - 1], i + 1)

        @block.scalar
        def _(act):
            with act.Fori(0, TURNS) as i:
                for r in range(R):
                    act.wait_ge(turn_full, i * TU + r + 1)
                    for kc in range(KC):
                        ins = act.activation(hid_T[r][:, kc, :], ps[:, 4 + r, kc * P:(kc + 1) * P], ACT.Identity,
                                             scale=W["g_state"][:, kc:kc + 1], bias=W["b_state"][:, kc:kc + 1])
                    ins.then_inc(turn_taken, 1)

                def take_scores(s, r):
                    for half in range(2):
                        n = use_no[s, r, half]
                        act.wait_ge(scores_full, i * SU + n + 1)
                        bank = 2 * (n % 2)
                        act.activation(S[r][:, 4 * half:4 * half + 4, :].rearrange("p a b -> p (a b)"),
                                       ps[:, bank:bank + 2, :].rearrange("p a b -> p (a b)"), ACT.Copy)\
                           .then_inc(scores_taken, 1)

                def relus(s, r, k):
                    act.wait_ge(nt_ready[r], i * STEPS * RELUS + s * RELUS + k + 1)
                    for h in range(ACT_HEADS):
                        act.activation(over[r][:, h, :], S[r][:, h, :], ACT.Relu, bias=vec["nt", r][:, h:h + 1])\
                           .then_inc(act_relu[r], 1)

                def root(s, r, k):
                    act.wait_ge(s2_ready[r], i * STEPS * EVALS + s * EVALS + k + 1)
                    act.activation(vec["root", r][:, :], vec["s2", r][:, :], ACT.Sqrt).then_inc(root_ready[r], 1)

                def squares(s, r):
                    for n in range(TG):
                        u = turn_no["w", r, s, n]
                        act.wait_ge(turn_full, i * TU + u + 1)
                        act.activation(weights_T[r][:, 4 * n:4 * n + 4, :].rearrange("p a b -> p (a b)"),
                                       ps[:, 4 + u % 2, :], ACT.Square).then_inc(turn_taken, 1)

                for s in range(STEPS):
                    for r in range(R):
                        take_scores(s, r)
                    relus(s, 0, 0)
                    for k in range(EVALS):
                        relus(s, 1, k)
                        root(s, 0, k)
                        relus(s, 0, k + 1)
                        root(s, 1, k)
                    relus(s, 1, EVALS)
                    for r in range(R):
                        squares(s, r)

        @block.vector
        def _(dve):
            with dve.Fori(0, TURNS) as i:
                x_of = [X[:, bass.ds(i * (R * C) + r * C, C)] for r in range(R)]
                for r in range(R):
                    dve.bn_stats(x_stats[r][:, :], x_of[r]).then_inc(x_stats_done, 1)
                stats_are_in(dve, x_stats[R][:, :], x_stats[0][:, :], x_stats_done, i * R + R)
                for r in range(R):
                    dve.bn_aggr(mean_var[:, r, :], x_stats[r][:, :]).then_inc(aggr_done, 1)
                dve.wait_ge(rstd_step, i * 7 + 7)
                for r in range(R):
                    dve.tensor_scalar(norm_x[r][:, :], x_of[r], mean_var[:, r, 0:1], v3[:, r:r + 1],
                                      ALU.subtract, ALU.mult).then_inc(normed[r], 1)

                def start(s, r):
                    base = i * STEPS * 2 + s * 2
                    for half in range(2):
                        dve.wait_ge(scores_taken, i * SU + use_no[s, r, half] + 1)
                        dve.reduce_max(vec["top", r][:, 4 * half:4 * half + 4], S[r][:, 4 * half:4 * half + 4, :], AX.X)\
                           .then_inc(top_done[r], 1)
                    dve.wait_ge(top_done[r], base + 2)
                    dve.tensor_scalar(vec["nt", r][:, :], vec["top", r][:, :], -1.0, 1.0, ALU.mult, ALU.add)\
                       .then_inc(nt_ready[r], 1)
                    dve.wait_ge(nt_ready[r], i * STEPS * RELUS + s * RELUS + 1)

                def own_relus(s, r, k):
                    for h in range(ACT_HEADS, RH):
                        dve.tensor_scalar(over[r][:, h, :], S[r][:, h, :], vec["nt", r][:, h:h + 1], 0.0,
                                          ALU.add, ALU.max).then_inc(dve_relu[r], 1)

                def evaluate(s, r, k):
                    own_relus(s, r, k)
                    step = i * STEPS * RELUS + s * RELUS + k
                    for h in range(RH):
                        if h < ACT_HEADS:
                            dve.wait_ge(act_relu[r], step * ACT_HEADS + h + 1)
                        else:
                            dve.wait_ge(dve_relu[r], step * DVE_HEADS + h - ACT_HEADS + 1)
                        dve.bn_stats(stats[r][:, h, :, :].rearrange("p a b -> p (a b)"), over[r][:, h, :])\
                           .then_inc(stats_ready[r], 1)

                def newton(s, r, k):
                    e = i * STEPS * EVALS + s * EVALS + k
                    half_n = float(MEM // 2)
                    mean, m2 = stats[r][:, :, :, 1], stats[r][:, :, :, 2]
                    sq, q = small[r]
                    s2, rt, s1, step, nt = (vec[n, r] for n in ("s2", "root", "s1", "step", "nt"))
                    dve.wait_ge(stats_ready[r], e * RH + RH)
                    dve.tensor_tensor(sq[:, :, :], mean, mean, ALU.mult).then_inc(chain[r], 1)
                    dve.tensor_tensor(s1[:, :], stats[r][:, :, 0, 1], stats[r][:, :, 1, 1], ALU.add).then_inc(chain[r], 1)
                    dve.wait_ge(chain[r], e * LINKS + 1)
                    dve.scalar_tensor_tensor(q[:, :, :], sq[:, :, :], half_n, m2, ALU.mult, ALU.add).then_inc(chain[r], 1)
                    dve.wait_ge(chain[r], e * LINKS + 3)
                    dve.tensor_tensor(s2[:, :], q[:, :, 0], q[:, :, 1], ALU.add).then_inc(s2_ready[r], 1)
                    dve.reciprocal(s1[:, :], s1[:, :]).then_inc(chain[r], 1)
                    dve.wait_ge(root_ready[r], e + 1)
                    dve.tensor_tensor(step[:, :], s2[:, :], rt[:, :], ALU.subtract).then_inc(chain[r], 1)
                    dve.wait_ge(chain[r], e * LINKS + 5)
                    dve.tensor_tensor(step[:, :], step[:, :], s1[:, :], ALU.mult).then_inc(chain[r], 1)
                    dve.wait_ge(chain[r], e * LINKS + 6)
                    dve.scalar_tensor_tensor(nt[:, :], step[:, :], -1.0 / half_n, nt[:, :], ALU.mult, ALU.add)\
                       .then_inc(nt_ready[r], 1)
                    dve.wait_ge(nt_ready[r], i * STEPS * RELUS + s * RELUS + k + 2)

                for s in range(STEPS):
                    for r in range(R):
                        start(s, r)
                    for k in range(EVALS):
                        for r in range(R):
                            evaluate(s, r, k)
                            newton(s, r, k)
                    for r in range(R):
                        own_relus(s, r, EVALS)
                for r in range(R):
                    dve.wait_ge(out_full[r], i + 1)
                    dve.tensor_tensor(x_of[r], x_of[r], ps[:, 6 + r, 0:C], ALU.add).then_inc(out_added[r], 1)
            for r in range(R):
                dve.wait_ge(out_added[r], TURNS)

        @block.tensor
        def _(pe):
            with pe.Fori(0, TURNS) as i:
                for r in range(R):
                    pe.wait_ge(normed[r], i + 1)
                    for kc in range(KC):
                        last = pe.transpose(ps[:, 4 + r, kc * P:(kc + 1) * P], norm_x[r][:, kc * P:(kc + 1) * P], ident[:, :])
                    last.then_inc(turn_full, 1)

                def scores(s, r):
                    if s == 0:
                        pe.wait_ge(turn_taken, i * TU + r + 1)
                        left, right = hid_T[r], G
                    else:
                        left, right = weights_T[r], M
                    for half in range(2):
                        n = use_no[s, r, half]
                        if n >= 2:
                            pe.wait_ge(scores_taken, i * SU + n - 1)
                        for h in range(4 * half, 4 * half + 4):
                            if s and h % 2 == 0:
                                pe.wait_ge(turn_taken, i * TU + turn_no["w", r, s - 1, h // 2] + 1)
                            for b in range(MC):
                                last = pe.matmul(ps[:, 2 * (n % 2) + h % 4 // 2, h % 2 * MEM:(h % 2 + 1) * MEM],
                                                 left[:, b if s == 0 else h * MC + b, :], right[:, h * MC + b, :],
                                                 start=b == 0, stop=b == MC - 1)
                        last.then_inc(scores_full, 1)

                def turn_weights(s, r):
                    for n in range(TG):
                        u = turn_no["w", r, s, n]
                        pe.wait_ge(turn_taken, i * TU + u - 1)
                        last_relu = i * STEPS * RELUS + s * RELUS + EVALS
                        for h in (2 * n, 2 * n + 1):
                            if h < ACT_HEADS:
                                pe.wait_ge(act_relu[r], last_relu * ACT_HEADS + h + 1)
                            else:
                                pe.wait_ge(dve_relu[r], last_relu * DVE_HEADS + h - ACT_HEADS + 1)
                            for b in range(MC):
                                last = pe.transpose(ps[:, 4 + u % 2, (h % 2 * MC + b) * P:(h % 2 * MC + b + 1) * P],
                                                    over[r][:, h, b * P:(b + 1) * P], ident[:, :])
                        last.then_inc(turn_full, 1)

                def output(r):
                    for n in range(RH * MC):
                        if n % 4 == 0:
                            pe.wait_ge(turn_taken, i * TU + turn_no["w", r, STEPS - 1, n // 4] + 1)
                        last = pe.matmul(ps[:, 6 + r, 0:C], weights_T[r][:, n, :], U[:, n, :],
                                         start=n == 0, stop=n == RH * MC - 1)
                    last.then_inc(out_full[r], 1)

                for r in range(R):
                    scores(0, r)
                for s in range(STEPS):
                    for r in range(R):
                        turn_weights(s, r)
                        if s + 1 < STEPS:
                            scores(s + 1, r)
                        else:
                            output(r)
                pe.wait_ge(turn_taken, i * TU + TU)
                for r in range(R):
                    pe.wait_ge(out_added[r], i + 1)


def lut_weights(nc, io, mem, W):
    names = ("gate", "up", "down")
    cols = {"gate": KC * HID1, "up": KC * HID1, "down": F1 * C}
    out = {"gate": W["w_gate1"], "up": W["w_up1"], "down": W["w_down1"]}
    NC = max(cols.values())
    idx = [mem.take(f"idx_{n}", [P, NC], I32) for n in names]
    low = mem.take("lut_low", [P, NC])
    bit = [mem.take(f"lut_bit{k}", [P, NC], I32) for k in range(4)]
    leaf = [mem.take(f"lut_leaf{k}", [P, NC]) for k in range(LUT // 2)]
    lut = mem.take("lut", [P, LUT])
    delta = mem.take("lut_delta", [P, LUT // 2])
    assert mem.at <= nc.sbuf_usable_end, mem.at
    sem = nc.alloc_semaphore
    idx_zeroed, lut_loaded = sem("idx_zeroed"), sem("lut_loaded")
    idx_loaded = {n: sem(f"idx_{n}_loaded") for n in names}
    step, placed = sem("lut_step"), sem("lut_placed")
    full = HID1 // P * P

    with nc.Block() as block:
        @block.sync
        def _(sp):
            sp.dma_start(lut[:, :], io["lut"].partition_broadcast(P)).then_inc(lut_loaded, DMA)
            for n in range(2):
                sp.dma_start(idx[n][:, 0:cols[names[n]]].rearrange("p (k n) -> p k n", k=KC),
                             io[f"{names[n]}_idx"].rearrange("(k p) n -> p k n", p=P)).then_inc(idx_loaded[names[n]], DMA)
            down = idx[2][:, :].rearrange("p (k n) -> p k n", n=C)
            sp.wait_ge(idx_zeroed, 1)
            sp.dma_start(down[:, 0:F1 - 1, :], io["down_idx"][0:full, :].rearrange("(k p) n -> p k n", p=P))\
              .then_inc(idx_loaded["down"], DMA)
            sp.dma_start(down[0:HID1 - full, F1 - 1, :], io["down_idx"][full:HID1, :]).then_inc(idx_loaded["down"], DMA)

        @block.gpsimd
        def _(pool):
            pool.memset(idx[2][:, (F1 - 1) * C:F1 * C], 0).then_inc(idx_zeroed, 1)
            for a in ("w_gate1", "w_up1"):
                pool.memset(W[a][:, :, HID1:F1 * P], 0.0).then_inc(placed, 1)
            pool.wait_ge(placed, 2)

        @block.vector
        def _(dve):
            count = [0]

            def link(ins):
                count[0] += 1
                ins.then_inc(step, 1)
                dve.wait_ge(step, count[0])

            dve.wait_ge(lut_loaded, DMA)
            pairs = lut[:, :].rearrange("p (k e) -> p k e", e=2)
            link(dve.tensor_tensor(delta[:, :], pairs[:, :, 1], pairs[:, :, 0], ALU.subtract))
            for a, name in enumerate(names):
                n = cols[name]
                dve.wait_ge(idx_loaded[name], DMA * (2 if name == "down" else 1))
                for k in range(4):
                    link(dve.tensor_scalar(bit[k][:, 0:n], idx[a][:, 0:n], 1 << k, None, ALU.bitwise_and))
                link(dve.tensor_copy(low[:, 0:n], bit[0][:, 0:n]))
                for k in range(LUT // 2):
                    link(dve.tensor_scalar(leaf[k][:, 0:n], low[:, 0:n], delta[:, k:k + 1], pairs[:, k, 0:1], ALU.mult, ALU.add))
                for k in range(1, 4):
                    stride = 1 << (k - 1)
                    for left in range(0, LUT // 2, 2 * stride):
                        link(dve.copy_predicated(leaf[left][:, 0:n], bit[k][:, 0:n], leaf[left + stride][:, 0:n]))
                if name == "down":
                    link(dve.tensor_copy(out[name][:, :, :].rearrange("p k n -> p (k n)"), leaf[0][:, 0:n]))
                else:
                    link(dve.tensor_copy(out[name][:, :, 0:HID1], leaf[0][:, 0:n].rearrange("p (k n) -> p k n", k=KC)))


def ffn(nc, mem, X, w_gate, w_up, w_down, hidden_blocks, ident, ps, name):
    TURNS = NT // TPF
    norm_x = mem.take(f"{name}_norm_x", [P, TPF * C])
    norm_T = mem.take(f"{name}_norm_T", [P, KC, FC])
    gate = mem.take(f"{name}_gate", [P, 2, FC])
    hidden = mem.take(f"{name}_hidden", [P, 2, FC])
    stats = mem.take(f"{name}_stats", [P, TPF + 1, 6])
    mean_var = mem.take(f"{name}_mean_var", [P, TPF, 2])
    rstd = mem.take(f"{name}_rstd", [P, TPF])
    power, eps = mem.take(f"{name}_power", [P, TPF]), mem.take(f"{name}_eps", [P, TPF])
    assert mem.at <= nc.sbuf_usable_end, mem.at
    sem = lambda n: nc.alloc_semaphore(f"{name}_{n}")
    power_set, stats_done, aggr_done, rstd_step, normed = (sem(n) for n in ("power_set", "stats_done", "aggr_done", "rstd_step", "normed"))
    turned, norm_T_ready = sem("turned"), sem("norm_T_ready")
    gate_full, up_full, gate_ready, hidden_ready, down_done, added = \
        (sem(n) for n in ("gate_full", "up_full", "gate_ready", "hidden_ready", "down_done", "added"))
    F = hidden_blocks

    with nc.Block() as block:
        @block.gpsimd
        def _(pool):
            pool.memset(power[:, :], -0.5).then_inc(power_set, 1)
            pool.memset(eps[:, :], LN_EPS).then_inc(power_set, 1)
            pool.wait_ge(power_set, 2)
            with pool.Fori(0, TURNS) as i:
                pool.wait_ge(aggr_done, i * TPF + TPF)
                pool.tensor_tensor(rstd[:, :], mean_var[:, :, 1], eps[:, :], ALU.add).then_inc(rstd_step, 1)
                pool.wait_ge(rstd_step, i * 2 + 1)
                pool.tensor_tensor(rstd[:, :], rstd[:, :], power[:, :], ALU.pow).then_inc(rstd_step, 1)
                pool.wait_ge(normed, i * TPF + TPF)

        @block.scalar
        def _(act):
            with act.Fori(0, TURNS) as i:
                for kc in range(KC):
                    act.wait_ge(turned, i * KC + kc + 1)
                    act.activation(norm_T[:, kc, :], ps[:, kc, :], ACT.Copy).then_inc(norm_T_ready, 1)
                for f in range(F):
                    act.wait_ge(gate_full, i * F + f + 1)
                    if f >= 2:
                        act.wait_ge(hidden_ready, i * F + f - 1)
                    act.activation(gate[:, f % 2, :], ps[:, 2 * (f % 2), :], ACT.Silu).then_inc(gate_ready, 1)

        @block.vector
        def _(dve):
            with dve.Fori(0, TURNS) as i:
                tile = [X[:, bass.ds(i * (TPF * C) + t * C, C)] for t in range(TPF)]
                for t in range(TPF):
                    dve.bn_stats(stats[:, t, :], tile[t]).then_inc(stats_done, 1)
                stats_are_in(dve, stats[:, TPF, :], stats[:, 0, :], stats_done, i * TPF + TPF)
                for t in range(TPF):
                    dve.bn_aggr(mean_var[:, t, :], stats[:, t, :]).then_inc(aggr_done, 1)
                dve.wait_ge(rstd_step, i * 2 + 2)
                for t in range(TPF):
                    dve.tensor_scalar(norm_x[:, t * C:(t + 1) * C], tile[t], mean_var[:, t, 0:1], rstd[:, t:t + 1],
                                      ALU.subtract, ALU.mult).then_inc(normed, 1)
                for f in range(F):
                    dve.wait_ge(gate_ready, i * F + f + 1)
                    dve.wait_ge(up_full, i * F + f + 1)
                    if f >= 2:
                        dve.wait_ge(down_done, i * F + f - 1)
                    dve.tensor_tensor(hidden[:, f % 2, :], gate[:, f % 2, :], ps[:, 2 * (f % 2) + 1, :], ALU.mult)\
                       .then_inc(hidden_ready, 1)
                dve.wait_ge(down_done, i * F + F)
                both = X[:, bass.ds(i * (TPF * C), TPF * C)].rearrange("p (t c) -> p t c", c=C)
                dve.tensor_tensor(both, both, ps[:, 4:4 + TPF, 0:C], ALU.add).then_inc(added, 1)
            dve.wait_ge(added, TURNS)

        @block.tensor
        def _(pe):
            with pe.Fori(0, TURNS) as i:
                pe.wait_ge(normed, i * TPF + TPF)
                for kc in range(KC):
                    for t in range(TPF):
                        last = pe.transpose(ps[:, kc, t * P:(t + 1) * P], norm_x[:, t * C + kc * P:t * C + (kc + 1) * P],
                                            ident[:, :])
                    last.then_inc(turned, 1)
                pe.wait_ge(norm_T_ready, i * KC + KC)

                def gate_up(f):
                    if f >= 2:
                        pe.wait_ge(gate_ready, i * F + f - 1)
                    for w, bank, full in ((w_gate, 0, gate_full), (w_up, 1, up_full)):
                        if w is w_up and f >= 2:
                            pe.wait_ge(hidden_ready, i * F + f - 1)
                        for kc in range(KC):
                            last = pe.matmul(ps[:, 2 * (f % 2) + bank, :], w[:, kc, f * P:(f + 1) * P], norm_T[:, kc, :],
                                             start=kc == 0, stop=kc == KC - 1)
                        last.then_inc(full, 1)

                gate_up(0)
                for f in range(F):
                    if f + 1 < F:
                        gate_up(f + 1)
                    pe.wait_ge(hidden_ready, i * F + f + 1)
                    for t in range(TPF):
                        last = pe.matmul(ps[:, 4 + t, 0:C], hidden[:, f % 2, t * P:(t + 1) * P], w_down[:, f, :],
                                         start=f == 0, stop=f == F - 1)
                    last.then_inc(down_done, 1)
                pe.wait_ge(added, i + 1)


def build(nc, io, out):
    mem = Memory(nc, 16512)
    X = mem.take("X", [P, NT * C])
    ident = mem.take("ident", [P, P])
    W = {"g_state": mem.take("g_state", [P, KC]), "b_state": mem.take("b_state", [P, KC])}
    ps = nc.alloc_psum_tensor("banks", [P, 8, BANK], F32)
    base = mem.at
    attention(nc, io, mem, X, ident, ps)

    mem.at = base
    W["GMU"] = [mem.take(f"w_{n}", [P, RH * MC, C]) for n in "GMU"]
    for n, shape in (("w_gate1", [P, KC, F1 * P]), ("w_up1", [P, KC, F1 * P]), ("w_down1", [P, F1, C])):
        W[n] = mem.take(n, shape)
    base = mem.at
    lut_weights(nc, io, mem, W)
    mem.at = base
    retrieval_weights(nc, io, mem, W, ident, ps)

    mem.at = base
    w0 = {n: mem.take(f"w_{n}0", shape) for n, shape in (("gate", [P, KC, HID0]), ("up", [P, KC, HID0]), ("down", [P, F0, C]))}
    w0_loaded = nc.alloc_semaphore("w0_loaded")
    with nc.Block() as block:
        @block.sync
        def _(sp):
            for n in ("gate", "up", "down"):
                sp.dma_start(w0[n][:, :, :], io[f"w_{n}"].rearrange("(k p) n -> p k n", p=P)).then_inc(w0_loaded, DMA)
            sp.wait_ge(w0_loaded, 3 * DMA)
    ffn(nc, mem, X, w0["gate"], w0["up"], w0["down"], F0, ident, ps, "ffn0")
    mem.at = base
    retrieval(nc, io, mem, X, W, ident, ps)
    mem.at = base
    ffn(nc, mem, X, W["w_gate1"], W["w_up1"], W["w_down1"], F1, ident, ps, "ffn1")

    stored = nc.alloc_semaphore("stored")
    with nc.Block() as block:
        @block.sync
        def _(sp):
            sp.dma_start(out.rearrange("(n p) c -> p n c", p=P), X[:, :].rearrange("p (n c) -> p n c", c=C))\
              .then_inc(stored, DMA)
            sp.wait_ge(stored, DMA)


def kernel(**inputs):
    import numpy as np
    import concourse.bacc as bacc
    from concourse.bass_utils import run_bass_kernel_spmd

    a0 = lambda n: np.asarray(inputs[f"L0_attn_{n}"])
    a1 = lambda n: np.asarray(inputs[f"L1_attn_{n}"])
    f0 = lambda n: np.asarray(inputs[f"L0_ffn_{n}"])
    f1 = lambda n: np.asarray(inputs[f"L1_ffn_{n}"])
    arrays = {"x": a0("x").reshape(B * T, C)}
    arrays.update({n: a0(n).T for n in ("wq", "wk", "wv", "wo")})
    arrays.update({n: a0(n) for n in ("lq1", "lk1", "lq2", "lk2")})
    arrays.update({n: f0(n).T for n in ("w_gate", "w_up", "w_down")})
    arrays.update({n: a1(n) for n in ("memory", "Wq", "log_beta", "g_mem", "b_mem")})
    arrays.update({n: a1(n).T for n in ("Wk", "Wv", "Wo")})
    arrays.update({n: a1(n).reshape(KC, P).T for n in ("g_state", "b_state")})
    arrays["lut"] = f1("lut")
    arrays.update({n: f1(n).T for n in ("gate_idx", "up_idx", "down_idx")})
    arrays = {n: np.ascontiguousarray(a) for n, a in arrays.items()}

    nc = bacc.Bacc("TRN2", target_bir_lowering=False, num_devices=1)
    io = {n: nc.dram_tensor(f"in_{n}", a.shape, mybir.dt.from_np(a.dtype), kind="ExternalInput").ap()
          for n, a in arrays.items()}
    out = nc.dram_tensor("out", (B * T, C), F32, kind="ExternalOutput").ap()
    build(nc, io, out)
    r = run_bass_kernel_spmd(nc, [{f"in_{n}": a for n, a in arrays.items()}], core_ids=[0])
    return r.results[0]["out"].reshape(B, T, C)
```

```python
from contextlib import ExitStack

import concourse.bass as bass
from concourse import mybir

F32 = mybir.dt.float32
BF16 = mybir.dt.bfloat16
I32 = mybir.dt.int32
ALU = mybir.AluOpType
ACT = mybir.ActivationFunctionType
AX = mybir.AxisListType

P = 128
B, T, C = 2, 1024, 256
NT = B * T // P
TPB = T // P
KC = C // P
BANK = 512
LN_EPS = 1e-5

HEADS, HALF = 8, 16
HD = 2 * HALF
HPG = P // HD
GROUPS = HEADS // HPG
MAPS = 2 * HPG
CHUNK = 512
CHUNKS = T // CHUNK
KPC = CHUNK // P
LAMBDA_INIT = 0.8
RMS_EPS = 1.1920929e-07
PIECES = [(0, 0), (0, 1), (1, 0), (1, 1), (0, 2), (2, 0)]
STACK = len(PIECES) * HALF
PARTS = 3
DMA = 16


class Memory:

    BYTES = {F32: 4, BF16: 2, I32: 4}

    def __init__(self, nc, at):
        self.nc, self.at = nc, at

    def take(self, name, shape, dtype=F32):
        size = self.BYTES[dtype]
        for n in shape[1:]:
            size *= n
        t = self.nc.alloc_sbuf_tensor_at(name, shape, dtype, offset=self.at)
        self.at = -(-(self.at + size) // 32) * 32
        return t


def stats_are_in(dve, spare, stats, semaphore, value):
    dve.wait_ge(semaphore, value)
    dve.bn_stats(spare, stats)


def attention(nc, io, mem, X, ident, ps):
    norm_x = mem.take("norm_x", [P, TPB * C])
    norm_T = mem.take("norm_T", [P, KC, T])
    w_qk = [mem.take("w_q", [P, KC, C]), mem.take("w_k", [P, KC, C])]
    w_v = mem.take("w_v", [P, KC, C])
    w_o = mem.take("w_o", [P, KC, C])
    parts = [mem.take("q_parts", [P, PARTS, T], BF16), mem.take("k_parts", [P, PARTS, T], BF16)]
    stacks = [[mem.take(f"stack_{n}{g}", [STACK, MAPS, T], BF16) for n in "qk"] for g in range(GROUPS)]
    V = mem.take("V", [P, TPB * C])
    probs = mem.take("probs", [P, 3, HPG, CHUNK])
    yT = mem.take("yT", [P, GROUPS, T])
    square = mem.take("square", [P, 2, CHUNK])
    root = mem.take("root", [P, 2, CHUNK])
    unit_qk = mem.take("unit_qk", [P, 2, CHUNK])
    rest = mem.take("rest", [P, 2, CHUNK])
    rden = mem.take("rden", [P, 2, CHUNK])
    y_half = mem.take("y_half", [P, 2, CHUNK])
    causal = mem.take("causal", [P, HPG, P])
    same_half = mem.take("same_half", [P, P])
    ones = mem.take("ones", [P, HD])
    stats = mem.take("stats", [P, TPB + 1, 6])
    mean_var = mem.take("mean_var", [P, TPB, 2])
    rstd = mem.take("rstd", [P, TPB])
    power, eps = mem.take("power", [P, TPB]), mem.take("eps", [P, TPB])
    rms_eps = mem.take("rms_eps", [P, 1])
    lvec = mem.take("lvec", [P, 4, HD])
    lprod = mem.take("lprod", [P, 2, HD])
    lsum = mem.take("lsum", [P, 2])
    lexp = mem.take("lexp", [P, 2])
    neg_lambda = mem.take("neg_lambda", [P, 1])
    assert mem.at <= nc.sbuf_usable_end, mem.at
    scratch = [[nc.dram_tensor(f"parts_{n}{g}", [P, PARTS, T], BF16, kind="Internal").ap() for n in "qk"]
               for g in range(GROUPS)]

    sem = nc.alloc_semaphore
    x_loaded = [sem(f"x_loaded{b}") for b in range(B)]
    w_loaded = {n: sem(f"{n}_loaded") for n in ("wq", "wk", "wv", "wo")}
    l_loaded = sem("l_loaded")
    consts_ready, const_step = sem("consts_ready"), sem("const_step")
    ident_step = sem("ident_step")
    lambda_step, lexp_ready = sem("lambda_step"), sem("lexp_ready")
    stats_done, rstd_step, rstd_ready, normed = sem("stats_done"), sem("rstd_step"), sem("rstd_ready"), sem("normed")
    aggr_done = sem("aggr_done")
    turned, norm_T_ready = sem("turned"), sem("norm_T_ready")
    proj_ready, square_ready, sumsq_ready, root_ready = sem("proj_ready"), sem("square_ready"), sem("sumsq_ready"), sem("root_ready")
    recip_done, unit_done, first_done, rest_ready = sem("recip_done"), sem("unit_done"), sem("first_done"), sem("rest_ready")
    second_ready, split_done = sem("second_ready"), sem("split_done")
    parts_saved = [[sem(f"parts_saved_{n}{g}") for n in "qk"] for g in range(GROUPS)]
    stack_loaded = [[sem(f"stack_loaded_{n}{g}") for n in "qk"] for g in range(GROUPS)]
    v_ready, V_copied = sem("v_ready"), sem("V_copied")
    scores_ready, probs_ready, masked, pv_done = sem("scores_ready"), sem("probs_ready"), sem("masked"), sem("pv_done")
    rden_done, y_free, half_done, y_ready = sem("rden_done"), sem("y_free"), sem("half_done"), sem("y_ready")
    o_ready, o_added = sem("o_ready"), sem("o_added")

    plan = [(g, c, s, kt) for g in range(GROUPS) for c in range(CHUNKS) for s in range(2)
            for kt in range(KPC * (c + 1))]
    TILES = len(plan)
    BLOCKS = GROUPS * CHUNKS * 2
    UNITS = GROUPS * 2 * CHUNKS
    TURNS = CHUNKS * KC
    SLOTS = 3
    OB = TPB // 2

    def first_query(c, kt):
        return max(0, kt - KPC * c) * P

    def is_diagonal(n):
        _, c, _, kt = plan[n]
        return kt >= KPC * c

    def is_last(n):
        _, c, _, kt = plan[n]
        return kt == KPC * (c + 1) - 1

    DIAGONALS = sum(is_diagonal(n) for n in range(TILES))

    def unit(u):
        return u // (2 * CHUNKS), u // CHUNKS % 2, u % CHUNKS, 2 * (u % 4)

    block = nc.Block()
    block.__enter__()

    @block.sync
    def _(sp):
        x_view = io["x"].rearrange("(n p) c -> p n c", p=P)
        for b in range(B):
            sp.dma_start(X[:, b * TPB * C:(b + 1) * TPB * C].rearrange("p (n c) -> p n c", c=C),
                         x_view[:, b * TPB:(b + 1) * TPB, :]).then_inc(x_loaded[b], DMA)
            if b == 0:
                for n, w in (("wq", w_qk[0]), ("wk", w_qk[1]), ("wv", w_v), ("wo", w_o)):
                    sp.dma_start(w[:, :, :], io[n].rearrange("(k p) n -> p k n", p=P)).then_inc(w_loaded[n], DMA)
                for n, name in enumerate(("lq1", "lk1", "lq2", "lk2")):
                    sp.dma_start(lvec[:, n, :], io[name].partition_broadcast(P)).then_inc(l_loaded, DMA)
        for i in range(B):
            for g in range(GROUPS):
                for t in range(2):
                    sp.wait_ge(split_done, i * UNITS + (2 * g + t + 1) * CHUNKS)
                    sp.dma_start(scratch[g][t], parts[t][:, :, :]).then_inc(parts_saved[g][t], DMA)
                    sp.wait_ge(parts_saved[g][t], i * DMA + DMA)
                    rows = scratch[g][t].rearrange("(m r) a n -> r m a n", r=HALF)
                    for n, piece in enumerate(PIECES):
                        sp.dma_start(stacks[g][t][n * HALF:(n + 1) * HALF, :, :],
                                     rows[:, :, piece[t], :]).then_inc(stack_loaded[g][t], DMA)
            for g in range(GROUPS):
                for t in range(2):
                    sp.wait_ge(stack_loaded[g][t], (i + 1) * (len(PIECES) * DMA))
            sp.wait_ge(scores_ready, (i + 1) * (2 * TILES))

    @block.gpsimd
    def _(pool):
        pool.memset(ident[:, :], 0.0).then_inc(ident_step, 1)
        pool.memset(causal[:, :, :], 1.0).then_inc(const_step, 1)
        pool.memset(same_half[:, :], 1.0).then_inc(const_step, 1)
        pool.memset(ones[:, :], 1.0).then_inc(consts_ready, 1)
        pool.memset(rms_eps[:, :], RMS_EPS).then_inc(consts_ready, 1)
        pool.memset(power[:, :], -0.5).then_inc(consts_ready, 1)
        pool.memset(eps[:, :], LN_EPS).then_inc(consts_ready, 1)
        pool.wait_ge(ident_step, 1)
        pool.affine_select(out=ident[:, :], in_=ident[:, :], compare_op=ALU.not_equal, fill=1.0, base=0,
                           pattern=[[-1, P]], channel_multiplier=1).then_inc(consts_ready, 1)
        pool.wait_ge(const_step, 2)
        pool.affine_select(out=causal[:, :, :], in_=causal[:, :, :], compare_op=ALU.is_ge, fill=0.0, base=0,
                           pattern=[[0, HPG], [1, P]], channel_multiplier=-1).then_inc(consts_ready, 1)
        halves = same_half[:, :].rearrange("p (a r) -> p a r", r=HALF)
        pool.affine_select(out=halves, in_=halves, compare_op=ALU.is_ge, fill=0.0, base=0,
                           pattern=[[-HALF, MAPS], [0, HALF]], channel_multiplier=1).then_inc(const_step, 1)
        pool.wait_ge(const_step, 3)
        pool.affine_select(out=halves, in_=halves, compare_op=ALU.is_ge, fill=0.0, base=HALF - 1,
                           pattern=[[HALF, MAPS], [0, HALF]], channel_multiplier=-1).then_inc(consts_ready, 1)
        pool.wait_ge(consts_ready, 4)
        with pool.Fori(0, B) as i:
            pool.wait_ge(aggr_done, i * TPB + TPB)
            pool.tensor_tensor(rstd[:, :], mean_var[:, :, 1], eps[:, :], ALU.add).then_inc(rstd_step, 1)
            pool.wait_ge(rstd_step, i + 1)
            pool.tensor_tensor(rstd[:, :], rstd[:, :], power[:, :], ALU.pow).then_inc(rstd_ready, 1)
            for u in range(UNITS):
                _, t, c, _ = unit(u)
                cols = slice(c * CHUNK, (c + 1) * CHUNK)
                pool.wait_ge(second_ready, i * UNITS + u + 1)
                pool.tensor_tensor(parts[t][:, 2, cols], rest[:, u % 2, :], parts[t][:, 1, cols],
                                   ALU.subtract).then_inc(split_done, 1)
            pool.wait_ge(normed, i * TPB + TPB)

    @block.scalar
    def _(act):
        act.wait_ge(lambda_step, 2)
        act.activation(lexp[:, :], lsum[:, :], ACT.Exp).then_inc(lexp_ready, 1)
        act.wait_ge(consts_ready, 7)
        with act.Fori(0, B) as i:
            for n in range(TURNS):
                c, kc = divmod(n, KC)
                act.wait_ge(turned, i * TURNS + n + 1)
                act.activation(norm_T[:, kc, c * CHUNK:(c + 1) * CHUNK], ps[:, n, :], ACT.Copy)\
                   .then_inc(norm_T_ready, 1)

            def squares(u):
                act.wait_ge(proj_ready, i * UNITS + u + 1)
                act.activation(square[:, u % 2, :], ps[:, unit(u)[3], :], ACT.Square).then_inc(square_ready, 1)

            def second_part(u):
                _, t, c, _ = unit(u)
                act.wait_ge(rest_ready, i * UNITS + u + 1)
                act.activation(parts[t][:, 1, c * CHUNK:(c + 1) * CHUNK], rest[:, u % 2, :], ACT.Copy)\
                   .then_inc(second_ready, 1)

            squares(0)
            for u in range(UNITS):
                if u + 1 < UNITS:
                    squares(u + 1)
                act.wait_ge(sumsq_ready, i * UNITS + u + 1)
                if u >= 2:
                    act.wait_ge(unit_done, i * UNITS + u - 1)
                act.activation(root[:, u % 2, :], ps[:, unit(u)[3] + 1, :], ACT.Sqrt,
                               bias=rms_eps[:, :], scale=1.0 / HALF).then_inc(root_ready, 1)
                if u >= 1:
                    second_part(u - 1)
            second_part(UNITS - 1)
            for n in range(OB // 2):
                act.wait_ge(v_ready, i * (OB // 2) + n + 1)
                act.activation(V[:, n * 2 * BANK:(n + 1) * 2 * BANK],
                               ps[:, 2 * n:2 * n + 2, :].rearrange("p a b -> p (a b)"), ACT.Copy).then_inc(V_copied, 1)
            for n, (g, c, s, kt) in enumerate(plan):
                lo = first_query(c, kt)
                for pair in range(2):
                    act.wait_ge(scores_ready, i * 2 * TILES + 2 * n + pair + 1)
                    if pair == 0 and n >= SLOTS:
                        act.wait_ge(pv_done, i * TILES + n - SLOTS + 1)
                    bank = 2 * ((2 * n + pair) % SLOTS)
                    act.activation(probs[:, n % SLOTS, 2 * pair:2 * pair + 2, lo:], ps[:, bank:bank + 2, lo:],
                                   ACT.Exp, scale=HALF ** -0.5).then_inc(probs_ready, 1)
            act.wait_ge(pv_done, i * TILES + TILES)

    @block.vector
    def _(dve):
        dve.wait_ge(l_loaded, 4 * DMA)
        for n in range(2):
            dve.tensor_tensor_reduce(out=lprod[:, n, :], in0=lvec[:, 2 * n, :], in1=lvec[:, 2 * n + 1, :], scale=1.0,
                                     scalar=0.0, op0=ALU.mult, op1=ALU.add,
                                     accum_out=lsum[:, n:n + 1]).then_inc(lambda_step, 1)
        dve.wait_ge(lexp_ready, 1)
        dve.tensor_tensor(neg_lambda[:, :], lexp[:, 1:2], lexp[:, 0:1], ALU.subtract).then_inc(lambda_step, 1)
        dve.wait_ge(lambda_step, 3)
        dve.tensor_scalar(neg_lambda[:, :], neg_lambda[:, :], -LAMBDA_INIT, None, ALU.add).then_inc(lambda_step, 1)
        dve.wait_ge(lambda_step, 4)
        dve.wait_ge(x_loaded[0], DMA)
        with dve.Fori(0, B) as i:
            for t in range(TPB):
                dve.bn_stats(stats[:, t, :], X[:, bass.ds(i * (TPB * C) + t * C, C)]).then_inc(stats_done, 1)
            stats_are_in(dve, stats[:, TPB, :], stats[:, 0, :], stats_done, i * TPB + TPB)
            for t in range(TPB):
                dve.bn_aggr(mean_var[:, t, :], stats[:, t, :]).then_inc(aggr_done, 1)
            dve.wait_ge(rstd_ready, i + 1)
            for t in range(TPB):
                dve.tensor_scalar(norm_x[:, t * C:(t + 1) * C], X[:, bass.ds(i * (TPB * C) + t * C, C)],
                                  mean_var[:, t, 0:1], rstd[:, t:t + 1], ALU.subtract, ALU.mult).then_inc(normed, 1)
            for u in range(UNITS):
                g, t, c, bank = unit(u)
                cols = slice(c * CHUNK, (c + 1) * CHUNK)
                now = i * UNITS + u + 1
                dve.wait_ge(root_ready, now)
                dve.reciprocal(root[:, u % 2, :], root[:, u % 2, :]).then_inc(recip_done, 1)
                dve.wait_ge(recip_done, now)
                dve.tensor_tensor(unit_qk[:, u % 2, :], ps[:, bank, :], root[:, u % 2, :], ALU.mult)\
                   .then_inc(unit_done, 1)
                dve.wait_ge(unit_done, now)
                if c == 0 and g > 0:
                    dve.wait_ge(parts_saved[g - 1][t], i * DMA + DMA)
                dve.tensor_copy(parts[t][:, 0, cols], unit_qk[:, u % 2, :]).then_inc(first_done, 1)
                dve.wait_ge(first_done, now)
                if u >= 2:
                    dve.wait_ge(split_done, i * UNITS + u - 1)
                dve.tensor_tensor(rest[:, u % 2, :], unit_qk[:, u % 2, :], parts[t][:, 0, cols], ALU.subtract)\
                   .then_inc(rest_ready, 1)
            diagonals = blocks = 0
            for n, (g, c, s, kt) in enumerate(plan):
                if is_diagonal(n):
                    lo = first_query(c, kt)
                    dve.wait_ge(probs_ready, i * 2 * TILES + 2 * n + 2)
                    seen = probs[:, n % SLOTS, :, lo:lo + P]
                    dve.tensor_tensor(seen, seen, causal[:, :, :], ALU.mult).then_inc(masked, 1)
                if is_last(n):
                    dve.wait_ge(pv_done, i * TILES + n + 1)
                    dve.reciprocal(rden[:, s, :], ps[:, 7, :]).then_inc(rden_done, 1)
                    dve.wait_ge(rden_done, i * BLOCKS + blocks + 1)
                    dve.tensor_tensor(y_half[:, s, :], ps[:, 6, :], rden[:, s, :], ALU.mult).then_inc(y_free, 1)
                    blocks += 1
                    if s == 1:
                        dve.wait_ge(y_free, i * BLOCKS + blocks)
                        dve.scalar_tensor_tensor(yT[:, g, c * CHUNK:(c + 1) * CHUNK], y_half[:, 1, :],
                                                 neg_lambda[:, :], y_half[:, 0, :], ALU.mult, ALU.add)\
                           .then_inc(y_ready, 1)
            for n in range(OB):
                dve.wait_ge(o_ready, i * OB + n + 1)
                tiles = X[:, bass.ds(i * (TPB * C) + n * BANK, BANK)]
                dve.scalar_tensor_tensor(tiles, ps[:, n, :], 1.0 - LAMBDA_INIT, tiles, ALU.mult, ALU.add)\
                   .then_inc(o_added, 1)
            dve.wait_ge(turned, i * TURNS + TURNS)
            dve.wait_ge(split_done, i * UNITS + UNITS)
            for t in range(2):
                dve.wait_ge(parts_saved[GROUPS - 1][t], i * DMA + DMA)
            dve.wait_ge(x_loaded[1], DMA)
        dve.wait_ge(o_added, B * OB)

    @block.tensor
    def _(pe):
        pe.wait_ge(consts_ready, 7)
        for n in ("wq", "wk", "wv", "wo"):
            pe.wait_ge(w_loaded[n], DMA)
        with pe.Fori(0, B) as i:
            for n in range(TURNS):
                c, kc = divmod(n, KC)
                pe.wait_ge(normed, i * TPB + (c + 1) * KPC)
                for t in range(KPC):
                    at = (c * KPC + t) * C + kc * P
                    last = pe.transpose(ps[:, n, t * P:(t + 1) * P], norm_x[:, at:at + P], ident[:, :])
                last.then_inc(turned, 1)
            pe.wait_ge(norm_T_ready, i * TURNS + TURNS)

            def project(u):
                g, t, c, bank = unit(u)
                if u >= 4:
                    pe.wait_ge(unit_done, i * UNITS + u - 3)
                for kc in range(KC):
                    last = pe.matmul(ps[:, bank, :], w_qk[t][:, kc, g * P:(g + 1) * P],
                                     norm_T[:, kc, c * CHUNK:(c + 1) * CHUNK], start=kc == 0, stop=kc == KC - 1)
                last.then_inc(proj_ready, 1)

            project(0)
            for u in range(UNITS):
                if u + 1 < UNITS:
                    project(u + 1)
                pe.wait_ge(square_ready, i * UNITS + u + 1)
                pe.matmul(ps[:, unit(u)[3] + 1, :], same_half[:, :], square[:, u % 2, :], start=True, stop=True)\
                  .then_inc(sumsq_ready, 1)
            pe.wait_ge(unit_done, i * UNITS + UNITS)
            for t in range(TPB):
                for kc in range(KC):
                    last = pe.matmul(ps[:, t // 2, t % 2 * C:(t % 2 + 1) * C], norm_T[:, kc, t * P:(t + 1) * P],
                                     w_v[:, kc, :], start=kc == 0, stop=kc == KC - 1)
                if t % 4 == 3:
                    last.then_inc(v_ready, 1)
            pe.wait_ge(V_copied, i * (OB // 2) + OB // 2)

            def scores(n):
                g, c, s, kt = plan[n]
                lo = first_query(c, kt)
                if n == 0 or plan[n - 1][0] != g:
                    for t in range(2):
                        pe.wait_ge(stack_loaded[g][t], (i + 1) * (len(PIECES) * DMA))
                for pair in range(2):
                    o = 2 * n + pair
                    if o >= SLOTS:
                        pe.wait_ge(probs_ready, i * 2 * TILES + o - SLOTS + 1)
                    for j in range(2):
                        m = (2 * pair + j) * 2 + s
                        last = pe.matmul(ps[:, 2 * (o % SLOTS) + j, lo:], stacks[g][1][:, m, kt * P:(kt + 1) * P],
                                         stacks[g][0][:, m, c * CHUNK + lo:(c + 1) * CHUNK], start=True, stop=True)
                    last.then_inc(scores_ready, 1)

            diagonals = blocks = 0
            scores(0)
            for n, (g, c, s, kt) in enumerate(plan):
                lo = first_query(c, kt)
                if n + 1 < TILES:
                    scores(n + 1)
                if kt == 0 and blocks:
                    pe.wait_ge(y_free, i * BLOCKS + blocks)
                pe.wait_ge(probs_ready, i * 2 * TILES + 2 * n + 2)
                if is_diagonal(n):
                    diagonals += 1
                    pe.wait_ge(masked, i * DIAGONALS + diagonals)
                for h in range(HPG):
                    at = kt * C + (g * HPG + h) * HD
                    pe.matmul(ps[h * HD:(h + 1) * HD, 6, lo:], V[:, at:at + HD], probs[:, n % SLOTS, h, lo:],
                              start=kt == 0, stop=is_last(n))
                for h in range(HPG):
                    last = pe.matmul(ps[h * HD:(h + 1) * HD, 7, lo:], ones[:, :], probs[:, n % SLOTS, h, lo:],
                                     start=kt == 0, stop=is_last(n))
                last.then_inc(pv_done, 1)
                blocks += is_last(n)
            pe.wait_ge(y_ready, i * (BLOCKS // 2) + BLOCKS // 2)
            for t in range(TPB):
                for g in range(GROUPS):
                    last = pe.matmul(ps[:, t // 2, t % 2 * C:(t % 2 + 1) * C], yT[:, g, t * P:(t + 1) * P],
                                     w_o[:, g, :], start=g == 0, stop=g == GROUPS - 1)
                if t % 2:
                    last.then_inc(o_ready, 1)
            pe.wait_ge(o_added, i * OB + OB)

    block.__exit__(None, None, None)


MEM, MW, RH, RD = 256, 128, 8, 128
MC = MEM // P
STEPS = 3
EVALS = 5
ACT_HEADS = 6

HID0, HID1 = 1024, 688
F0, F1 = HID0 // P, -(-HID1 // P)
LUT = 16
FC = 512
TPF = FC // P


def retrieval_weights(nc, io, mem, W, ident, ps):
    mem_x = mem.take("mem_x", [P, MC, MW])
    mem_n = mem.take("mem_n", [P, MC, MW])
    mem_T = mem.take("mem_T", [P, MEM])
    wk = mem.take("r_wk", [P, RH * RD])
    wv = mem.take("r_wv", [P, RH * RD])
    wq = mem.take("r_wq", [P, RH, C])
    wo = mem.take("r_wo", [P, RH, C])
    K = mem.take("r_K", [P, RH, MEM])
    V = mem.take("r_V", [P, RH, MEM])
    gb_mem = mem.take("gb_mem", [P, 2])
    beta = mem.take("beta", [P, RH])
    stats = mem.take("m_stats", [P, MC, 6])
    mean_var = mem.take("m_mean_var", [P, MC, 2])
    rstd = mem.take("m_rstd", [P, MC])
    power, eps = mem.take("m_power", [P, MC]), mem.take("m_eps", [P, MC])
    assert mem.at <= nc.sbuf_usable_end, mem.at
    sem = nc.alloc_semaphore
    loaded = {n: sem(f"m_{n}_loaded") for n in ("x", "gb", "beta", "wk", "wv", "wq", "wo")}
    state_loaded = sem("state_loaded")
    stats_done, aggr_done, rstd_step, normed = sem("m_stats_done"), sem("m_aggr_done"), sem("m_rstd_step"), sem("m_normed")
    power_set = sem("m_power_set")
    turned, mem_T_ready, beta_step = sem("m_turned"), sem("m_mem_T_ready"), sem("m_beta_step")
    kv_ready, K_copied, V_copied = sem("kv_ready"), sem("K_copied"), sem("m_V_copied")
    product_ready, product_copied = sem("product_ready"), [sem("product_copied_act"), sem("product_copied_dve")]
    groups = [(a, pair) for a in range(3) for pair in range(RH // 2)]

    with nc.Block() as block:
        @block.sync
        def _(sp):
            sp.dma_start(mem_x[:, :, :], io["memory"].rearrange("(n p) c -> p n c", p=P)).then_inc(loaded["x"], DMA)
            sp.dma_start(gb_mem[:, 0:1], io["g_mem"].rearrange("(p a) -> p a", a=1)).then_inc(loaded["gb"], DMA)
            sp.dma_start(gb_mem[:, 1:2], io["b_mem"].rearrange("(p a) -> p a", a=1)).then_inc(loaded["gb"], DMA)
            sp.dma_start(beta[:, :], io["log_beta"].partition_broadcast(P)).then_inc(loaded["beta"], DMA)
            sp.dma_start(wk[:, :], io["Wk"]).then_inc(loaded["wk"], DMA)
            sp.dma_start(wv[:, :], io["Wv"]).then_inc(loaded["wv"], DMA)
            sp.dma_start(wq[:, :, :], io["Wq"].rearrange("(h d) c -> d h c", d=RD)).then_inc(loaded["wq"], DMA)
            sp.dma_start(wo[:, :, :], io["Wo"].rearrange("(h d) c -> d h c", d=RD)).then_inc(loaded["wo"], DMA)
            sp.dma_start(W["g_state"][:, :], io["g_state"]).then_inc(state_loaded, DMA)
            sp.dma_start(W["b_state"][:, :], io["b_state"]).then_inc(state_loaded, DMA)
            sp.wait_ge(state_loaded, 2 * DMA)

        @block.gpsimd
        def _(pool):
            pool.memset(power[:, :], -0.5).then_inc(power_set, 1)
            pool.memset(eps[:, :], LN_EPS).then_inc(power_set, 1)
            pool.wait_ge(power_set, 2)
            pool.wait_ge(aggr_done, MC)
            pool.tensor_tensor(rstd[:, :], mean_var[:, :, 1], eps[:, :], ALU.add).then_inc(rstd_step, 1)
            pool.wait_ge(rstd_step, 1)
            pool.tensor_tensor(rstd[:, :], rstd[:, :], power[:, :], ALU.pow).then_inc(rstd_step, 1)

        @block.scalar
        def _(act):
            act.wait_ge(loaded["beta"], DMA)
            act.activation(beta[:, :], beta[:, :], ACT.Exp).then_inc(beta_step, 1)
            act.wait_ge(turned, 1)
            act.wait_ge(loaded["gb"], 2 * DMA)
            act.activation(mem_T[:, :], ps[:, 0, 0:MEM], ACT.Identity, scale=gb_mem[:, 0:1], bias=gb_mem[:, 1:2])\
               .then_inc(mem_T_ready, 1)
            for n in range(RH // 4):
                act.wait_ge(kv_ready, RH // 4 + n + 1)
                act.activation(V[:, 4 * n:4 * n + 4, :].rearrange("p a b -> p (a b)"),
                               ps[:, 4 + 2 * n:6 + 2 * n, :].rearrange("p a b -> p (a b)"), ACT.Copy).then_inc(V_copied, 1)
            for n, (a, pair) in enumerate(groups):
                if n % 2 == 0:
                    act.wait_ge(product_ready, n + 1)
                    bank = 2 * (n % 4)
                    act.activation(W["GMU"][a][:, 2 * pair * MC:(2 * pair + 2) * MC, :].rearrange("p a b -> p (a b)"),
                                   ps[:, bank:bank + 2, :].rearrange("p a b -> p (a b)"), ACT.Copy)\
                       .then_inc(product_copied[0], 1)
            act.wait_ge(product_copied[0], len(groups) // 2)

        @block.vector
        def _(dve):
            dve.wait_ge(loaded["x"], DMA)
            for n in range(MC):
                dve.bn_stats(stats[:, n, :], mem_x[:, n, :]).then_inc(stats_done, 1)
            for n in range(MC):
                dve.wait_ge(stats_done, n + 1)
                dve.bn_aggr(mean_var[:, n, :], stats[:, n, :]).then_inc(aggr_done, 1)
            dve.wait_ge(rstd_step, 2)
            for n in range(MC):
                dve.tensor_scalar(mem_n[:, n, :], mem_x[:, n, :], mean_var[:, n, 0:1], rstd[:, n:n + 1],
                                  ALU.subtract, ALU.mult).then_inc(normed, 1)
            dve.wait_ge(beta_step, 1)
            dve.tensor_scalar(beta[:, :], beta[:, :], 0.5, None, ALU.mult).then_inc(beta_step, 1)
            dve.wait_ge(beta_step, 2)
            for h in range(RH):
                dve.wait_ge(kv_ready, h // 4 + 1)
                dve.tensor_scalar(K[:, h, :], ps[:, h // 2, h % 2 * MEM:(h % 2 + 1) * MEM], beta[:, h:h + 1], None,
                                  ALU.mult).then_inc(K_copied, 1)
            for n, (a, pair) in enumerate(groups):
                if n % 2 == 1:
                    dve.wait_ge(product_ready, n + 1)
                    bank = 2 * (n % 4)
                    dve.tensor_copy(W["GMU"][a][:, 2 * pair * MC:(2 * pair + 2) * MC, :].rearrange("p a b -> p (a b)"),
                                    ps[:, bank:bank + 2, :].rearrange("p a b -> p (a b)")).then_inc(product_copied[1], 1)
            dve.wait_ge(product_copied[1], len(groups) // 2)

        @block.tensor
        def _(pe):
            pe.wait_ge(normed, MC)
            for n in range(MC):
                last = pe.transpose(ps[:, 0, n * P:(n + 1) * P], mem_n[:, n, :], ident[:, :])
            last.then_inc(turned, 1)
            pe.wait_ge(mem_T_ready, 1)
            for name, w, bank in (("wk", wk, 0), ("wv", wv, 4)):
                pe.wait_ge(loaded[name], DMA)
                for h in range(RH):
                    last = pe.matmul(ps[:, bank + h // 2, h % 2 * MEM:(h % 2 + 1) * MEM], w[:, h * RD:(h + 1) * RD],
                                     mem_T[:, :], start=True, stop=True)
                    if h % 4 == 3:
                        last.then_inc(kv_ready, 1)
            pe.wait_ge(K_copied, RH)
            pe.wait_ge(V_copied, RH // 4)
            pe.wait_ge(loaded["wq"], DMA)
            pe.wait_ge(loaded["wo"], DMA)
            for n, (a, pair) in enumerate(groups):
                if n >= 4:
                    pe.wait_ge(product_copied[n % 2], (n - 4) // 2 + 1)
                left, right = ((wq, K), (V, K), (V, wo))[a]
                for k in range(2 * MC):
                    h, block_ = 2 * pair + k // MC, k % MC
                    last = pe.matmul(ps[:, 2 * (n % 4) + k // 2, k % 2 * MEM:(k % 2 + 1) * MEM],
                                     left[:, h, block_ * P:(block_ + 1) * P], right[:, h, :], start=True, stop=True)
                last.then_inc(product_ready, 1)


def retrieval(nc, mem, X, W, ident, ps):
    R, APART, STEP_LEN = 4, 2, EVALS + 3
    TICKS = STEPS * STEP_LEN
    FIRST = 3
    LEN = FIRST + TICKS + 1
    TURNS = NT // R
    assert R * APART == STEP_LEN and LEN + (R - 1) * APART < 2 * TICKS
    G, M, U = W["GMU"]
    norm_x = [mem.take(f"rt_norm_x{r}", [P, C]) for r in range(R)]
    hid_T = [mem.take(f"rt_hid_T{r}", [P, KC, P]) for r in range(R)]
    S = [mem.take(f"rt_scores{r}", [P, RH, MEM]) for r in range(R)]
    over = [mem.take(f"rt_over{r}", [P, RH, MEM]) for r in range(R)]
    weights_T = [mem.take(f"rt_weights_T{r}", [P, RH * MC, P]) for r in range(R)]
    stats = [mem.take(f"rt_stats{r}", [P, RH, 2, 3]) for r in range(R)]
    small = [[mem.take(f"rt_small{r}{n}", [P, RH, 2]) for n in range(3)] for r in range(R)]
    vec = {(n, r): mem.take(f"rt_{n}{r}", [P, RH]) for r in range(R)
           for n in ("top", "nt", "s2", "root", "s1", "rs1", "step", "move")}
    x_stats = [[mem.take(f"rt_x_stats{r}{n}", [P, 6]) for n in range(2)] for r in range(R)]
    mean_var = [mem.take(f"rt_mean_var{r}", [P, 2]) for r in range(R)]
    rv = [[mem.take(f"rt_rv{r}{n}", [P, 1]) for n in range(7)] for r in range(R)]
    power, eps = mem.take("rt_power", [P, 1]), mem.take("rt_eps", [P, 1])
    per_half = mem.take("rt_per_half", [P, RH, 2])
    assert mem.at <= nc.sbuf_usable_end, mem.at
    sem = nc.alloc_semaphore
    each = lambda name: [sem(f"rt_{name}{r}") for r in range(R)]
    consts_set = sem("rt_consts_set")
    x_stats_done, aggr_done, rstd_step, normed = each("x_stats_done"), each("aggr_done"), each("rstd_step"), each("normed")
    hid_full, hid_taken, turn_full, turn_taken = each("hid_full"), each("hid_taken"), each("turn_full"), each("turn_taken")
    scores_full, scores_taken = each("scores_full"), each("scores_taken")
    top_done, start_ready, nt_ready = each("top_done"), each("start_ready"), each("nt_ready")
    act_relu, dve_relu = each("act_relu"), each("dve_relu")
    stats_ready, s1_ready, rs1_ready = each("stats_ready"), each("s1_ready"), each("rs1_ready")
    s2_ready, root_ready, chain = each("s2_ready"), each("root_ready"), each("chain")
    out_full, out_added = each("out_full"), each("out_added")
    DVE_HEADS = RH - ACT_HEADS
    RELUS = EVALS + 1
    TG = RH * MC // 4
    TU, SU = STEPS * TG, 2 * STEPS
    LINKS = 5
    NORM_LINKS = 7
    HID = -1

    def phases(t):
        return [(r, back, t - APART * r + TICKS * back) for r in range(R) for back in range(2)
                if 0 <= t - APART * r + TICKS * back <= LEN]

    def in_step(phase):
        return (phase - FIRST) // STEP_LEN, (phase - FIRST) % STEP_LEN

    def at_place(t, place):
        return [(r, back, in_step(ph)[0]) for r, back, ph in phases(t)
                if FIRST <= ph < FIRST + TICKS and in_step(ph)[1] == place]

    def at_phase(t, phase):
        return [(r, back) for r, back, ph in phases(t) if ph == phase]

    def newtons(t):
        return [(r, back, s, k) for k in range(EVALS) for r, back, s in at_place(t, 2 + k)]

    turn_uses = [use for t in range(TICKS)
                 for use in [(r, back, HID) for r, back in at_phase(t, 1)] +
                 [(r, back, s * TG + n) for r, back, s in at_place(t, STEP_LEN - 1) for n in range(TG)]]
    score_uses = [(r, back, 2 * s + half) for t in range(TICKS) for r, back, s in at_place(t, 0) for half in range(2)]
    assert len(turn_uses) % 2 == 0 and len(score_uses) % 2 == 0

    def number_of(uses, r, use):
        return next(n for n, (r_, _, use_) in enumerate(uses) if (r_, use_) == (r, use))

    def place_of(uses, r, use):
        return number_of(uses, r, use) % 2

    def await_place(engine, uses, taken, count, r, use, turn, edge):
        n = number_of(uses, r, use)
        back = uses[n][1]
        for before in range(n - 2, n - 2 - len(uses), -2):
            r_, back_, use_ = uses[before]
            if before < 0 and edge == "first":
                return
            if before >= 0 and (edge, back_) in (("first", 1), ("last", 0)):
                continue
            turn_ = turn + back - back_ - (before < 0)
            if use_ == HID:
                engine.wait_ge(hid_taken[r_], turn_ + 1)
            else:
                engine.wait_ge(taken[r_], turn_ * count + use_ + 1)
            return

    def run(engine, tick):
        def turn(i, edge):
            for t in range(TICKS):
                tick(t, lambda back: None if (edge, back) in (("first", 1), ("last", 0)) else i - back, edge)
        turn(0, "first")
        with engine.Fori(1, TURNS) as i:
            turn(i, "middle")
        turn(TURNS, "last")

    with nc.Block() as block:
        @block.gpsimd
        def _(pool):
            pool.memset(power[:, :], -0.5).then_inc(consts_set, 1)
            pool.memset(eps[:, :], LN_EPS).then_inc(consts_set, 1)
            pool.memset(per_half[:, :, :], 2.0 / MEM).then_inc(consts_set, 1)
            pool.wait_ge(consts_set, 3)

            def tick(t, turn_of, edge):
                for r, back in at_phase(t, 0):
                    turn = turn_of(back)
                    if turn is None:
                        continue
                    var, v = mean_var[r][:, 1:2], [x[:, :] for x in rv[r]]
                    links = ((v[0], var, eps[:, :], ALU.add), (v[1], v[0], power[:, :], ALU.pow),
                             (v[2], v[1], v[1], ALU.mult), (v[3], v[2], var, ALU.mult),
                             (v[4], v[3], eps[:, :], ALU.add), (v[5], v[4], power[:, :], ALU.pow),
                             (v[6], v[1], v[5], ALU.mult))
                    pool.wait_ge(aggr_done[r], turn + 1)
                    for n, (out, a, b, op) in enumerate(links):
                        if n:
                            pool.wait_ge(rstd_step[r], turn * NORM_LINKS + n)
                        pool.tensor_tensor(out, a, b, op).then_inc(rstd_step[r], 1)
                for r, back, s, k in newtons(t):
                    turn = turn_of(back)
                    if turn is None:
                        continue
                    e = turn * (STEPS * EVALS) + s * EVALS + k
                    mean, m2 = stats[r][:, :, :, 1], stats[r][:, :, :, 2]
                    sq, m2_per, q = small[r]
                    s2, root, s1, rs1, step, move, nt = (vec[n, r] for n in ("s2", "root", "s1", "rs1", "step", "move", "nt"))
                    pool.wait_ge(stats_ready[r], e * RH + RH)
                    pool.tensor_tensor(s1[:, :], stats[r][:, :, 0, 1], stats[r][:, :, 1, 1], ALU.add).then_inc(s1_ready[r], 1)
                    pool.tensor_tensor(sq[:, :, :], mean, mean, ALU.mult).then_inc(chain[r], 1)
                    pool.tensor_tensor(m2_per[:, :, :], m2, per_half[:, :, :], ALU.mult).then_inc(chain[r], 1)
                    pool.wait_ge(chain[r], e * LINKS + 2)
                    pool.tensor_tensor(q[:, :, :], sq[:, :, :], m2_per[:, :, :], ALU.add).then_inc(chain[r], 1)
                    pool.wait_ge(chain[r], e * LINKS + 3)
                    pool.tensor_tensor(s2[:, :], q[:, :, 0], q[:, :, 1], ALU.add).then_inc(s2_ready[r], 1)
                    pool.wait_ge(root_ready[r], e + 1)
                    pool.tensor_tensor(step[:, :], s2[:, :], root[:, :], ALU.subtract).then_inc(chain[r], 1)
                    pool.wait_ge(rs1_ready[r], e + 1)
                    pool.wait_ge(chain[r], e * LINKS + 4)
                    pool.tensor_tensor(move[:, :], step[:, :], rs1[:, :], ALU.mult).then_inc(chain[r], 1)
                    pool.wait_ge(chain[r], e * LINKS + 5)
                    pool.tensor_tensor(nt[:, :], nt[:, :], move[:, :], ALU.subtract).then_inc(nt_ready[r], 1)

            run(pool, tick)

        def await_threshold(engine, r, turn, s, k):
            if k == 0:
                engine.wait_ge(start_ready[r], turn * STEPS + s + 1)
            else:
                engine.wait_ge(nt_ready[r], turn * (STEPS * EVALS) + s * EVALS + k)

        @block.scalar
        def _(act):
            def relus(r, turn, s, k):
                await_threshold(act, r, turn, s, k)
                for h in range(ACT_HEADS):
                    act.activation(over[r][:, h, :], S[r][:, h, :], ACT.Relu, bias=vec["nt", r][:, h:h + 1])\
                       .then_inc(act_relu[r], 1)

            def root(r, turn, s, k):
                act.wait_ge(s2_ready[r], turn * (STEPS * EVALS) + s * EVALS + k + 1)
                act.activation(vec["root", r][:, :], vec["s2", r][:, :], ACT.Sqrt, scale=2.0 / MEM)\
                   .then_inc(root_ready[r], 1)

            def squares(r, turn, s):
                for n in range(TG):
                    use = s * TG + n
                    act.wait_ge(turn_full[r], turn * TU + use + 1)
                    act.activation(weights_T[r][:, 4 * n:4 * n + 4, :].rearrange("p a b -> p (a b)"),
                                   ps[:, 4 + place_of(turn_uses, r, use), :], ACT.Square).then_inc(turn_taken[r], 1)

            def take_scores(r, turn, s):
                for half in range(2):
                    act.wait_ge(scores_full[r], turn * SU + 2 * s + half + 1)
                    bank = 2 * place_of(score_uses, r, 2 * s + half)
                    act.activation(S[r][:, 4 * half:4 * half + 4, :].rearrange("p a b -> p (a b)"),
                                   ps[:, bank:bank + 2, :].rearrange("p a b -> p (a b)"), ACT.Copy)\
                       .then_inc(scores_taken[r], 1)

            def take_hidden(r, turn):
                act.wait_ge(hid_full[r], turn + 1)
                bank = 4 + place_of(turn_uses, r, HID)
                for kc in range(KC):
                    ins = act.activation(hid_T[r][:, kc, :], ps[:, bank, kc * P:(kc + 1) * P], ACT.Identity,
                                         scale=W["g_state"][:, kc:kc + 1], bias=W["b_state"][:, kc:kc + 1])
                ins.then_inc(hid_taken[r], 1)

            def between(t, turn_of):
                for r, back, s in at_place(t, 0):
                    if s and turn_of(back) is not None:
                        squares(r, turn_of(back), s - 1)
                for r, back in at_phase(t, LEN - 1):
                    if turn_of(back) is not None:
                        squares(r, turn_of(back), STEPS - 1)
                for r, back in at_phase(t, 2):
                    if turn_of(back) is not None:
                        take_hidden(r, turn_of(back))
                for r, back, s in at_place(t, 1):
                    if turn_of(back) is not None:
                        take_scores(r, turn_of(back), s)

            def tick(t, turn_of, edge):
                late = [(r, back + (t == 0), s, k) for r, back, s, k in newtons((t - 1) % TICKS)[-1:]]
                for n, (r, back, s, k) in enumerate(newtons(t)):
                    if turn_of(back) is not None:
                        relus(r, turn_of(back), s, k)
                    for r_, back_, s_, k_ in late:
                        if t == 0 and back_ > 1:
                            continue
                        if turn_of(back_) is not None:
                            root(r_, turn_of(back_), s_, k_)
                    late = [(r, back, s, k)]
                    if n == 0:
                        between(t, turn_of)
                for r, back, s in at_place(t, STEP_LEN - 1):
                    if turn_of(back) is not None:
                        relus(r, turn_of(back), s, EVALS)

            run(act, tick)

        @block.vector
        def _(dve):
            def x_of(r, turn):
                return X[:, bass.ds(turn * (R * C) + r * C, C)]

            def own_relus(r, turn, s, k):
                await_threshold(dve, r, turn, s, k)
                for h in range(ACT_HEADS, RH):
                    dve.tensor_scalar(over[r][:, h, :], S[r][:, h, :], vec["nt", r][:, h:h + 1], 0.0,
                                      ALU.add, ALU.max).then_inc(dve_relu[r], 1)

            def start(r, turn, s):
                for half in range(2):
                    dve.wait_ge(scores_taken[r], turn * SU + 2 * s + half + 1)
                    dve.reduce_max(vec["top", r][:, 4 * half:4 * half + 4], S[r][:, 4 * half:4 * half + 4, :], AX.X)\
                       .then_inc(top_done[r], 1)
                dve.wait_ge(top_done[r], turn * SU + 2 * s + 2)
                dve.tensor_scalar(vec["nt", r][:, :], vec["top", r][:, :], -1.0, 1.0, ALU.mult, ALU.add)\
                   .then_inc(start_ready[r], 1)

            def moments(r, turn, s, k):
                relu = turn * (STEPS * RELUS) + s * RELUS + k
                for h in range(RH):
                    if h < ACT_HEADS:
                        dve.wait_ge(act_relu[r], relu * ACT_HEADS + h + 1)
                    else:
                        dve.wait_ge(dve_relu[r], relu * DVE_HEADS + h - ACT_HEADS + 1)
                    dve.bn_stats(stats[r][:, h, :, :].rearrange("p a b -> p (a b)"), over[r][:, h, :])\
                       .then_inc(stats_ready[r], 1)

            def reciprocal(r, turn, s, k):
                dve.wait_ge(s1_ready[r], turn * (STEPS * EVALS) + s * EVALS + k + 1)
                dve.reciprocal(vec["rs1", r][:, :], vec["s1", r][:, :]).then_inc(rs1_ready[r], 1)

            def tick(t, turn_of, edge):
                for r, back in at_phase(t, 0):
                    turn = turn_of(back)
                    if turn is not None:
                        dve.bn_stats(x_stats[r][0][:, :], x_of(r, turn)).then_inc(x_stats_done[r], 1)
                        stats_are_in(dve, x_stats[r][1][:, :], x_stats[r][0][:, :], x_stats_done[r], turn + 1)
                        dve.bn_aggr(mean_var[r][:, :], x_stats[r][0][:, :]).then_inc(aggr_done[r], 1)
                for r, back in at_phase(t, 1):
                    turn = turn_of(back)
                    if turn is not None:
                        dve.wait_ge(rstd_step[r], turn * NORM_LINKS + NORM_LINKS)
                        dve.tensor_scalar(norm_x[r][:, :], x_of(r, turn), mean_var[r][:, 0:1], rv[r][6][:, :],
                                          ALU.subtract, ALU.mult).then_inc(normed[r], 1)
                late = None
                for n, (r, back, s, k) in enumerate(newtons(t)):
                    if turn_of(back) is not None:
                        own_relus(r, turn_of(back), s, k)
                    if late:
                        reciprocal(*late)
                        late = None
                    if turn_of(back) is not None:
                        moments(r, turn_of(back), s, k)
                        late = r, turn_of(back), s, k
                    if n == 0:
                        for r, back, s in at_place(t, 1):
                            if turn_of(back) is not None:
                                start(r, turn_of(back), s)
                for r, back, s in at_place(t, STEP_LEN - 1):
                    if turn_of(back) is not None:
                        own_relus(r, turn_of(back), s, EVALS)
                if late:
                    reciprocal(*late)
                for r, back in at_phase(t, LEN):
                    turn = turn_of(back)
                    if turn is not None:
                        dve.wait_ge(out_full[r], turn + 1)
                        dve.tensor_tensor(x_of(r, turn), x_of(r, turn), ps[:, 6, 0:C], ALU.add).then_inc(out_added[r], 1)

            run(dve, tick)
            for r in range(R):
                dve.wait_ge(out_added[r], TURNS)

        @block.tensor
        def _(pe):
            def scores(r, turn, s, edge):
                if s == 0:
                    pe.wait_ge(hid_taken[r], turn + 1)
                left, right = (weights_T[r], M) if s else (hid_T[r], G)
                for half in range(2):
                    use = 2 * s + half
                    await_place(pe, score_uses, scores_taken, SU, r, use, turn, edge)
                    slot = place_of(score_uses, r, use)
                    for h in range(4 * half, 4 * half + 4):
                        if s and h % 2 == 0:
                            pe.wait_ge(turn_taken[r], turn * TU + (s - 1) * TG + h // 2 + 1)
                        for b in range(MC):
                            last = pe.matmul(ps[:, 2 * slot + h % 4 // 2, h % 2 * MEM:(h % 2 + 1) * MEM],
                                             left[:, h * MC + b if s else b, :], right[:, h * MC + b, :],
                                             start=b == 0, stop=b == MC - 1)
                    last.then_inc(scores_full[r], 1)

            def turn_weights(r, turn, s, edge):
                relu = turn * (STEPS * RELUS) + s * RELUS + EVALS
                for n in range(TG):
                    use = s * TG + n
                    await_place(pe, turn_uses, turn_taken, TU, r, use, turn, edge)
                    bank = 4 + place_of(turn_uses, r, use)
                    for h in (2 * n, 2 * n + 1):
                        if h < ACT_HEADS:
                            pe.wait_ge(act_relu[r], relu * ACT_HEADS + h + 1)
                        else:
                            pe.wait_ge(dve_relu[r], relu * DVE_HEADS + h - ACT_HEADS + 1)
                        for b in range(MC):
                            last = pe.transpose(ps[:, bank, (h % 2 * MC + b) * P:(h % 2 * MC + b + 1) * P],
                                                over[r][:, h, b * P:(b + 1) * P], ident[:, :])
                    last.then_inc(turn_full[r], 1)

            def tick(t, turn_of, edge):
                for r, back, s in at_place(t, 0):
                    if turn_of(back) is not None:
                        scores(r, turn_of(back), s, edge)
                for r, back in at_phase(t, LEN - 1):
                    turn = turn_of(back)
                    if turn is not None:
                        for n in range(RH * MC):
                            if n % 4 == 0:
                                pe.wait_ge(turn_taken[r], turn * TU + (STEPS - 1) * TG + n // 4 + 1)
                            last = pe.matmul(ps[:, 6, 0:C], weights_T[r][:, n, :], U[:, n, :],
                                             start=n == 0, stop=n == RH * MC - 1)
                        last.then_inc(out_full[r], 1)
                for r, back in at_phase(t, 1):
                    turn = turn_of(back)
                    if turn is not None:
                        pe.wait_ge(normed[r], turn + 1)
                        await_place(pe, turn_uses, turn_taken, TU, r, HID, turn, edge)
                        bank = 4 + place_of(turn_uses, r, HID)
                        for kc in range(KC):
                            last = pe.transpose(ps[:, bank, kc * P:(kc + 1) * P], norm_x[r][:, kc * P:(kc + 1) * P], ident[:, :])
                        last.then_inc(hid_full[r], 1)
                for r, back, s in at_place(t, STEP_LEN - 1):
                    if turn_of(back) is not None:
                        turn_weights(r, turn_of(back), s, edge)
                for r, back in at_phase(t, LEN):
                    if turn_of(back) is not None:
                        pe.wait_ge(out_added[r], turn_of(back) + 1)

            run(pe, tick)


def lut_weights(nc, io, mem, W):
    names = ("gate", "up", "down")
    cols = {"gate": KC * HID1, "up": KC * HID1, "down": F1 * C}
    out = {"gate": W["w_gate1"], "up": W["w_up1"], "down": W["w_down1"]}
    NC = max(cols.values())
    idx = [mem.take(f"idx_{n}", [P, NC], I32) for n in names]
    low = mem.take("lut_low", [P, NC])
    bit = [mem.take(f"lut_bit{k}", [P, NC], I32) for k in range(4)]
    leaf = [mem.take(f"lut_leaf{k}", [P, NC]) for k in range(LUT // 2)]
    lut = mem.take("lut", [P, LUT])
    delta = mem.take("lut_delta", [P, LUT // 2])
    assert mem.at <= nc.sbuf_usable_end, mem.at
    sem = nc.alloc_semaphore
    idx_zeroed, lut_loaded = sem("idx_zeroed"), sem("lut_loaded")
    idx_loaded = {n: sem(f"idx_{n}_loaded") for n in names}
    step, placed = sem("lut_step"), sem("lut_placed")
    full = HID1 // P * P

    with nc.Block() as block:
        @block.sync
        def _(sp):
            sp.dma_start(lut[:, :], io["lut"].partition_broadcast(P)).then_inc(lut_loaded, DMA)
            for n in range(2):
                sp.dma_start(idx[n][:, 0:cols[names[n]]].rearrange("p (k n) -> p k n", k=KC),
                             io[f"{names[n]}_idx"].rearrange("(k p) n -> p k n", p=P)).then_inc(idx_loaded[names[n]], DMA)
            down = idx[2][:, :].rearrange("p (k n) -> p k n", n=C)
            sp.wait_ge(idx_zeroed, 1)
            sp.dma_start(down[:, 0:F1 - 1, :], io["down_idx"][0:full, :].rearrange("(k p) n -> p k n", p=P))\
              .then_inc(idx_loaded["down"], DMA)
            sp.dma_start(down[0:HID1 - full, F1 - 1, :], io["down_idx"][full:HID1, :]).then_inc(idx_loaded["down"], DMA)

        @block.gpsimd
        def _(pool):
            pool.memset(idx[2][:, (F1 - 1) * C:F1 * C], 0).then_inc(idx_zeroed, 1)
            for a in ("w_gate1", "w_up1"):
                pool.memset(W[a][:, :, HID1:F1 * P], 0.0).then_inc(placed, 1)
            pool.wait_ge(placed, 2)

        @block.vector
        def _(dve):
            count = [0]

            def link(ins):
                count[0] += 1
                ins.then_inc(step, 1)
                dve.wait_ge(step, count[0])

            dve.wait_ge(lut_loaded, DMA)
            pairs = lut[:, :].rearrange("p (k e) -> p k e", e=2)
            link(dve.tensor_tensor(delta[:, :], pairs[:, :, 1], pairs[:, :, 0], ALU.subtract))
            for a, name in enumerate(names):
                n = cols[name]
                dve.wait_ge(idx_loaded[name], DMA * (2 if name == "down" else 1))
                for k in range(4):
                    link(dve.tensor_scalar(bit[k][:, 0:n], idx[a][:, 0:n], 1 << k, None, ALU.bitwise_and))
                link(dve.tensor_copy(low[:, 0:n], bit[0][:, 0:n]))
                for k in range(LUT // 2):
                    link(dve.tensor_scalar(leaf[k][:, 0:n], low[:, 0:n], delta[:, k:k + 1], pairs[:, k, 0:1], ALU.mult, ALU.add))
                for k in range(1, 4):
                    stride = 1 << (k - 1)
                    for left in range(0, LUT // 2, 2 * stride):
                        link(dve.copy_predicated(leaf[left][:, 0:n], bit[k][:, 0:n], leaf[left + stride][:, 0:n]))
                if name == "down":
                    link(dve.tensor_copy(out[name][:, :, :].rearrange("p k n -> p (k n)"), leaf[0][:, 0:n]))
                else:
                    link(dve.tensor_copy(out[name][:, :, 0:HID1], leaf[0][:, 0:n].rearrange("p (k n) -> p k n", k=KC)))


def ffn(nc, mem, X, w_gate, w_up, w_down, hidden_blocks, ident, ps, name):
    TURNS = NT // TPF
    norm_x = mem.take(f"{name}_norm_x", [P, TPF * C])
    norm_T = mem.take(f"{name}_norm_T", [P, KC, FC])
    gate = mem.take(f"{name}_gate", [P, 2, FC])
    hidden = mem.take(f"{name}_hidden", [P, 2, FC])
    stats = mem.take(f"{name}_stats", [P, TPF + 1, 6])
    mean_var = mem.take(f"{name}_mean_var", [P, TPF, 2])
    rstd = mem.take(f"{name}_rstd", [P, TPF])
    power, eps = mem.take(f"{name}_power", [P, TPF]), mem.take(f"{name}_eps", [P, TPF])
    assert mem.at <= nc.sbuf_usable_end, mem.at
    sem = lambda n: nc.alloc_semaphore(f"{name}_{n}")
    power_set, stats_done, aggr_done, rstd_step, normed = (sem(n) for n in ("power_set", "stats_done", "aggr_done", "rstd_step", "normed"))
    turned, norm_T_ready = sem("turned"), sem("norm_T_ready")
    gate_full, up_full, gate_ready, hidden_ready, down_done, added = \
        (sem(n) for n in ("gate_full", "up_full", "gate_ready", "hidden_ready", "down_done", "added"))
    F = hidden_blocks

    with nc.Block() as block:
        @block.gpsimd
        def _(pool):
            pool.memset(power[:, :], -0.5).then_inc(power_set, 1)
            pool.memset(eps[:, :], LN_EPS).then_inc(power_set, 1)
            pool.wait_ge(power_set, 2)
            with pool.Fori(0, TURNS) as i:
                pool.wait_ge(aggr_done, i * TPF + TPF)
                pool.tensor_tensor(rstd[:, :], mean_var[:, :, 1], eps[:, :], ALU.add).then_inc(rstd_step, 1)
                pool.wait_ge(rstd_step, i * 2 + 1)
                pool.tensor_tensor(rstd[:, :], rstd[:, :], power[:, :], ALU.pow).then_inc(rstd_step, 1)
                pool.wait_ge(normed, i * TPF + TPF)

        @block.scalar
        def _(act):
            with act.Fori(0, TURNS) as i:
                for kc in range(KC):
                    act.wait_ge(turned, i * KC + kc + 1)
                    act.activation(norm_T[:, kc, :], ps[:, kc, :], ACT.Copy).then_inc(norm_T_ready, 1)
                for f in range(F):
                    act.wait_ge(gate_full, i * F + f + 1)
                    if f >= 2:
                        act.wait_ge(hidden_ready, i * F + f - 1)
                    act.activation(gate[:, f % 2, :], ps[:, 2 * (f % 2), :], ACT.Silu).then_inc(gate_ready, 1)

        @block.vector
        def _(dve):
            with dve.Fori(0, TURNS) as i:
                tile = [X[:, bass.ds(i * (TPF * C) + t * C, C)] for t in range(TPF)]
                for t in range(TPF):
                    dve.bn_stats(stats[:, t, :], tile[t]).then_inc(stats_done, 1)
                stats_are_in(dve, stats[:, TPF, :], stats[:, 0, :], stats_done, i * TPF + TPF)
                for t in range(TPF):
                    dve.bn_aggr(mean_var[:, t, :], stats[:, t, :]).then_inc(aggr_done, 1)
                dve.wait_ge(rstd_step, i * 2 + 2)
                for t in range(TPF):
                    dve.tensor_scalar(norm_x[:, t * C:(t + 1) * C], tile[t], mean_var[:, t, 0:1], rstd[:, t:t + 1],
                                      ALU.subtract, ALU.mult).then_inc(normed, 1)
                for f in range(F):
                    dve.wait_ge(gate_ready, i * F + f + 1)
                    dve.wait_ge(up_full, i * F + f + 1)
                    if f >= 2:
                        dve.wait_ge(down_done, i * F + f - 1)
                    dve.tensor_tensor(hidden[:, f % 2, :], gate[:, f % 2, :], ps[:, 2 * (f % 2) + 1, :], ALU.mult)\
                       .then_inc(hidden_ready, 1)
                dve.wait_ge(down_done, i * F + F)
                both = X[:, bass.ds(i * (TPF * C), TPF * C)].rearrange("p (t c) -> p t c", c=C)
                dve.tensor_tensor(both, both, ps[:, 4:4 + TPF, 0:C], ALU.add).then_inc(added, 1)
            dve.wait_ge(added, TURNS)

        @block.tensor
        def _(pe):
            with pe.Fori(0, TURNS) as i:
                pe.wait_ge(normed, i * TPF + TPF)
                for kc in range(KC):
                    for t in range(TPF):
                        last = pe.transpose(ps[:, kc, t * P:(t + 1) * P], norm_x[:, t * C + kc * P:t * C + (kc + 1) * P],
                                            ident[:, :])
                    last.then_inc(turned, 1)
                pe.wait_ge(norm_T_ready, i * KC + KC)

                def gate_up(f):
                    if f >= 2:
                        pe.wait_ge(gate_ready, i * F + f - 1)
                    for w, bank, full in ((w_gate, 0, gate_full), (w_up, 1, up_full)):
                        if w is w_up and f >= 2:
                            pe.wait_ge(hidden_ready, i * F + f - 1)
                        for kc in range(KC):
                            last = pe.matmul(ps[:, 2 * (f % 2) + bank, :], w[:, kc, f * P:(f + 1) * P], norm_T[:, kc, :],
                                             start=kc == 0, stop=kc == KC - 1)
                        last.then_inc(full, 1)

                gate_up(0)
                for f in range(F):
                    if f + 1 < F:
                        gate_up(f + 1)
                    pe.wait_ge(hidden_ready, i * F + f + 1)
                    for t in range(TPF):
                        last = pe.matmul(ps[:, 4 + t, 0:C], hidden[:, f % 2, t * P:(t + 1) * P], w_down[:, f, :],
                                         start=f == 0, stop=f == F - 1)
                    last.then_inc(down_done, 1)
                pe.wait_ge(added, i + 1)


def give_back_semaphores(nc, free):
    nc.clear_and_free_semaphores([n for n in sorted(free) if n not in nc.free_semaphores])
    nc.all_engine_barrier()


def build(nc, io, out):
    nc.disable_value_cache = True
    mem = Memory(nc, 16512)
    X = mem.take("X", [P, NT * C])
    ident = mem.take("ident", [P, P])
    W = {"g_state": mem.take("g_state", [P, KC]), "b_state": mem.take("b_state", [P, KC])}
    ps = nc.alloc_psum_tensor("banks", [P, 8, BANK], F32)
    base = mem.at
    free = set(nc.free_semaphores)
    attention(nc, io, mem, X, ident, ps)
    give_back_semaphores(nc, free)

    mem.at = base
    W["GMU"] = [mem.take(f"w_{n}", [P, RH * MC, C]) for n in "GMU"]
    for n, shape in (("w_gate1", [P, KC, F1 * P]), ("w_up1", [P, KC, F1 * P]), ("w_down1", [P, F1, C])):
        W[n] = mem.take(n, shape)
    base = mem.at
    lut_weights(nc, io, mem, W)
    mem.at = base
    retrieval_weights(nc, io, mem, W, ident, ps)

    mem.at = base
    w0 = {n: mem.take(f"w_{n}0", shape) for n, shape in (("gate", [P, KC, HID0]), ("up", [P, KC, HID0]), ("down", [P, F0, C]))}
    w0_loaded = nc.alloc_semaphore("w0_loaded")
    with nc.Block() as block:
        @block.sync
        def _(sp):
            for n in ("gate", "up", "down"):
                sp.dma_start(w0[n][:, :, :], io[f"w_{n}"].rearrange("(k p) n -> p k n", p=P)).then_inc(w0_loaded, DMA)
            sp.wait_ge(w0_loaded, 3 * DMA)
    ffn(nc, mem, X, w0["gate"], w0["up"], w0["down"], F0, ident, ps, "ffn0")
    mem.at = base
    retrieval(nc, mem, X, W, ident, ps)
    mem.at = base
    ffn(nc, mem, X, W["w_gate1"], W["w_up1"], W["w_down1"], F1, ident, ps, "ffn1")

    stored = nc.alloc_semaphore("stored")
    with nc.Block() as block:
        @block.sync
        def _(sp):
            sp.dma_start(out.rearrange("(n p) c -> p n c", p=P), X[:, :].rearrange("p (n c) -> p n c", c=C))\
              .then_inc(stored, DMA)
            sp.wait_ge(stored, DMA)


def kernel(**inputs):
    import numpy as np
    import concourse.bacc as bacc
    from concourse.bass_utils import run_bass_kernel_spmd

    a0 = lambda n: np.asarray(inputs[f"L0_attn_{n}"])
    a1 = lambda n: np.asarray(inputs[f"L1_attn_{n}"])
    f0 = lambda n: np.asarray(inputs[f"L0_ffn_{n}"])
    f1 = lambda n: np.asarray(inputs[f"L1_ffn_{n}"])
    arrays = {"x": a0("x").reshape(B * T, C)}
    arrays.update({n: a0(n).T for n in ("wq", "wk", "wv", "wo")})
    arrays.update({n: a0(n) for n in ("lq1", "lk1", "lq2", "lk2")})
    arrays.update({n: f0(n).T for n in ("w_gate", "w_up", "w_down")})
    arrays.update({n: a1(n) for n in ("memory", "Wq", "log_beta", "g_mem", "b_mem")})
    arrays.update({n: a1(n).T for n in ("Wk", "Wv", "Wo")})
    arrays.update({n: a1(n).reshape(KC, P).T for n in ("g_state", "b_state")})
    arrays["lut"] = f1("lut")
    arrays.update({n: f1(n).T for n in ("gate_idx", "up_idx", "down_idx")})
    arrays = {n: np.ascontiguousarray(a) for n, a in arrays.items()}

    nc = bacc.Bacc("TRN2", target_bir_lowering=False, num_devices=1)
    io = {n: nc.dram_tensor(f"in_{n}", a.shape, mybir.dt.from_np(a.dtype), kind="ExternalInput").ap()
          for n, a in arrays.items()}
    out = nc.dram_tensor("out", (B * T, C), F32, kind="ExternalOutput").ap()
    build(nc, io, out)
    r = run_bass_kernel_spmd(nc, [{f"in_{n}": a for n, a in arrays.items()}], core_ids=[0])
    return r.results[0]["out"].reshape(B, T, C)
```

```python
from contextlib import ExitStack

import concourse.bass as bass
from concourse import mybir

F32 = mybir.dt.float32
F32R = mybir.dt.float32r
BF16 = mybir.dt.bfloat16
I32 = mybir.dt.int32
ALU = mybir.AluOpType
ACT = mybir.ActivationFunctionType
AX = mybir.AxisListType

P = 128
B, T, C = 2, 1024, 256
NT = B * T // P
TPB = T // P
KC = C // P
BANK = 512
LN_EPS = 1e-5

HEADS, HALF = 8, 16
HD = 2 * HALF
HPG = P // HD
GROUPS = HEADS // HPG
MAPS = 2 * HPG
HALVES = 2 * C // HALF
CHUNK = 512
CHUNKS = T // CHUNK
KPC = CHUNK // P
LAMBDA_INIT = 0.8
RMS_EPS = 1.1920929e-07
PIECES = [(0, 0), (0, 1), (1, 0), (1, 1), (0, 2), (2, 0)]
STACK = len(PIECES) * HALF
PARTS = 3
DMA = 16


class Memory:

    BYTES = {F32: 4, F32R: 4, BF16: 2, I32: 4}

    def __init__(self, nc, at):
        self.nc, self.at = nc, at

    def take(self, name, shape, dtype=F32):
        size = self.BYTES[dtype]
        for n in shape[1:]:
            size *= n
        t = self.nc.alloc_sbuf_tensor_at(name, shape, dtype, offset=self.at)
        self.at = -(-(self.at + size) // 32) * 32
        return t


def stats_are_in(dve, spare, stats, semaphore, value):
    dve.wait_ge(semaphore, value)
    dve.bn_stats(spare, stats)


def attention(nc, io, mem, X, ident, ps):
    norm_x = mem.take("norm_x", [P, TPB * C])
    norm_T = mem.take("norm_T", [P, KC, T])
    w_qk = mem.take("w_qk", [P, KC, 2 * C])
    w_v = mem.take("w_v", [P, KC, C])
    w_o = mem.take("w_o", [P, KC, C])
    parts = [[mem.take(f"parts_{n}{g}", [P, PARTS, T], BF16) for n in "qk"] for g in range(GROUPS)]
    stacks = [[mem.take(f"stack_{n}{g}", [STACK, MAPS, T], BF16) for n in "qk"] for g in range(GROUPS)]
    V = mem.take("V", [P, TPB * C])
    probs = mem.take("probs", [P, 3, HPG, CHUNK])
    yT = mem.take("yT", [P, GROUPS, T])
    square = mem.take("square", [P, 2, CHUNK])
    sumsq = mem.take("sumsq", [P, 2, HALVES])
    root = mem.take("root", [P, 2, HALVES])
    rroot = mem.take("rroot", [P, 2, HALVES])
    unit_qk = mem.take("unit_qk", [P, 2, 2 * C])
    rest = mem.take("rest", [P, 2, CHUNK])
    den = mem.take("den", [P, 2, CHUNK])
    y_sum = mem.take("y_sum", [P, 2, CHUNK])
    rden = mem.take("rden", [P, 2, CHUNK])
    y_half = mem.take("y_half", [P, 2, CHUNK])
    causal = mem.take("causal", [P, HPG, P])
    ones = mem.take("ones", [P, HD])
    stats = mem.take("stats", [P, TPB + 1, 6])
    mean_var = mem.take("mean_var", [P, TPB, 2])
    rstd = mem.take("rstd", [P, TPB])
    power, eps = mem.take("power", [P, TPB]), mem.take("eps", [P, TPB])
    rms_eps = mem.take("rms_eps", [P, 1])
    lvec = mem.take("lvec", [P, 4, HD])
    lprod = mem.take("lprod", [P, 2, HD])
    lsum = mem.take("lsum", [P, 2])
    lexp = mem.take("lexp", [P, 2])
    neg_lambda = mem.take("neg_lambda", [P, 1])
    assert mem.at <= nc.sbuf_usable_end, mem.at
    scratch = [[nc.dram_tensor(f"saved_{n}{g}", [P, PARTS, T], BF16, kind="Internal").ap() for n in "qk"]
               for g in range(GROUPS)]

    sem = nc.alloc_semaphore
    x_loaded = [sem(f"x_loaded{b}") for b in range(B)]
    w_loaded = {n: sem(f"{n}_loaded") for n in ("wq", "wk", "wv", "wo")}
    l_loaded = sem("l_loaded")
    consts_ready, const_step = sem("consts_ready"), sem("const_step")
    ident_step = sem("ident_step")
    lambda_step, lexp_ready = sem("lambda_step"), sem("lexp_ready")
    stats_done, rstd_step, rstd_ready, normed = sem("stats_done"), sem("rstd_step"), sem("rstd_ready"), sem("normed")
    aggr_done = sem("aggr_done")
    turned, norm_T_ready = sem("turned"), sem("norm_T_ready")
    proj_ready, square_ready, sumsq_ready, root_ready = sem("proj_ready"), sem("square_ready"), sem("sumsq_ready"), sem("root_ready")
    recip_done, unit_done, unit_turned = sem("recip_done"), sem("unit_done"), sem("unit_turned")
    first_done, rest_ready, second_ready, split_done = sem("first_done"), sem("rest_ready"), sem("second_ready"), sem("split_done")
    parts_saved = [sem(f"parts_saved{g}") for g in range(GROUPS)]
    stack_loaded = [[sem(f"stack_loaded{g}{c}") for c in range(CHUNKS)] for g in range(GROUPS)]
    v_ready, V_copied = sem("v_ready"), sem("V_copied")
    scores_ready, probs_ready, masked, pv_done = sem("scores_ready"), sem("probs_ready"), sem("masked"), sem("pv_done")
    y_taken, den_taken, rden_done, half_done, y_ready = sem("y_taken"), sem("den_taken"), sem("rden_done"), sem("half_done"), sem("y_ready")
    o_ready, o_added = sem("o_ready"), sem("o_added")

    plan = [(g, c, s, kt) for g in range(GROUPS) for c in range(CHUNKS) for s in range(2)
            for kt in range(KPC * (c + 1))]
    TILES = len(plan)
    BLOCKS = GROUPS * CHUNKS * 2
    PAIRS = 2 * GROUPS
    UNITS = CHUNKS * PAIRS
    TURNS = CHUNKS * KC
    SLOTS = 3
    OB = TPB // 2

    def first_query(c, kt):
        return max(0, kt - KPC * c) * P

    def is_diagonal(n):
        _, c, _, kt = plan[n]
        return kt >= KPC * c

    def is_last(n):
        _, c, _, kt = plan[n]
        return kt == KPC * (c + 1) - 1

    DIAGONALS = sum(is_diagonal(n) for n in range(TILES))

    def unit(u):
        return u // PAIRS, u // 2 % GROUPS, u % 2

    block = nc.Block()
    block.__enter__()

    @block.sync
    def _(sp):
        x_view = io["x"].rearrange("(n p) c -> p n c", p=P)
        for b in range(B):
            sp.dma_start(X[:, b * TPB * C:(b + 1) * TPB * C].rearrange("p (n c) -> p n c", c=C),
                         x_view[:, b * TPB:(b + 1) * TPB, :]).then_inc(x_loaded[b], DMA)
            if b == 0:
                for n, w in (("wq", w_qk[:, :, 0:C]), ("wk", w_qk[:, :, C:2 * C]), ("wv", w_v[:, :, :]), ("wo", w_o[:, :, :])):
                    sp.dma_start(w, io[n].rearrange("(k p) n -> p k n", p=P)).then_inc(w_loaded[n], DMA)
                for n, name in enumerate(("lq1", "lk1", "lq2", "lk2")):
                    sp.dma_start(lvec[:, n, :], io[name].partition_broadcast(P)).then_inc(l_loaded, DMA)
        for i in range(B):
            for c in range(CHUNKS):
                cols = slice(c * CHUNK, (c + 1) * CHUNK)
                for g in range(GROUPS):
                    for t in range(2):
                        sp.wait_ge(split_done, i * UNITS + c * PAIRS + 2 * g + t + 1)
                        sp.dma_start(scratch[g][t][:, :, cols], parts[g][t][:, :, cols]).then_inc(parts_saved[g], DMA)
                    sp.wait_ge(parts_saved[g], i * (2 * CHUNKS * DMA) + 2 * (c + 1) * DMA)
                    for t in range(2):
                        rows = scratch[g][t].rearrange("(m r) a n -> r m a n", r=HALF)
                        for n, piece in enumerate(PIECES):
                            sp.dma_start(stacks[g][t][n * HALF:(n + 1) * HALF, :, cols],
                                         rows[:, :, piece[t], cols]).then_inc(stack_loaded[g][c], DMA)
            for g in range(GROUPS):
                for c in range(CHUNKS):
                    sp.wait_ge(stack_loaded[g][c], (i + 1) * (2 * len(PIECES) * DMA))
            sp.wait_ge(scores_ready, (i + 1) * (2 * TILES))

    @block.gpsimd
    def _(pool):
        pool.memset(ident[:, :], 0.0).then_inc(ident_step, 1)
        pool.memset(causal[:, :, :], 1.0).then_inc(const_step, 1)
        pool.memset(ones[:, :], 1.0).then_inc(consts_ready, 1)
        pool.memset(rms_eps[:, :], RMS_EPS).then_inc(consts_ready, 1)
        pool.memset(power[:, :], -0.5).then_inc(consts_ready, 1)
        pool.memset(eps[:, :], LN_EPS).then_inc(consts_ready, 1)
        pool.wait_ge(ident_step, 1)
        pool.affine_select(out=ident[:, :], in_=ident[:, :], compare_op=ALU.not_equal, fill=1.0, base=0,
                           pattern=[[-1, P]], channel_multiplier=1).then_inc(consts_ready, 1)
        pool.wait_ge(const_step, 1)
        pool.affine_select(out=causal[:, :, :], in_=causal[:, :, :], compare_op=ALU.is_ge, fill=0.0, base=0,
                           pattern=[[0, HPG], [1, P]], channel_multiplier=-1).then_inc(consts_ready, 1)
        pool.wait_ge(consts_ready, 4)
        with pool.Fori(0, B) as i:
            pool.wait_ge(aggr_done, i * TPB + TPB)
            pool.tensor_tensor(rstd[:, :], mean_var[:, :, 1], eps[:, :], ALU.add).then_inc(rstd_step, 1)
            pool.wait_ge(rstd_step, i + 1)
            pool.tensor_tensor(rstd[:, :], rstd[:, :], power[:, :], ALU.pow).then_inc(rstd_ready, 1)
            for u in range(UNITS):
                c, g, t = unit(u)
                cols = slice(c * CHUNK, (c + 1) * CHUNK)
                pool.wait_ge(second_ready, i * UNITS + u + 1)
                pool.tensor_tensor(parts[g][t][:, 2, cols], rest[:, u % 2, :], parts[g][t][:, 1, cols],
                                   ALU.subtract).then_inc(split_done, 1)
            pool.wait_ge(normed, i * TPB + TPB)

    @block.scalar
    def _(act):
        act.wait_ge(lambda_step, 2)
        act.activation(lexp[:, :], lsum[:, :], ACT.Exp).then_inc(lexp_ready, 1)
        act.wait_ge(consts_ready, 6)
        with act.Fori(0, B) as i:
            for n in range(TURNS):
                c, kc = divmod(n, KC)
                act.wait_ge(turned, i * TURNS + n + 1)
                act.activation(norm_T[:, kc, c * CHUNK:(c + 1) * CHUNK], ps[:, n, :], ACT.Copy)\
                   .then_inc(norm_T_ready, 1)

            def squares(t):
                act.wait_ge(proj_ready, i * TPB + t + 1)
                if t >= 2:
                    act.wait_ge(sumsq_ready, i * TPB + t - 1)
                act.activation(square[:, t % 2, :], ps[:, 4 + t % 3, :], ACT.Square).then_inc(square_ready, 1)

            def part_of(u, n):
                c, g, t = unit(u)
                return parts[g][t][:, n, c * CHUNK:(c + 1) * CHUNK]

            def split(units):
                for u in units:
                    act.wait_ge(unit_turned, i * TPB + (unit(u)[0] + 1) * KPC)
                    act.activation(part_of(u, 0), ps[:, u % PAIRS, :], ACT.Copy).then_inc(first_done, 1)
                for u in units:
                    act.wait_ge(rest_ready, i * UNITS + u + 1)
                    act.activation(part_of(u, 1), rest[:, u % 2, :], ACT.Copy).then_inc(second_ready, 1)

            squares(0)
            for t in range(TPB):
                if t + 1 < TPB:
                    squares(t + 1)
                act.wait_ge(sumsq_ready, i * TPB + t + 1)
                if t >= 2:
                    act.wait_ge(recip_done, i * TPB + t - 1)
                act.activation(root[:, t % 2, :], sumsq[:, t % 2, :], ACT.Sqrt, bias=rms_eps[:, :], scale=1.0 / HALF)\
                   .then_inc(root_ready, 1)
                if t % 2:
                    act.wait_ge(v_ready, i * OB + t // 2 + 1)
                    act.activation(V[:, t // 2 * BANK:(t // 2 + 1) * BANK], ps[:, 7, :], ACT.Copy).then_inc(V_copied, 1)
                if KPC <= t < KPC + 2:
                    split((2 * (t - KPC), 2 * (t - KPC) + 1))
            split((PAIRS, PAIRS + 1))
            split((PAIRS + 2, PAIRS + 3))
            blocks = 0
            for n, (g, c, s, kt) in enumerate(plan):
                lo = first_query(c, kt)
                for pair in range(2):
                    act.wait_ge(scores_ready, i * 2 * TILES + 2 * n + pair + 1)
                    if pair == 0 and n >= SLOTS:
                        act.wait_ge(pv_done, i * TILES + n - SLOTS + 1)
                    bank = 2 * ((2 * n + pair) % SLOTS)
                    act.activation(probs[:, n % SLOTS, 2 * pair:2 * pair + 2, lo:], ps[:, bank:bank + 2, lo:],
                                   ACT.Exp, scale=HALF ** -0.5).then_inc(probs_ready, 1)
                for done in (n - 1, n):
                    if done >= 0 and is_last(done) and (done == n - 1 or n == TILES - 1):
                        act.wait_ge(pv_done, i * TILES + done + 1)
                        if blocks >= 2:
                            act.wait_ge(half_done, i * BLOCKS + blocks - 1)
                        act.activation(den[:, blocks % 2, :], ps[:, 7, :], ACT.Copy).then_inc(den_taken, 1)
                        blocks += 1
            act.wait_ge(pv_done, i * TILES + TILES)
            for g in range(GROUPS):
                act.wait_ge(parts_saved[g], (i + 1) * (2 * CHUNKS * DMA))
            act.wait_ge(half_done, i * BLOCKS + BLOCKS)

    @block.vector
    def _(dve):
        dve.wait_ge(l_loaded, 4 * DMA)
        for n in range(2):
            dve.tensor_tensor_reduce(out=lprod[:, n, :], in0=lvec[:, 2 * n, :], in1=lvec[:, 2 * n + 1, :], scale=1.0,
                                     scalar=0.0, op0=ALU.mult, op1=ALU.add,
                                     accum_out=lsum[:, n:n + 1]).then_inc(lambda_step, 1)
        dve.wait_ge(lexp_ready, 1)
        dve.tensor_tensor(neg_lambda[:, :], lexp[:, 1:2], lexp[:, 0:1], ALU.subtract).then_inc(lambda_step, 1)
        dve.wait_ge(lambda_step, 3)
        dve.tensor_scalar(neg_lambda[:, :], neg_lambda[:, :], -LAMBDA_INIT, None, ALU.add).then_inc(lambda_step, 1)
        dve.wait_ge(lambda_step, 4)
        dve.wait_ge(x_loaded[0], DMA)
        with dve.Fori(0, B) as i:
            for t in range(TPB):
                dve.bn_stats(stats[:, t, :], X[:, bass.ds(i * (TPB * C) + t * C, C)]).then_inc(stats_done, 1)
            stats_are_in(dve, stats[:, TPB, :], stats[:, 0, :], stats_done, i * TPB + TPB)
            for t in range(TPB):
                dve.bn_aggr(mean_var[:, t, :], stats[:, t, :]).then_inc(aggr_done, 1)
            dve.wait_ge(rstd_ready, i + 1)
            for t in range(TPB):
                dve.tensor_scalar(norm_x[:, t * C:(t + 1) * C], X[:, bass.ds(i * (TPB * C) + t * C, C)],
                                  mean_var[:, t, 0:1], rstd[:, t:t + 1], ALU.subtract, ALU.mult).then_inc(normed, 1)
            def sum_squares(t):
                dve.wait_ge(square_ready, i * TPB + t + 1)
                dve.reduce_sum(sumsq[:, t % 2, :], square[:, t % 2, :].rearrange("p (a r) -> p a r", r=HALF), AX.X)\
                   .then_inc(sumsq_ready, 1)

            def rests(units):
                for u in units:
                    c, g, t = unit(u)
                    dve.wait_ge(first_done, i * UNITS + u + 1)
                    if u >= 2:
                        dve.wait_ge(split_done, i * UNITS + u - 1)
                    dve.tensor_tensor(rest[:, u % 2, :], ps[:, u % PAIRS, :], parts[g][t][:, 0, c * CHUNK:(c + 1) * CHUNK],
                                      ALU.subtract).then_inc(rest_ready, 1)

            sum_squares(0)
            for t in range(TPB):
                if t + 1 < TPB:
                    sum_squares(t + 1)
                dve.wait_ge(root_ready, i * TPB + t + 1)
                dve.reciprocal(rroot[:, t % 2, :], root[:, t % 2, :]).then_inc(recip_done, 1)
                dve.wait_ge(recip_done, i * TPB + t + 1)
                if t >= 2:
                    dve.wait_ge(unit_turned, i * TPB + t - 1)
                halves = lambda a: a.rearrange("p (a r) -> p a r", r=HALF)
                dve.tensor_tensor(halves(unit_qk[:, t % 2, :]), halves(ps[:, 4 + t % 3, :]),
                                  rroot[:, t % 2, :].unsqueeze(2).to_broadcast([P, HALVES, HALF]), ALU.mult)\
                   .then_inc(unit_done, 1)
                if KPC <= t < KPC + 2:
                    rests((2 * (t - KPC), 2 * (t - KPC) + 1))
            rests(range(PAIRS, UNITS))

            def take_values(b):
                dve.tensor_copy(y_sum[:, b % 2, :], ps[:, 6, :]).then_inc(y_taken, 1)

            def invert(b, part):
                dve.wait_ge(den_taken, i * BLOCKS + b + 1)
                cols = slice(part * CHUNK // 2, (part + 1) * CHUNK // 2)
                dve.reciprocal(rden[:, b % 2, cols], den[:, b % 2, cols]).then_inc(rden_done, 1)

            def divide(b):
                dve.wait_ge(y_taken, i * BLOCKS + b + 1)
                dve.wait_ge(rden_done, i * (2 * BLOCKS) + 2 * b + 2)
                dve.tensor_tensor(y_half[:, b % 2, :], y_sum[:, b % 2, :], rden[:, b % 2, :], ALU.mult).then_inc(half_done, 1)

            def subtract_half(b):
                g, c = b // (2 * CHUNKS), b // 2 % CHUNKS
                dve.wait_ge(half_done, i * BLOCKS + b + 1)
                dve.scalar_tensor_tensor(yT[:, g, c * CHUNK:(c + 1) * CHUNK], y_half[:, 1, :],
                                         neg_lambda[:, :], y_half[:, 0, :], ALU.mult, ALU.add).then_inc(y_ready, 1)

            diagonals, blocks, since = 0, 0, None
            for n, (g, c, s, kt) in enumerate(plan):
                if is_diagonal(n):
                    lo = first_query(c, kt)
                    dve.wait_ge(probs_ready, i * 2 * TILES + 2 * n + 2)
                    seen = probs[:, n % SLOTS, :, lo:lo + P]
                    dve.tensor_tensor(seen, seen, causal[:, :, :], ALU.mult).then_inc(masked, 1)
                if blocks and since == 0:
                    invert(blocks - 1, 0)
                if blocks and since == 1:
                    invert(blocks - 1, 1)
                    divide(blocks - 1)
                if blocks and since == 2 and blocks % 2 == 0:
                    subtract_half(blocks - 1)
                if since is not None:
                    since += 1
                if is_last(n):
                    dve.wait_ge(pv_done, i * TILES + n + 1)
                    take_values(blocks)
                    blocks, since = blocks + 1, 0
            invert(BLOCKS - 1, 0)
            invert(BLOCKS - 1, 1)
            divide(BLOCKS - 1)
            subtract_half(BLOCKS - 1)
            for n in range(OB):
                dve.wait_ge(o_ready, i * OB + n + 1)
                tiles = X[:, bass.ds(i * (TPB * C) + n * BANK, BANK)]
                dve.scalar_tensor_tensor(tiles, ps[:, n, :], 1.0 - LAMBDA_INIT, tiles, ALU.mult, ALU.add)\
                   .then_inc(o_added, 1)
            dve.wait_ge(turned, i * TURNS + TURNS)
            dve.wait_ge(split_done, i * UNITS + UNITS)
            dve.wait_ge(unit_turned, i * TPB + TPB)
            dve.wait_ge(x_loaded[1], DMA)
        dve.wait_ge(o_added, B * OB)

    @block.tensor
    def _(pe):
        pe.wait_ge(consts_ready, 6)
        for n in ("wq", "wk", "wv", "wo"):
            pe.wait_ge(w_loaded[n], DMA)
        with pe.Fori(0, B) as i:
            for n in range(TURNS):
                c, kc = divmod(n, KC)
                pe.wait_ge(normed, i * TPB + (c + 1) * KPC)
                for t in range(KPC):
                    at = (c * KPC + t) * C + kc * P
                    last = pe.transpose(ps[:, n, t * P:(t + 1) * P], norm_x[:, at:at + P], ident[:, :])
                last.then_inc(turned, 1)

            def project(t):
                pe.wait_ge(norm_T_ready, i * TURNS + (t // KPC + 1) * KC)
                if t >= 3:
                    pe.wait_ge(unit_done, i * TPB + t - 2)
                for kc in range(KC):
                    last = pe.matmul(ps[:, 4 + t % 3, :], norm_T[:, kc, t * P:(t + 1) * P], w_qk[:, kc, :],
                                     start=kc == 0, stop=kc == KC - 1)
                last.then_inc(proj_ready, 1)

            def values(t):
                if t >= 2 and t % 2 == 0:
                    pe.wait_ge(V_copied, i * OB + t // 2)
                for kc in range(KC):
                    last = pe.matmul(ps[:, 7, t % 2 * C:(t % 2 + 1) * C], norm_T[:, kc, t * P:(t + 1) * P],
                                     w_v[:, kc, :], start=kc == 0, stop=kc == KC - 1)
                if t % 2:
                    last.then_inc(v_ready, 1)

            def turn_units(t):
                if t == 0:
                    pe.wait_ge(norm_T_ready, i * TURNS + TURNS)
                if t == KPC:
                    pe.wait_ge(rest_ready, i * UNITS + PAIRS)
                pe.wait_ge(unit_done, i * TPB + t + 1)
                for g in range(GROUPS):
                    for n in range(2):
                        at = n * C + g * P
                        last = pe.transpose(ps[:, 2 * g + n, t % KPC * P:(t % KPC + 1) * P], unit_qk[:, t % 2, at:at + P],
                                            ident[:, :])
                last.then_inc(unit_turned, 1)

            for t in range(2):
                project(t)
                values(t)
            for t in range(TPB):
                if t + 2 < TPB:
                    project(t + 2)
                    values(t + 2)
                turn_units(t)
            pe.wait_ge(V_copied, i * OB + OB)
            pe.wait_ge(rest_ready, i * UNITS + UNITS)

            def scores(n):
                g, c, s, kt = plan[n]
                lo = first_query(c, kt)
                if n == 0 or plan[n - 1][0:2] != (g, c):
                    pe.wait_ge(stack_loaded[g][c], (i + 1) * (2 * len(PIECES) * DMA))
                for pair in range(2):
                    o = 2 * n + pair
                    if o >= SLOTS:
                        pe.wait_ge(probs_ready, i * 2 * TILES + o - SLOTS + 1)
                    for j in range(2):
                        m = (2 * pair + j) * 2 + s
                        last = pe.matmul(ps[:, 2 * (o % SLOTS) + j, lo:], stacks[g][1][:, m, kt * P:(kt + 1) * P],
                                         stacks[g][0][:, m, c * CHUNK + lo:(c + 1) * CHUNK], start=True, stop=True)
                    last.then_inc(scores_ready, 1)

            diagonals = blocks = 0
            scores(0)
            for n, (g, c, s, kt) in enumerate(plan):
                lo = first_query(c, kt)
                if n + 1 < TILES:
                    scores(n + 1)
                if kt == 0 and blocks:
                    pe.wait_ge(y_taken, i * BLOCKS + blocks)
                    pe.wait_ge(den_taken, i * BLOCKS + blocks)
                pe.wait_ge(probs_ready, i * 2 * TILES + 2 * n + 2)
                if is_diagonal(n):
                    diagonals += 1
                    pe.wait_ge(masked, i * DIAGONALS + diagonals)
                for h in range(HPG):
                    at = kt * C + (g * HPG + h) * HD
                    pe.matmul(ps[h * HD:(h + 1) * HD, 6, lo:], V[:, at:at + HD], probs[:, n % SLOTS, h, lo:],
                              start=kt == 0, stop=is_last(n))
                for h in range(HPG):
                    last = pe.matmul(ps[h * HD:(h + 1) * HD, 7, lo:], ones[:, :], probs[:, n % SLOTS, h, lo:],
                                     start=kt == 0, stop=is_last(n))
                last.then_inc(pv_done, 1)
                blocks += is_last(n)
            for t in range(TPB):
                pe.wait_ge(y_ready, i * (BLOCKS // 2) + BLOCKS // 2 - CHUNKS + t // KPC + 1)
                for g in range(GROUPS):
                    last = pe.matmul(ps[:, t // 2, t % 2 * C:(t % 2 + 1) * C], yT[:, g, t * P:(t + 1) * P],
                                     w_o[:, g, :], start=g == 0, stop=g == GROUPS - 1)
                if t % 2:
                    last.then_inc(o_ready, 1)
            pe.wait_ge(o_added, i * OB + OB)

    block.__exit__(None, None, None)


MEM, MW, RH, RD = 256, 128, 8, 128
MC = MEM // P
STEPS = 3
EVALS = 5
ACT_HEADS = (5, 8, 6, 8, 7, 4)

HID0, HID1 = 1024, 688
F0, F1 = HID0 // P, -(-HID1 // P)
LUT = 16
FC = 512
TPF = FC // P
LUT_TURNS = NT // TPF


def retrieval_weights(nc, io, mem, W, ident, ps, w0, w0_loaded, lut):
    mem_x = mem.take("mem_x", [P, MC, MW])
    mem_n = mem.take("mem_n", [P, MC, MW])
    mem_T = mem.take("mem_T", [P, MEM])
    wk = mem.take("r_wk", [P, RH * RD])
    wv = mem.take("r_wv", [P, RH * RD])
    wq = mem.take("r_wq", [P, RH, C])
    wo = mem.take("r_wo", [P, RH, C])
    K = mem.take("r_K", [P, RH, MEM])
    V = mem.take("r_V", [P, RH, MEM])
    gb_mem = mem.take("gb_mem", [P, 2])
    beta = mem.take("beta", [P, RH])
    stats = mem.take("m_stats", [P, MC, 6])
    mean_var = mem.take("m_mean_var", [P, MC, 2])
    rstd = mem.take("m_rstd", [P, MC])
    power, eps = mem.take("m_power", [P, MC]), mem.take("m_eps", [P, MC])
    assert mem.at <= nc.sbuf_usable_end, mem.at
    sem = nc.alloc_semaphore
    loaded = {n: sem(f"m_{n}_loaded") for n in ("x", "gb", "beta", "wk", "wv", "wq", "wo")}
    state_loaded = sem("state_loaded")
    stats_done, aggr_done, rstd_step, normed = sem("m_stats_done"), sem("m_aggr_done"), sem("m_rstd_step"), sem("m_normed")
    power_set = sem("m_power_set")
    turned, mem_T_ready, beta_step = sem("m_turned"), sem("m_mem_T_ready"), sem("m_beta_step")
    kv_ready, K_copied, V_copied = sem("kv_ready"), sem("K_copied"), sem("m_V_copied")
    product_ready, product_copied = sem("product_ready"), [sem("product_copied_act"), sem("product_copied_dve")]
    groups = [(a, pair) for a in range(3) for pair in range(RH // 2)]

    with nc.Block() as block:
        @block.sync
        def _(sp):
            sp.dma_start(mem_x[:, :, :], io["memory"].rearrange("(n p) c -> p n c", p=P)).then_inc(loaded["x"], DMA)
            sp.dma_start(gb_mem[:, 0:1], io["g_mem"].rearrange("(p a) -> p a", a=1)).then_inc(loaded["gb"], DMA)
            sp.dma_start(gb_mem[:, 1:2], io["b_mem"].rearrange("(p a) -> p a", a=1)).then_inc(loaded["gb"], DMA)
            sp.dma_start(beta[:, :], io["log_beta"].partition_broadcast(P)).then_inc(loaded["beta"], DMA)
            sp.dma_start(wk[:, :], io["Wk"]).then_inc(loaded["wk"], DMA)
            sp.dma_start(wv[:, :], io["Wv"]).then_inc(loaded["wv"], DMA)
            sp.dma_start(wq[:, :, :], io["Wq"].rearrange("(h d) c -> d h c", d=RD)).then_inc(loaded["wq"], DMA)
            sp.dma_start(wo[:, :, :], io["Wo"].rearrange("(h d) c -> d h c", d=RD)).then_inc(loaded["wo"], DMA)
            sp.dma_start(W["g_state"][:, :], io["g_state"]).then_inc(state_loaded, DMA)
            sp.dma_start(W["b_state"][:, :], io["b_state"]).then_inc(state_loaded, DMA)
            lut.load(sp, io)
            for n in ("gate", "up", "down"):
                sp.dma_start(w0[n][:, :, :], io[f"w_{n}"].rearrange("(k p) n -> p k n", p=P)).then_inc(w0_loaded, DMA)
            sp.wait_ge(state_loaded, 2 * DMA)
            sp.wait_ge(w0_loaded, 3 * DMA)
            sp.wait_ge(lut.loaded, lut.LOADS * DMA)

        @block.gpsimd
        def _(pool):
            lut.zero(pool)
            pool.memset(power[:, :], -0.5).then_inc(power_set, 1)
            pool.memset(eps[:, :], LN_EPS).then_inc(power_set, 1)
            pool.wait_ge(power_set, 2)
            pool.wait_ge(aggr_done, MC)
            pool.tensor_tensor(rstd[:, :], mean_var[:, :, 1], eps[:, :], ALU.add).then_inc(rstd_step, 1)
            pool.wait_ge(rstd_step, 1)
            pool.tensor_tensor(rstd[:, :], rstd[:, :], power[:, :], ALU.pow).then_inc(rstd_step, 1)

        @block.scalar
        def _(act):
            act.wait_ge(loaded["beta"], DMA)
            act.activation(beta[:, :], beta[:, :], ACT.Exp).then_inc(beta_step, 1)
            act.wait_ge(turned, 1)
            act.wait_ge(loaded["gb"], 2 * DMA)
            act.activation(mem_T[:, :], ps[:, 0, 0:MEM], ACT.Identity, scale=gb_mem[:, 0:1], bias=gb_mem[:, 1:2])\
               .then_inc(mem_T_ready, 1)
            for n in range(RH // 4):
                act.wait_ge(kv_ready, RH // 4 + n + 1)
                act.activation(V[:, 4 * n:4 * n + 4, :].rearrange("p a b -> p (a b)"),
                               ps[:, 4 + 2 * n:6 + 2 * n, :].rearrange("p a b -> p (a b)"), ACT.Copy).then_inc(V_copied, 1)
            for n, (a, pair) in enumerate(groups):
                if n % 2 == 0:
                    act.wait_ge(product_ready, n + 1)
                    bank = 2 * (n % 4)
                    act.activation(W["GMU"][a][:, 2 * pair * MC:(2 * pair + 2) * MC, :].rearrange("p a b -> p (a b)"),
                                   ps[:, bank:bank + 2, :].rearrange("p a b -> p (a b)"), ACT.Copy)\
                       .then_inc(product_copied[0], 1)
            act.wait_ge(product_copied[0], len(groups) // 2)

        @block.vector
        def _(dve):
            dve.wait_ge(loaded["x"], DMA)
            for n in range(MC):
                dve.bn_stats(stats[:, n, :], mem_x[:, n, :]).then_inc(stats_done, 1)
            for n in range(MC):
                dve.wait_ge(stats_done, n + 1)
                dve.bn_aggr(mean_var[:, n, :], stats[:, n, :]).then_inc(aggr_done, 1)
            dve.wait_ge(rstd_step, 2)
            for n in range(MC):
                dve.tensor_scalar(mem_n[:, n, :], mem_x[:, n, :], mean_var[:, n, 0:1], rstd[:, n:n + 1],
                                  ALU.subtract, ALU.mult).then_inc(normed, 1)
            dve.wait_ge(beta_step, 1)
            dve.tensor_scalar(beta[:, :], beta[:, :], 0.5, None, ALU.mult).then_inc(beta_step, 1)
            dve.wait_ge(beta_step, 2)
            for h in range(RH):
                dve.wait_ge(kv_ready, h // 4 + 1)
                dve.tensor_scalar(K[:, h, :], ps[:, h // 2, h % 2 * MEM:(h % 2 + 1) * MEM], beta[:, h:h + 1], None,
                                  ALU.mult).then_inc(K_copied, 1)
            for n, (a, pair) in enumerate(groups):
                if n % 2 == 1:
                    dve.wait_ge(product_ready, n + 1)
                    bank = 2 * (n % 4)
                    dve.tensor_copy(W["GMU"][a][:, 2 * pair * MC:(2 * pair + 2) * MC, :].rearrange("p a b -> p (a b)"),
                                    ps[:, bank:bank + 2, :].rearrange("p a b -> p (a b)")).then_inc(product_copied[1], 1)
            dve.wait_ge(product_copied[1], len(groups) // 2)

        @block.tensor
        def _(pe):
            pe.wait_ge(normed, MC)
            for n in range(MC):
                last = pe.transpose(ps[:, 0, n * P:(n + 1) * P], mem_n[:, n, :], ident[:, :])
            last.then_inc(turned, 1)
            pe.wait_ge(mem_T_ready, 1)
            for name, w, bank in (("wk", wk, 0), ("wv", wv, 4)):
                pe.wait_ge(loaded[name], DMA)
                for h in range(RH):
                    last = pe.matmul(ps[:, bank + h // 2, h % 2 * MEM:(h % 2 + 1) * MEM], w[:, h * RD:(h + 1) * RD],
                                     mem_T[:, :], start=True, stop=True)
                    if h % 4 == 3:
                        last.then_inc(kv_ready, 1)
            pe.wait_ge(K_copied, RH)
            pe.wait_ge(V_copied, RH // 4)
            pe.wait_ge(loaded["wq"], DMA)
            pe.wait_ge(loaded["wo"], DMA)
            for n, (a, pair) in enumerate(groups):
                if n >= 4:
                    pe.wait_ge(product_copied[n % 2], (n - 4) // 2 + 1)
                left, right = ((wq, K), (V, K), (V, wo))[a]
                for k in range(2 * MC):
                    h, block_ = 2 * pair + k // MC, k % MC
                    last = pe.matmul(ps[:, 2 * (n % 4) + k // 2, k % 2 * MEM:(k % 2 + 1) * MEM],
                                     left[:, h, block_ * P:(block_ + 1) * P], right[:, h, :], start=True, stop=True)
                last.then_inc(product_ready, 1)


def retrieval(nc, mem, X, W, ident, ps):
    R, APART, STEP_LEN = 4, 2, EVALS + 3
    TICKS = STEPS * STEP_LEN
    FIRST = 3
    LEN = FIRST + TICKS + 1
    TURNS = NT // R
    assert R * APART == STEP_LEN and LEN + (R - 1) * APART < 2 * TICKS
    G, M, U = W["GMU"]
    norm_x = [mem.take(f"rt_norm_x{r}", [P, C]) for r in range(R)]
    hid_T = [mem.take(f"rt_hid_T{r}", [P, KC, P]) for r in range(R)]
    S = [mem.take(f"rt_scores{r}", [P, RH, MEM]) for r in range(R)]
    over = [mem.take(f"rt_over{r}", [P, RH, MEM]) for r in range(R)]
    weights_T = [mem.take(f"rt_weights_T{r}", [P, RH * MC, P]) for r in range(R)]
    stats = [mem.take(f"rt_stats{r}", [P, RH, 3]) for r in range(R)]
    vec = {(n, r): mem.take(f"rt_{n}{r}", [P, RH]) for r in range(R)
           for n in ("top", "nt", "mean_sq", "var", "s2", "root", "rs1", "step", "move")}
    x_stats = [[mem.take(f"rt_x_stats{r}{n}", [P, 6]) for n in range(2)] for r in range(R)]
    mean_var = [mem.take(f"rt_mean_var{r}", [P, 2]) for r in range(R)]
    rv = [[mem.take(f"rt_rv{r}{n}", [P, 1]) for n in range(7)] for r in range(R)]
    power, eps = mem.take("rt_power", [P, 1]), mem.take("rt_eps", [P, 1])
    per_entry = mem.take("rt_per_entry", [P, RH])
    assert mem.at <= nc.sbuf_usable_end, mem.at
    sem = nc.alloc_semaphore
    each = lambda name: [sem(f"rt_{name}{r}") for r in range(R)]
    consts_set = sem("rt_consts_set")
    x_stats_done, aggr_done, rstd_step, normed = each("x_stats_done"), each("aggr_done"), each("rstd_step"), each("normed")
    hid_full, hid_taken, turn_full, turn_taken = each("hid_full"), each("hid_taken"), each("turn_full"), each("turn_taken")
    scores_full = each("scores_full")
    top_done, start_ready, nt_ready = each("top_done"), each("start_ready"), each("nt_ready")
    act_relu, dve_relu = each("act_relu"), each("dve_relu")
    stats_ready, rs1_ready = each("stats_ready"), each("rs1_ready")
    s2_ready, root_ready, chain = each("s2_ready"), each("root_ready"), each("chain")
    out_full, out_added = each("out_full"), each("out_added")
    assert len(ACT_HEADS) == EVALS + 1
    TG = RH * MC // 4
    TU, SU = STEPS * TG, 2 * STEPS
    LINKS = 4
    NORM_LINKS = 7
    HID = -1

    def relus_before(turn, s, k, act):
        heads = [n if act else RH - n for n in ACT_HEADS]
        return turn * (STEPS * sum(heads)) + s * sum(heads) + sum(heads[:k])

    def await_relu(engine, r, turn, s, k, h):
        if h < ACT_HEADS[k]:
            engine.wait_ge(act_relu[r], relus_before(turn, s, k, True) + h + 1)
        else:
            engine.wait_ge(dve_relu[r], relus_before(turn, s, k, False) + h - ACT_HEADS[k] + 1)

    def phases(t):
        return [(r, back, t - APART * r + TICKS * back) for r in range(R) for back in range(2)
                if 0 <= t - APART * r + TICKS * back <= LEN]

    def in_step(phase):
        return (phase - FIRST) // STEP_LEN, (phase - FIRST) % STEP_LEN

    def at_place(t, place):
        return [(r, back, in_step(ph)[0]) for r, back, ph in phases(t)
                if FIRST <= ph < FIRST + TICKS and in_step(ph)[1] == place]

    def at_phase(t, phase):
        return [(r, back) for r, back, ph in phases(t) if ph == phase]

    def newtons(t):
        return [(r, back, s, k) for k in range(EVALS) for r, back, s in at_place(t, 2 + k)]

    turn_uses = [use for t in range(TICKS)
                 for use in [(r, back, HID) for r, back in at_phase(t, 1)] +
                 [(r, back, s * TG + n) for r, back, s in at_place(t, STEP_LEN - 1) for n in range(TG)]]
    score_uses = [(r, back, 2 * s + half) for t in range(TICKS) for r, back, s in at_place(t, 0) for half in range(2)]
    assert len(turn_uses) % 2 == 0 and len(score_uses) % 2 == 0

    def number_of(uses, r, use):
        return next(n for n, (r_, _, use_) in enumerate(uses) if (r_, use_) == (r, use))

    def place_of(uses, r, use):
        return number_of(uses, r, use) % 2

    def turn_taken_by(r, turn, use):
        return (hid_taken[r], turn + 1) if use == HID else (turn_taken[r], turn * TU + use + 1)

    def scores_taken_by(r, turn, use):
        return top_done[r], (turn * STEPS + use // 2) * RH + use % 2 * 4 + 4

    def await_place(engine, uses, taken_by, r, use, turn, edge):
        n = number_of(uses, r, use)
        back = uses[n][1]
        for before in range(n - 2, n - 2 - len(uses), -2):
            r_, back_, use_ = uses[before]
            if before < 0 and edge == "first":
                return
            if before >= 0 and (edge, back_) in (("first", 1), ("last", 0)):
                continue
            turn_ = turn + back - back_ - (before < 0)
            engine.wait_ge(*taken_by(r_, turn_, use_))
            return

    def run(engine, tick):
        def turn(i, edge):
            for t in range(TICKS):
                tick(t, lambda back: None if (edge, back) in (("first", 1), ("last", 0)) else i - back, edge)
        turn(0, "first")
        with engine.Fori(1, TURNS) as i:
            turn(i, "middle")
        turn(TURNS, "last")

    with nc.Block() as block:
        @block.gpsimd
        def _(pool):
            pool.memset(power[:, :], -0.5).then_inc(consts_set, 1)
            pool.memset(eps[:, :], LN_EPS).then_inc(consts_set, 1)
            pool.memset(per_entry[:, :], 1.0 / MEM).then_inc(consts_set, 1)
            pool.wait_ge(consts_set, 3)

            def tick(t, turn_of, edge):
                for r, back in at_phase(t, 0):
                    turn = turn_of(back)
                    if turn is None:
                        continue
                    var, v = mean_var[r][:, 1:2], [x[:, :] for x in rv[r]]
                    links = ((v[0], var, eps[:, :], ALU.add), (v[1], v[0], power[:, :], ALU.pow),
                             (v[2], v[1], v[1], ALU.mult), (v[3], v[2], var, ALU.mult),
                             (v[4], v[3], eps[:, :], ALU.add), (v[5], v[4], power[:, :], ALU.pow),
                             (v[6], v[1], v[5], ALU.mult))
                    pool.wait_ge(aggr_done[r], turn + 1)
                    for n, (out, a, b, op) in enumerate(links):
                        if n:
                            pool.wait_ge(rstd_step[r], turn * NORM_LINKS + n)
                        pool.tensor_tensor(out, a, b, op).then_inc(rstd_step[r], 1)
                for r, back, s, k in newtons(t):
                    turn = turn_of(back)
                    if turn is None:
                        continue
                    e = turn * (STEPS * EVALS) + s * EVALS + k
                    s1 = stats[r][:, :, 1]
                    mean_sq, var, s2, root, rs1, step, move, nt = \
                        (vec[n, r][:, :] for n in ("mean_sq", "var", "s2", "root", "rs1", "step", "move", "nt"))
                    pool.wait_ge(stats_ready[r], e * (RH // 2) + RH // 2)
                    pool.tensor_tensor(mean_sq, s1, s1, ALU.mult).then_inc(chain[r], 1)
                    pool.tensor_tensor(var, stats[r][:, :, 2], per_entry[:, :], ALU.mult).then_inc(chain[r], 1)
                    pool.wait_ge(chain[r], e * LINKS + 2)
                    pool.tensor_tensor(s2, mean_sq, var, ALU.add).then_inc(s2_ready[r], 1)
                    pool.wait_ge(root_ready[r], e + 1)
                    pool.tensor_tensor(step, s2, root, ALU.subtract).then_inc(chain[r], 1)
                    pool.wait_ge(rs1_ready[r], e + 1)
                    pool.wait_ge(chain[r], e * LINKS + 3)
                    pool.tensor_tensor(move, step, rs1, ALU.mult).then_inc(chain[r], 1)
                    pool.wait_ge(chain[r], e * LINKS + 4)
                    pool.tensor_tensor(nt, nt, move, ALU.subtract).then_inc(nt_ready[r], 1)

            run(pool, tick)

        def await_threshold(engine, r, turn, s, k):
            if k == 0:
                engine.wait_ge(start_ready[r], turn * STEPS + s + 1)
            else:
                engine.wait_ge(nt_ready[r], turn * (STEPS * EVALS) + s * EVALS + k)

        @block.scalar
        def _(act):
            def relus(r, turn, s, k):
                await_threshold(act, r, turn, s, k)
                for h in range(ACT_HEADS[k]):
                    act.activation(over[r][:, h, :], S[r][:, h, :], ACT.Relu, bias=vec["nt", r][:, h:h + 1])\
                       .then_inc(act_relu[r], 1)

            def root(r, turn, s, k):
                act.wait_ge(s2_ready[r], turn * (STEPS * EVALS) + s * EVALS + k + 1)
                act.activation(vec["root", r][:, :], vec["s2", r][:, :], ACT.Sqrt, scale=1.0 / MEM)\
                   .then_inc(root_ready[r], 1)

            def squares(r, turn, s):
                for n in range(TG):
                    use = s * TG + n
                    act.wait_ge(turn_full[r], turn * TU + use + 1)
                    act.activation(weights_T[r][:, 4 * n:4 * n + 4, :].rearrange("p a b -> p (a b)"),
                                   ps[:, 4 + place_of(turn_uses, r, use), :], ACT.Square).then_inc(turn_taken[r], 1)

            def take_hidden(r, turn):
                act.wait_ge(hid_full[r], turn + 1)
                bank = 4 + place_of(turn_uses, r, HID)
                for kc in range(KC):
                    ins = act.activation(hid_T[r][:, kc, :], ps[:, bank, kc * P:(kc + 1) * P], ACT.Identity,
                                         scale=W["g_state"][:, kc:kc + 1], bias=W["b_state"][:, kc:kc + 1])
                ins.then_inc(hid_taken[r], 1)

            def between(t, turn_of):
                for r, back, s in at_place(t, 0):
                    if s and turn_of(back) is not None:
                        squares(r, turn_of(back), s - 1)
                for r, back in at_phase(t, LEN - 1):
                    if turn_of(back) is not None:
                        squares(r, turn_of(back), STEPS - 1)
                for r, back in at_phase(t, 2):
                    if turn_of(back) is not None:
                        take_hidden(r, turn_of(back))

            def tick(t, turn_of, edge):
                late = [(r, back + (t == 0), s, k) for r, back, s, k in newtons((t - 1) % TICKS)[-1:]]
                for n, (r, back, s, k) in enumerate(newtons(t)):
                    if turn_of(back) is not None:
                        relus(r, turn_of(back), s, k)
                    for r_, back_, s_, k_ in late:
                        if t == 0 and back_ > 1:
                            continue
                        if turn_of(back_) is not None:
                            root(r_, turn_of(back_), s_, k_)
                    late = [(r, back, s, k)]
                    if n == 0:
                        between(t, turn_of)
                for r, back, s in at_place(t, STEP_LEN - 1):
                    if turn_of(back) is not None:
                        relus(r, turn_of(back), s, EVALS)

            run(act, tick)

        @block.vector
        def _(dve):
            def x_of(r, turn):
                return X[:, bass.ds(turn * (R * C) + r * C, C)]

            def own_relus(r, turn, s, k):
                await_threshold(dve, r, turn, s, k)
                for h in range(ACT_HEADS[k], RH):
                    dve.tensor_scalar(over[r][:, h, :], S[r][:, h, :], vec["nt", r][:, h:h + 1], 0.0,
                                      ALU.add, ALU.max).then_inc(dve_relu[r], 1)

            def start(r, turn, s):
                for half in range(2):
                    heads = range(4 * half, 4 * half + 4)
                    dve.wait_ge(scores_full[r], turn * SU + 2 * s + half + 1)
                    bank = 2 * place_of(score_uses, r, 2 * s + half)
                    for h in heads:
                        dve.tensor_scalar(S[r][:, h, :], ps[:, bank + h % 4 // 2, h % 2 * MEM:(h % 2 + 1) * MEM],
                                          0.0, None, ALU.add, ALU.max, accum_out=vec["top", r][:, h:h + 1])\
                           .then_inc(top_done[r], 1)
                dve.wait_ge(top_done[r], (turn * STEPS + s + 1) * RH)
                dve.tensor_scalar(vec["nt", r][:, :], vec["top", r][:, :], -1.0, 1.0, ALU.mult, ALU.add)\
                   .then_inc(start_ready[r], 1)

            def moments(r, turn, s, k):
                for h in range(0, RH, 2):
                    if h + 1 == ACT_HEADS[k]:
                        await_relu(dve, r, turn, s, k, h)
                    await_relu(dve, r, turn, s, k, h + 1)
                    dve.bn_stats(stats[r][:, h:h + 2, :].rearrange("p a b -> p (a b)"),
                                 over[r][:, h:h + 2, :].rearrange("p a b -> p b a")).then_inc(stats_ready[r], 1)

            def reciprocal(r, turn, s, k):
                dve.wait_ge(stats_ready[r], (turn * (STEPS * EVALS) + s * EVALS + k + 1) * (RH // 2))
                dve.reciprocal(vec["rs1", r][:, :], stats[r][:, :, 1]).then_inc(rs1_ready[r], 1)

            def tick(t, turn_of, edge):
                for r, back in at_phase(t, 0):
                    turn = turn_of(back)
                    if turn is not None:
                        dve.bn_stats(x_stats[r][0][:, :], x_of(r, turn)).then_inc(x_stats_done[r], 1)
                        stats_are_in(dve, x_stats[r][1][:, :], x_stats[r][0][:, :], x_stats_done[r], turn + 1)
                        dve.bn_aggr(mean_var[r][:, :], x_stats[r][0][:, :]).then_inc(aggr_done[r], 1)
                for r, back in at_phase(t, 1):
                    turn = turn_of(back)
                    if turn is not None:
                        dve.wait_ge(rstd_step[r], turn * NORM_LINKS + NORM_LINKS)
                        dve.tensor_scalar(norm_x[r][:, :], x_of(r, turn), mean_var[r][:, 0:1], rv[r][6][:, :],
                                          ALU.subtract, ALU.mult).then_inc(normed[r], 1)
                late = None
                for n, (r, back, s, k) in enumerate(newtons(t)):
                    if turn_of(back) is not None:
                        own_relus(r, turn_of(back), s, k)
                    if late:
                        reciprocal(*late)
                        late = None
                    if turn_of(back) is not None:
                        moments(r, turn_of(back), s, k)
                        late = r, turn_of(back), s, k
                    if n == 0:
                        for r, back, s in at_place(t, 1):
                            if turn_of(back) is not None:
                                start(r, turn_of(back), s)
                for r, back, s in at_place(t, STEP_LEN - 1):
                    if turn_of(back) is not None:
                        own_relus(r, turn_of(back), s, EVALS)
                if late:
                    reciprocal(*late)
                for r, back in at_phase(t, LEN):
                    turn = turn_of(back)
                    if turn is not None:
                        dve.wait_ge(out_full[r], turn + 1)
                        dve.tensor_tensor(x_of(r, turn), x_of(r, turn), ps[:, 6, 0:C], ALU.add).then_inc(out_added[r], 1)

            run(dve, tick)
            for r in range(R):
                dve.wait_ge(out_added[r], TURNS)

        @block.tensor
        def _(pe):
            def scores(r, turn, s, edge):
                if s == 0:
                    pe.wait_ge(hid_taken[r], turn + 1)
                left, right = (weights_T[r], M) if s else (hid_T[r], G)
                for half in range(2):
                    use = 2 * s + half
                    await_place(pe, score_uses, scores_taken_by, r, use, turn, edge)
                    slot = place_of(score_uses, r, use)
                    for h in range(4 * half, 4 * half + 4):
                        if s and h % 2 == 0:
                            pe.wait_ge(turn_taken[r], turn * TU + (s - 1) * TG + h // 2 + 1)
                        for b in range(MC):
                            last = pe.matmul(ps[:, 2 * slot + h % 4 // 2, h % 2 * MEM:(h % 2 + 1) * MEM],
                                             left[:, h * MC + b if s else b, :], right[:, h * MC + b, :],
                                             start=b == 0, stop=b == MC - 1)
                    last.then_inc(scores_full[r], 1)

            def turn_weights(r, turn, s, edge):
                for n in range(TG):
                    use = s * TG + n
                    await_place(pe, turn_uses, turn_taken_by, r, use, turn, edge)
                    bank = 4 + place_of(turn_uses, r, use)
                    for h in (2 * n, 2 * n + 1):
                        await_relu(pe, r, turn, s, EVALS, h)
                        for b in range(MC):
                            last = pe.transpose(ps[:, bank, (h % 2 * MC + b) * P:(h % 2 * MC + b + 1) * P],
                                                over[r][:, h, b * P:(b + 1) * P], ident[:, :])
                    last.then_inc(turn_full[r], 1)

            def tick(t, turn_of, edge):
                for r, back, s in at_place(t, 0):
                    if turn_of(back) is not None:
                        scores(r, turn_of(back), s, edge)
                for r, back in at_phase(t, 1):
                    turn = turn_of(back)
                    if turn is not None:
                        pe.wait_ge(normed[r], turn + 1)
                        await_place(pe, turn_uses, turn_taken_by, r, HID, turn, edge)
                        bank = 4 + place_of(turn_uses, r, HID)
                        for kc in range(KC):
                            last = pe.transpose(ps[:, bank, kc * P:(kc + 1) * P], norm_x[r][:, kc * P:(kc + 1) * P], ident[:, :])
                        last.then_inc(hid_full[r], 1)
                for r, back in at_phase(t, LEN - 1):
                    turn = turn_of(back)
                    if turn is not None:
                        for n in range(RH * MC):
                            if n % 4 == 0:
                                pe.wait_ge(turn_taken[r], turn * TU + (STEPS - 1) * TG + n // 4 + 1)
                            last = pe.matmul(ps[:, 6, 0:C], weights_T[r][:, n, :], U[:, n, :],
                                             start=n == 0, stop=n == RH * MC - 1)
                        last.then_inc(out_full[r], 1)
                for r, back, s in at_place(t, STEP_LEN - 1):
                    if turn_of(back) is not None:
                        turn_weights(r, turn_of(back), s, edge)
                for r, back in at_phase(t, LEN):
                    if turn_of(back) is not None:
                        pe.wait_ge(out_added[r], turn_of(back) + 1)

            run(pe, tick)


class LutWeights:

    COLS = (KC * HID1, KC * HID1, F1 * C)
    ALL = sum(COLS)
    PIECE = ALL // LUT_TURNS
    assert PIECE * LUT_TURNS == ALL
    OPS = 4 + 1 + LUT // 2 + (LUT // 2 - 1) + 1

    def __init__(self, nc, mem):
        self.out = mem.take("lut_out", [P, self.ALL])
        self.lut = mem.take("lut", [P, LUT])
        sem = nc.alloc_semaphore
        self.idx_zeroed, self.loaded, self.delta_ready, self.step = \
            sem("idx_zeroed"), sem("lut_loaded"), sem("lut_delta_ready"), sem("lut_step")
        self.LOADS = 5

    def take_indices(self, mem):
        self.idx = mem.take("idx", [P, self.ALL], I32)

    def take_scratch(self, mem):
        self.bit = [mem.take(f"lut_bit{k}", [P, self.PIECE], I32) for k in range(4)]
        self.low = mem.take("lut_low", [P, self.PIECE])
        self.leaf = [mem.take(f"lut_leaf{k}", [P, self.PIECE]) for k in range(LUT // 2)]
        self.delta = mem.take("lut_delta", [P, LUT // 2])
        self.spare = mem.take("lut_spare", [P, 6])

    def weights(self, a):
        at = sum(self.COLS[:a])
        return self.out[:, at:at + self.COLS[a]].rearrange("p (k n) -> p k n", n=C if a == 2 else HID1)

    def zero(self, pool):
        pool.memset(self.idx[:, self.ALL - C:], 0).then_inc(self.idx_zeroed, 1)

    def load(self, sp, io):
        sp.dma_start(self.lut[:, :], io["lut"].partition_broadcast(P)).then_inc(self.loaded, DMA)
        for a, name in enumerate(("gate_idx", "up_idx")):
            sp.dma_start(self.idx[:, a * self.COLS[0]:(a + 1) * self.COLS[0]].rearrange("p (k n) -> p k n", k=KC),
                         io[name].rearrange("(k p) n -> p k n", p=P)).then_inc(self.loaded, DMA)
        full = HID1 // P * P
        down = self.idx[:, 2 * self.COLS[0]:].rearrange("p (k n) -> p k n", n=C)
        sp.dma_start(down[:, 0:F1 - 1, :], io["down_idx"][0:full, :].rearrange("(k p) n -> p k n", p=P))\
          .then_inc(self.loaded, DMA)
        sp.wait_ge(self.idx_zeroed, 1)
        sp.dma_start(down[0:HID1 - full, F1 - 1, :], io["down_idx"][full:HID1, :]).then_inc(self.loaded, DMA)

    def differences(self, dve):
        pairs = self.lut[:, :].rearrange("p (k e) -> p k e", e=2)
        dve.wait_ge(self.loaded, self.LOADS * DMA)
        dve.tensor_tensor(self.delta[:, :], pairs[:, :, 1], pairs[:, :, 0], ALU.subtract).then_inc(self.delta_ready, 1)
        dve.wait_ge(self.delta_ready, 1)

    def select(self, dve, turn, n):
        bit, leaf, low = self.bit, self.leaf, self.low
        cols = bass.ds(turn * self.PIECE, self.PIECE)
        pairs = self.lut[:, :].rearrange("p (k e) -> p k e", e=2)
        if n:
            dve.wait_ge(self.step, turn * self.OPS + n)
        if 5 + LUT // 2 <= n < self.OPS - 1:
            dve.bn_stats(self.spare[:, :], self.delta[:, :])
        if n < 4:
            ins = dve.tensor_scalar(bit[n][:, :], self.idx[:, cols], 1 << n, None, ALU.bitwise_and)
        elif n == 4:
            ins = dve.tensor_copy(low[:, :], bit[0][:, :])
        elif n < 5 + LUT // 2:
            k = n - 5
            ins = dve.tensor_scalar(leaf[k][:, :], low[:, :], self.delta[:, k:k + 1], pairs[:, k, 0:1], ALU.mult, ALU.add)
        elif n < self.OPS - 1:
            k, left = [(k, left) for k in range(1, 4) for left in range(0, LUT // 2, 1 << k)][n - 5 - LUT // 2]
            ins = dve.copy_predicated(leaf[left][:, :], bit[k][:, :], leaf[left + (1 << k - 1)][:, :])
        else:
            ins = dve.tensor_copy(self.out[:, cols], leaf[0][:, :])
        ins.then_inc(self.step, 1)


def ffn(nc, mem, X, w_gate, w_up, w_down, width, ident, ps, name, lut=None, out=None):
    TURNS = NT // TPF
    F = -(-width // P)
    norm_x = mem.take(f"{name}_norm_x", [P, TPF * C])
    SPLIT = len(w_gate) == 2
    names, dtype = (("high", "low"), F32R) if SPLIT else (("all",), F32)
    PRODUCTS = ((0, 0), (0, 1), (1, 0)) if SPLIT else ((0, 0),)
    norm_T = [mem.take(f"{name}_norm_T_{part}", [P, KC, FC], dtype) for part in names]
    gate = mem.take(f"{name}_gate", [P, 2, FC])
    hidden = mem.take(f"{name}_hidden", [P, 2, FC])
    hidden_part = [mem.take(f"{name}_hidden_{part}", [P, 2, FC], F32R) for part in names] if SPLIT else [hidden]
    stats = mem.take(f"{name}_stats", [P, TPF + 1, 6])
    mean_var = mem.take(f"{name}_mean_var", [P, TPF, 2])
    rstd = mem.take(f"{name}_rstd", [P, TPF])
    power, eps = mem.take(f"{name}_power", [P, TPF]), mem.take(f"{name}_eps", [P, TPF])
    assert mem.at <= nc.sbuf_usable_end, mem.at
    sem = lambda n: nc.alloc_semaphore(f"{name}_{n}")
    power_set, stats_done, aggr_done, rstd_step, normed = (sem(n) for n in ("power_set", "stats_done", "aggr_done", "rstd_step", "normed"))
    turned, norm_T_ready = sem("turned"), sem("norm_T_ready")
    norm_T_low, hidden_high, hidden_low = sem("norm_T_low"), sem("hidden_high"), sem("hidden_low")
    stored = sem("stored")
    gate_full, up_full, gate_ready, hidden_ready, down_done, added = \
        (sem(n) for n in ("gate_full", "up_full", "gate_ready", "hidden_ready", "down_done", "added"))
    assert F % 2 == 0
    norm_T_whole, hidden_whole, hidden_used = \
        (norm_T_low, hidden_low, hidden_low) if SPLIT else (norm_T_ready, hidden_ready, down_done)
    OUT = 4

    def run(engine, turn):
        turn(0, True, False)
        with engine.Fori(1, TURNS - 1) as i:
            turn(i, False, False)
        turn(TURNS - 1, False, True)

    with nc.Block() as block:
        @block.sync
        def _(sp):
            if out is not None:
                for i in range(TURNS):
                    sp.wait_ge(added, i + 1)
                    tiles = slice(i * TPF, (i + 1) * TPF)
                    sp.dma_start(out.rearrange("(n p) c -> p n c", p=P)[:, tiles, :],
                                 X[:, :].rearrange("p (n c) -> p n c", c=C)[:, tiles, :]).then_inc(stored, DMA)
                sp.wait_ge(stored, TURNS * DMA)

        @block.gpsimd
        def _(pool):
            def root(i, first):
                pool.wait_ge(aggr_done, i * TPF + TPF)
                if not first:
                    pool.wait_ge(normed, i * TPF)
                pool.tensor_tensor(rstd[:, :], mean_var[:, :, 1], eps[:, :], ALU.add).then_inc(rstd_step, 1)
                pool.wait_ge(rstd_step, i * 2 + 1)
                pool.tensor_tensor(rstd[:, :], rstd[:, :], power[:, :], ALU.pow).then_inc(rstd_step, 1)

            pool.memset(power[:, :], -0.5).then_inc(power_set, 1)
            pool.memset(eps[:, :], LN_EPS).then_inc(power_set, 1)
            pool.wait_ge(power_set, 2)

            def turn(i, first, last):
                if not SPLIT:
                    if not last:
                        root(i + 1, False)
                    return
                for f in range(F):
                    pool.wait_ge(hidden_high, i * F + f + 1)
                    if f >= 2 or not first:
                        pool.wait_ge(down_done, i * F + f - 1)
                    pool.tensor_tensor(hidden_part[1][:, f % 2, :], hidden[:, f % 2, :],
                                       hidden_part[0][:, f % 2, :].bitcast(F32), ALU.subtract).then_inc(hidden_low, 1)
                    if f == 0 and not last:
                        root(i + 1, False)

            root(0, True)
            run(pool, turn)

        @block.scalar
        def _(act):
            def transposed(i):
                for kc in range(KC):
                    act.wait_ge(turned, i * KC + kc + 1)
                    act.activation(norm_T[0][:, kc, :], ps[:, kc, :], ACT.Copy).then_inc(norm_T_ready, 1)

            def high(i, f, first):
                act.wait_ge(hidden_ready, i * F + f + 1)
                if f >= 2 or not first:
                    act.wait_ge(down_done, i * F + f - 1)
                act.activation(hidden_part[0][:, f % 2, :], hidden[:, f % 2, :], ACT.Copy).then_inc(hidden_high, 1)

            def turn(i, first, last):
                for f in range(F):
                    act.wait_ge(gate_full, i * F + f + 1)
                    if f >= 2 or not first:
                        act.wait_ge(hidden_ready, i * F + f - 1)
                    act.activation(gate[:, f % 2, :], ps[:, 2 * (f % 2), :], ACT.Silu).then_inc(gate_ready, 1)
                    if SPLIT:
                        high(i, f, first)
                if not last:
                    act.wait_ge(up_full, i * F + F)
                    transposed(i + 1)

            transposed(0)
            run(act, turn)

        @block.vector
        def _(dve):
            def tiles(i):
                return [X[:, bass.ds(i * (TPF * C) + t * C, C)] for t in range(TPF)]

            def moments(i):
                for t in range(TPF):
                    dve.bn_stats(stats[:, t, :], tiles(i)[t]).then_inc(stats_done, 1)
                stats_are_in(dve, stats[:, TPF, :], stats[:, 0, :], stats_done, i * TPF + TPF)
                for t in range(TPF):
                    dve.bn_aggr(mean_var[:, t, :], stats[:, t, :]).then_inc(aggr_done, 1)

            def norm(i, first):
                dve.wait_ge(rstd_step, i * 2 + 2)
                if not first:
                    dve.wait_ge(turned, i * KC)
                for t in range(TPF):
                    dve.tensor_scalar(norm_x[:, t * C:(t + 1) * C], tiles(i)[t], mean_var[:, t, 0:1], rstd[:, t:t + 1],
                                      ALU.subtract, ALU.mult).then_inc(normed, 1)

            def low(i):
                for kc in range(KC if SPLIT else 0):
                    dve.wait_ge(norm_T_ready, i * KC + kc + 1)
                    dve.tensor_tensor(norm_T[1][:, kc, :], ps[:, kc, :], norm_T[0][:, kc, :].bitcast(F32), ALU.subtract)\
                       .then_inc(norm_T_low, 1)

            def turn(i, first, last):
                selected = 0
                for f in range(F):
                    dve.wait_ge(gate_ready, i * F + f + 1)
                    dve.wait_ge(up_full, i * F + f + 1)
                    if f >= 2 or not first:
                        dve.wait_ge(hidden_used, i * F + f - 1)
                    dve.tensor_tensor(hidden[:, f % 2, :], gate[:, f % 2, :], ps[:, 2 * (f % 2) + 1, :], ALU.mult)\
                       .then_inc(hidden_ready, 1)
                    if f == 0 and not last:
                        moments(i + 1)
                    if f == 2 and not last:
                        norm(i + 1, False)
                    while lut and selected < min(lut.OPS, (f + 1) * -(-lut.OPS // (F - 1))):
                        lut.select(dve, i, selected)
                        selected += 1
                if not last:
                    low(i + 1)
                dve.wait_ge(down_done, i * F + F)
                both = X[:, bass.ds(i * (TPF * C), TPF * C)].rearrange("p (t c) -> p t c", c=C)
                dve.tensor_tensor(both, both, ps[:, OUT:OUT + TPF, 0:C], ALU.add).then_inc(added, 1)

            moments(0)
            norm(0, True)
            low(0)
            if lut:
                lut.differences(dve)
            run(dve, turn)
            dve.wait_ge(added, TURNS)
            if lut:
                dve.wait_ge(lut.step, TURNS * lut.OPS)

        @block.tensor
        def _(pe):
            def turn_norm(i):
                pe.wait_ge(normed, i * TPF + TPF)
                for kc in range(KC):
                    for t in range(TPF):
                        last = pe.transpose(ps[:, kc, t * P:(t + 1) * P], norm_x[:, t * C + kc * P:t * C + (kc + 1) * P],
                                            ident[:, :])
                    last.then_inc(turned, 1)

            def gate_up(i, f, first):
                if f >= 2 or not first:
                    pe.wait_ge(gate_ready, i * F + f - 1)
                    pe.wait_ge(hidden_ready, i * F + f - 1)
                for w, bank, full in ((w_gate, 0, gate_full), (w_up, 1, up_full)):
                    steps = [(kc, a, b) for kc in range(KC) for a, b in PRODUCTS]
                    for n, (kc, a, b) in enumerate(steps):
                        last = pe.matmul(ps[:, 2 * (f % 2) + bank, :], w[a][:, kc, f * P:(f + 1) * P], norm_T[b][:, kc, :],
                                         start=n == 0, stop=n == len(steps) - 1)
                    last.then_inc(full, 1)

            def turn(i, first, last):
                pe.wait_ge(norm_T_whole, i * KC + KC)
                gate_up(i, 0, first)
                for f in range(F):
                    if f + 1 < F:
                        gate_up(i, f + 1, first)
                    if f == 0 and not first:
                        pe.wait_ge(added, i)
                    pe.wait_ge(hidden_whole, i * F + f + 1)
                    for t in range(TPF):
                        for n, (a, b) in enumerate(PRODUCTS):
                            done = pe.matmul(ps[:, OUT + t, 0:C], hidden_part[b][:, f % 2, t * P:(t + 1) * P], w_down[a][:, f, :],
                                             start=f == 0 and n == 0, stop=f == F - 1 and n == len(PRODUCTS) - 1)
                    done.then_inc(down_done, 1)
                    if f == F - 2 and not last:
                        turn_norm(i + 1)

            turn_norm(0)
            run(pe, turn)


def split_weights(nc, mem, weights, name):
    parts = []
    for n, w in enumerate(weights):
        columns = -(-w.shape[2] // P) * P
        parts.append([mem.take(f"{name}_{n}_{part}", [P, w.shape[1], columns], F32R) for part in ("high", "low")])
    assert mem.at <= nc.sbuf_usable_end, mem.at
    high_done, low_done, padded = (nc.alloc_semaphore(f"{name}_{n}") for n in ("high_done", "low_done", "padded"))
    with nc.Block() as block:
        @block.gpsimd
        def _(pool):
            pads = 0
            for w, both in zip(weights, parts):
                if both[0].shape[2] > w.shape[2]:
                    for part in both:
                        pool.memset(part[:, :, w.shape[2]:].bitcast(F32), 0.0).then_inc(padded, 1)
                        pads += 1
            if pads:
                pool.wait_ge(padded, pads)

        @block.scalar
        def _(act):
            for w, (high, _) in zip(weights, parts):
                act.activation(high[:, :, 0:w.shape[2]], w, ACT.Copy).then_inc(high_done, 1)

        @block.vector
        def _(dve):
            for n, (w, (high, low)) in enumerate(zip(weights, parts)):
                dve.wait_ge(high_done, n + 1)
                dve.tensor_tensor(low[:, :, 0:w.shape[2]], w, high[:, :, 0:w.shape[2]].bitcast(F32), ALU.subtract)\
                   .then_inc(low_done, 1)
            dve.wait_ge(low_done, len(weights))
    return parts


def give_back_semaphores(nc, free):
    nc.clear_and_free_semaphores([n for n in sorted(free) if n not in nc.free_semaphores])
    nc.all_engine_barrier()


def build(nc, io, out):
    nc.disable_value_cache = True
    mem = Memory(nc, 16512)
    X = mem.take("X", [P, NT * C])
    ident = mem.take("ident", [P, P])
    W = {"g_state": mem.take("g_state", [P, KC]), "b_state": mem.take("b_state", [P, KC])}
    ps = nc.alloc_psum_tensor("banks", [P, 8, BANK], F32)
    base = mem.at
    free = set(nc.free_semaphores)
    attention(nc, io, mem, X, ident, ps)
    give_back_semaphores(nc, free)

    mem.at = base
    W["GMU"] = [mem.take(f"w_{n}", [P, RH * MC, C]) for n in "GMU"]
    lut = LutWeights(nc, mem)
    base = mem.at
    w0 = {n: mem.take(f"w_{n}0", shape) for n, shape in (("gate", [P, KC, HID0]), ("up", [P, KC, HID0]), ("down", [P, F0, C]))}
    w0_loaded = nc.alloc_semaphore("w0_loaded")
    lut.take_indices(mem)
    scratch = mem.at
    retrieval_weights(nc, io, mem, W, ident, ps, w0, w0_loaded, lut)

    mem.at = scratch
    lut.take_scratch(mem)
    ffn(nc, mem, X, [w0["gate"]], [w0["up"]], [w0["down"]], HID0, ident, ps, "ffn0", lut)
    mem.at = base
    retrieval(nc, mem, X, W, ident, ps)
    mem.at = base
    parts = split_weights(nc, mem, [lut.weights(a) for a in range(3)], "w1")
    ffn(nc, mem, X, *parts, HID1, ident, ps, "ffn1", out=out)


def kernel(**inputs):
    import numpy as np
    import concourse.bacc as bacc
    from concourse.bass_utils import run_bass_kernel_spmd

    a0 = lambda n: np.asarray(inputs[f"L0_attn_{n}"])
    a1 = lambda n: np.asarray(inputs[f"L1_attn_{n}"])
    f0 = lambda n: np.asarray(inputs[f"L0_ffn_{n}"])
    f1 = lambda n: np.asarray(inputs[f"L1_ffn_{n}"])
    arrays = {"x": a0("x").reshape(B * T, C)}
    arrays.update({n: a0(n).T for n in ("wq", "wk", "wv", "wo")})
    arrays.update({n: a0(n) for n in ("lq1", "lk1", "lq2", "lk2")})
    arrays.update({n: f0(n).T for n in ("w_gate", "w_up", "w_down")})
    arrays.update({n: a1(n) for n in ("memory", "Wq", "log_beta", "g_mem", "b_mem")})
    arrays.update({n: a1(n).T for n in ("Wk", "Wv", "Wo")})
    arrays.update({n: a1(n).reshape(KC, P).T for n in ("g_state", "b_state")})
    arrays["lut"] = f1("lut")
    arrays.update({n: f1(n).T for n in ("gate_idx", "up_idx", "down_idx")})
    arrays = {n: np.ascontiguousarray(a) for n, a in arrays.items()}

    nc = bacc.Bacc("TRN2", target_bir_lowering=False, num_devices=1)
    io = {n: nc.dram_tensor(f"in_{n}", a.shape, mybir.dt.from_np(a.dtype), kind="ExternalInput").ap()
          for n, a in arrays.items()}
    out = nc.dram_tensor("out", (B * T, C), F32, kind="ExternalOutput").ap()
    build(nc, io, out)
    r = run_bass_kernel_spmd(nc, [{f"in_{n}": a for n, a in arrays.items()}], core_ids=[0])
    return r.results[0]["out"].reshape(B, T, C)
```
